# Optimizing a Trainium2 kernel written in Bass

```python
import numpy as np
import jax
import jax.numpy as jnp

def _softmax(x, axis=-1):
    return jax.nn.softmax(x, axis=axis)

def _gelu(x):
    return jax.nn.gelu(x, approximate=True)

def _silu(x):
    return jax.nn.silu(x)

def _sigmoid(x):
    return jax.nn.sigmoid(x)

def _layernorm(x, axis=-1, eps=1e-05):
    m = jnp.mean(x, axis=axis, keepdims=True)
    v = jnp.var(x, axis=axis, keepdims=True)
    return (x - m) / jnp.sqrt(v + eps)

def _scatter_add(tgt, idx, src, axis=0):
    return tgt.at[idx].add(src)

def _segment_sum(src, seg, n):
    return jax.ops.segment_sum(src, seg, n)
kernel_name = 'mk_seq_postln_d2_jaxref_r4_267e1d'

def setup_inputs(seed: int=0):
    np.random.seed(seed)
    _w = jnp.asarray

    def _L0_attn_setup():
        import jax, jax.numpy as jnp
        import numpy as np
        NUM_HEADS = 16
        key = jax.random.key(seed)
        ks = jax.random.split(key, 5)
        B, S, H = (2, 512, 256)
        scale = 0.02
        return {'x': jax.random.normal(ks[0], (B, S, H), dtype=jnp.float32), 'w_qkv': jax.random.normal(ks[1], (H, 3 * H), dtype=jnp.float32) * scale, 'b_qkv': jax.random.normal(ks[2], (3 * H,), dtype=jnp.float32) * scale, 'w_out': jax.random.normal(ks[3], (H, H), dtype=jnp.float32) * scale, 'b_out': jax.random.normal(ks[4], (H,), dtype=jnp.float32) * scale}
    _L0_attn_in = _L0_attn_setup()

    def _L0_ffn_setup():
        import math
        import jax, jax.numpy as jnp
        import numpy as np
        NUM_EXPERTS = 8
        TOP_K = 2
        CAPACITY_FACTOR = 1.0
        B, S, H, I = (4, 512, 256, 1024)
        key = jax.random.key(seed)
        k_x, k_rw, k_wi, k_wo = jax.random.split(key, 4)
        x = jax.random.normal(k_x, (B, S, H), dtype=jnp.float32)
        lim = math.sqrt(6.0 / (H + NUM_EXPERTS))
        router_w = jax.random.uniform(k_rw, (NUM_EXPERTS, H), minval=-lim, maxval=lim, dtype=jnp.float32)
        router_b = jnp.zeros((NUM_EXPERTS,), dtype=jnp.float32)
        experts_inter = jax.random.normal(k_wi, (NUM_EXPERTS - 1, H, I), dtype=jnp.float32) / math.sqrt(H)
        experts_out = jax.random.normal(k_wo, (NUM_EXPERTS - 1, I, H), dtype=jnp.float32) / math.sqrt(I)
        return {'x': x, 'router_w': router_w, 'router_b': router_b, 'experts_inter': experts_inter, 'experts_out': experts_out}
    _L0_ffn_in = _L0_ffn_setup()

    def _L1_attn_setup():
        import jax, jax.numpy as jnp
        import numpy as np
        D = 256
        H = 16
        HD = D // H
        ROPE_BASE = 10000.0
        EPS_RMS = 1e-08
        EPS_RENORM = 1e-08

        def rms_norm(x, scale):
            norm = jnp.mean(x * x, axis=-1, keepdims=True)
            return scale * (x * jax.lax.rsqrt(norm + EPS_RMS))

        def rope_tables(seq_len):
            inv_freq = 1.0 / ROPE_BASE ** (jnp.arange(0, HD, 2, dtype=jnp.float32) / HD)
            t = jnp.arange(seq_len, dtype=jnp.float32)
            freqs = t[:, None] * inv_freq[None, :]
            emb = jnp.concatenate([freqs, freqs], axis=-1)
            return (jnp.cos(emb), jnp.sin(emb))

        def apply_rotary(x, cos, sin):
            x1 = x[..., ::2]
            x2 = x[..., 1::2]
            x_rot = jnp.stack([-x2, x1], axis=-1).reshape(x.shape)
            return x * cos + x_rot * sin
        key = jax.random.key(seed)
        ks = jax.random.split(key, 11)
        B, L = (2, 512)
        s = 1.0 / np.sqrt(D)
        inp = {'x': jax.random.normal(ks[0], (B, L, D), dtype=jnp.float32), 'q_w': jax.random.uniform(ks[1], (D, D), jnp.float32, -s, s), 'q_b': jax.random.uniform(ks[2], (D,), jnp.float32, -s, s), 'k_w': jax.random.uniform(ks[3], (D, D), jnp.float32, -s, s), 'k_b': jax.random.uniform(ks[4], (D,), jnp.float32, -s, s), 'v_w': jax.random.uniform(ks[5], (D, D), jnp.float32, -s, s), 'v_b': jax.random.uniform(ks[6], (D,), jnp.float32, -s, s), 'o_w': jax.random.uniform(ks[7], (D, D), jnp.float32, -s, s), 'o_b': jax.random.uniform(ks[8], (D,), jnp.float32, -s, s), 'qn_scale': jnp.ones((D,), dtype=jnp.float32), 'kn_scale': jnp.ones((D,), dtype=jnp.float32)}
        return inp
    _L1_attn_in = _L1_attn_setup()

    def _L1_ffn_setup():
        import jax, jax.numpy as jnp
        import numpy as np
        B, S, D = (2, 512, 256)
        DFF = 512
        E_FFN = 8
        E_ZERO = 4
        E_TOT = E_FFN + E_ZERO
        TOP_K = 2
        key = jax.random.key(seed)
        k1, k2, k3, k4 = jax.random.split(key, 4)
        x = jax.random.normal(k1, (B, S, D), dtype=jnp.float32)
        gate_w = jax.random.normal(k2, (E_TOT, D), dtype=jnp.float32) * (1.0 / np.sqrt(D))
        expert_bias = jnp.zeros((E_TOT,), dtype=jnp.float32)
        w1 = jax.random.normal(k3, (E_FFN, DFF, D), dtype=jnp.float32) * (1.0 / np.sqrt(D))
        w2 = jax.random.normal(k4, (E_FFN, D, DFF), dtype=jnp.float32) * (1.0 / np.sqrt(DFF))
        return {'x': x, 'gate_w': gate_w, 'expert_bias': expert_bias, 'w1': w1, 'w2': w2}
    _L1_ffn_in = _L1_ffn_setup()
    _d = {'L0_attn_x': _L0_attn_in['x'], 'L0_attn_w_qkv': _L0_attn_in['w_qkv'], 'L0_attn_b_qkv': _L0_attn_in['b_qkv'], 'L0_attn_w_out': _L0_attn_in['w_out'], 'L0_attn_b_out': _L0_attn_in['b_out'], 'L0_ffn_router_w': _L0_ffn_in['router_w'], 'L0_ffn_router_b': _L0_ffn_in['router_b'], 'L0_ffn_experts_inter': _L0_ffn_in['experts_inter'], 'L0_ffn_experts_out': _L0_ffn_in['experts_out'], 'L1_attn_q_w': _L1_attn_in['q_w'], 'L1_attn_q_b': _L1_attn_in['q_b'], 'L1_attn_k_w': _L1_attn_in['k_w'], 'L1_attn_k_b': _L1_attn_in['k_b'], 'L1_attn_v_w': _L1_attn_in['v_w'], 'L1_attn_v_b': _L1_attn_in['v_b'], 'L1_attn_o_w': _L1_attn_in['o_w'], 'L1_attn_o_b': _L1_attn_in['o_b'], 'L1_attn_qn_scale': _L1_attn_in['qn_scale'], 'L1_attn_kn_scale': _L1_attn_in['kn_scale'], 'L1_ffn_gate_w': _L1_ffn_in['gate_w'], 'L1_ffn_expert_bias': _L1_ffn_in['expert_bias'], 'L1_ffn_w1': _L1_ffn_in['w1'], 'L1_ffn_w2': _L1_ffn_in['w2']}
    _x0 = _d['L0_attn_x']
    _d['L0_attn_x'] = jax.random.normal(jax.random.fold_in(jax.random.key(seed), 1), (8, 512, 256), dtype=_x0.dtype)
    del _x0
    return _d

def reference(L0_attn_x, L0_attn_w_qkv, L0_attn_b_qkv, L0_attn_w_out, L0_attn_b_out, L0_ffn_router_w, L0_ffn_router_b, L0_ffn_experts_inter, L0_ffn_experts_out, L1_attn_q_w, L1_attn_q_b, L1_attn_k_w, L1_attn_k_b, L1_attn_v_w, L1_attn_v_b, L1_attn_o_w, L1_attn_o_b, L1_attn_qn_scale, L1_attn_kn_scale, L1_ffn_gate_w, L1_ffn_expert_bias, L1_ffn_w1, L1_ffn_w2):

    def _L0_attn_ref(x, w_qkv, b_qkv, w_out, b_out):
        import jax, jax.numpy as jnp
        import numpy as np
        NUM_HEADS = 16
        B, S, H = x.shape
        nh = NUM_HEADS
        hd = H // nh
        attn_scale = 1.0 / np.sqrt(hd).astype(np.float32)
        qkv = x @ w_qkv + b_qkv
        q, k, v = jnp.split(qkv, 3, axis=-1)
        to_heads = lambda t: t.reshape(B, S, nh, hd).transpose(0, 2, 1, 3)
        q, k, v = (to_heads(q), to_heads(k), to_heads(v))
        scores = jnp.einsum('bhid,bhjd->bhij', q, k) * attn_scale
        i = jnp.arange(S)[:, None]
        j = jnp.arange(S)[None, :]
        scores = jnp.where(j >= i, scores, -jnp.inf)
        attn = jax.nn.softmax(scores, axis=-1)
        out = jnp.einsum('bhij,bhjd->bhid', attn, v)
        out = out.transpose(0, 2, 1, 3).reshape(B, S, H)
        return out @ w_out + b_out

    def _L0_ffn_ref(x, router_w, router_b, experts_inter, experts_out):
        import math
        import jax, jax.numpy as jnp
        import numpy as np
        NUM_EXPERTS = 8
        TOP_K = 2
        CAPACITY_FACTOR = 1.0
        B, S, H, I = (4, 512, 256, 1024)
        batch, seq, hidden = x.shape
        n_exp = router_w.shape[0]
        n_tok = batch * seq
        cap = math.ceil(n_tok / n_exp * CAPACITY_FACTOR)
        logits = jnp.einsum('bsh,eh->bse', x, router_w) + router_b
        weights_flat = jax.nn.softmax(logits, axis=-1).reshape(n_tok, n_exp)
        x_flat = x.reshape(n_tok, hidden)
        topk_vals, topk_idx = jax.lax.top_k(weights_flat, TOP_K)
        rows = jnp.arange(n_tok)[:, None]
        topk_flat = jnp.zeros_like(weights_flat).at[rows, topk_idx].set(topk_vals)
        routing_mask = (topk_flat > 0).astype(jnp.int32)
        noop_w = topk_flat[:, -1]
        noop_mask = routing_mask[:, -1].astype(x.dtype)
        expert_w = topk_flat[:, :-1]
        expert_mask = routing_mask[:, :-1]
        sorted_indices = jnp.argsort(-expert_mask, axis=0)[:cap]
        sorted_mask = jnp.take_along_axis(expert_mask, sorted_indices, axis=0)
        used_idx = (sorted_indices * sorted_mask).reshape(-1)
        inputs = x_flat[used_idx] * sorted_mask.reshape(-1).astype(x.dtype)[:, None]
        inputs = inputs.reshape(cap, n_exp - 1, hidden)
        in_w = jnp.take_along_axis(expert_w, sorted_indices, axis=0)
        h = jax.nn.relu(jnp.einsum('ceh,ehi->cei', inputs, experts_inter))
        out = jnp.einsum('cei,eih->ceh', h, experts_out) * in_w[..., None]
        combined = jnp.zeros_like(x_flat).at[used_idx].add(out.reshape(-1, hidden))
        combined = combined + x_flat * (noop_w * noop_mask)[:, None]
        return combined.reshape(batch, seq, hidden)

    def _L1_attn_ref(x, q_w, q_b, k_w, k_b, v_w, v_b, o_w, o_b, qn_scale, kn_scale):
        import jax, jax.numpy as jnp
        import numpy as np
        D = 256
        H = 16
        HD = D // H
        ROPE_BASE = 10000.0
        EPS_RMS = 1e-08
        EPS_RENORM = 1e-08

        def rms_norm(x, scale):
            norm = jnp.mean(x * x, axis=-1, keepdims=True)
            return scale * (x * jax.lax.rsqrt(norm + EPS_RMS))

        def rope_tables(seq_len):
            inv_freq = 1.0 / ROPE_BASE ** (jnp.arange(0, HD, 2, dtype=jnp.float32) / HD)
            t = jnp.arange(seq_len, dtype=jnp.float32)
            freqs = t[:, None] * inv_freq[None, :]
            emb = jnp.concatenate([freqs, freqs], axis=-1)
            return (jnp.cos(emb), jnp.sin(emb))

        def apply_rotary(x, cos, sin):
            x1 = x[..., ::2]
            x2 = x[..., 1::2]
            x_rot = jnp.stack([-x2, x1], axis=-1).reshape(x.shape)
            return x * cos + x_rot * sin
        B, L, _ = x.shape
        q = rms_norm(x, qn_scale) @ q_w.T + q_b
        k = rms_norm(x, kn_scale) @ k_w.T + k_b
        v = x @ v_w.T + v_b
        q = q.reshape(B, L, H, HD).transpose(0, 2, 1, 3)
        k = k.reshape(B, L, H, HD).transpose(0, 2, 1, 3)
        v = v.reshape(B, L, H, HD).transpose(0, 2, 1, 3)
        cos, sin = rope_tables(L)
        q = apply_rotary(q, cos, sin)
        k = apply_rotary(k, cos, sin)
        scale = 1.0 / np.sqrt(HD)
        scores = jnp.einsum('bhqd,bhkd->bhqk', q, k) * scale
        weights = jax.nn.sigmoid(scores)
        weights = weights / (jnp.sum(weights, axis=-1, keepdims=True) + EPS_RENORM)
        attn = jnp.einsum('bhqk,bhkd->bhqd', weights, v)
        attn = attn.transpose(0, 2, 1, 3).reshape(B, L, D)
        return attn @ o_w.T + o_b

    def _L1_ffn_ref(x, gate_w, expert_bias, w1, w2):
        import jax, jax.numpy as jnp
        import numpy as np
        B, S, D = (2, 512, 256)
        DFF = 512
        E_FFN = 8
        E_ZERO = 4
        E_TOT = E_FFN + E_ZERO
        TOP_K = 2
        logits = jnp.einsum('btd,ed->bte', x, gate_w) + expert_bias
        topk_logits, topk_idx = jax.lax.top_k(logits, TOP_K)
        topk_w = jax.nn.softmax(topk_logits, axis=-1)
        onehot = jax.nn.one_hot(topk_idx, E_TOT, dtype=x.dtype)
        w = jnp.einsum('btk,btke->bte', topk_w, onehot)
        w_ffn = w[..., :E_FFN]
        w_zero = jnp.sum(w[..., E_FFN:], axis=-1)
        h = jax.nn.silu(jnp.einsum('btd,efd->btef', x, w1))
        y = jnp.einsum('btef,edf->bted', h, w2)
        out = jnp.einsum('bte,bted->btd', w_ffn, y) + w_zero[..., None] * x
        return out
    x = L0_attn_x
    x = _layernorm(x + _L0_attn_ref(x, L0_attn_w_qkv, L0_attn_b_qkv, L0_attn_w_out, L0_attn_b_out), axis=-1)
    x = _layernorm(x + _L0_ffn_ref(x, L0_ffn_router_w, L0_ffn_router_b, L0_ffn_experts_inter, L0_ffn_experts_out), axis=-1)
    x = _layernorm(x + _L1_attn_ref(x, L1_attn_q_w, L1_attn_q_b, L1_attn_k_w, L1_attn_k_b, L1_attn_v_w, L1_attn_v_b, L1_attn_o_w, L1_attn_o_b, L1_attn_qn_scale, L1_attn_kn_scale), axis=-1)
    x = _layernorm(x + _L1_ffn_ref(x, L1_ffn_gate_w, L1_ffn_expert_bias, L1_ffn_w1, L1_ffn_w2), axis=-1)
    return x

_drawn_inputs = setup_inputs


def setup_inputs(seed=0):
    import zlib

    import numpy as np

    out = dict(_drawn_inputs(seed))
    spreads = {'L0_ffn_router_b': (0.0, 0.1),
     'L1_attn_qn_scale': (1.0, 0.6),
     'L1_attn_kn_scale': (1.0, 0.6),
     'L1_ffn_expert_bias': (0.0, 0.1)}
    factors = {'L1_attn_q_w': 3.932, 'L1_attn_q_b': 34.291, 'L1_attn_k_w': 4.352, 'L1_attn_k_b': 51.09}
    for name, (base, spread) in spreads.items():
        noise = np.random.default_rng([zlib.crc32(name.encode()), seed]).standard_normal(out[name].shape)
        drawn = base * np.exp(spread * noise) if base else spread * noise
        out[name] = jnp.asarray(drawn.astype(out[name].dtype))
    for name, factor in factors.items():
        out[name] = (out[name] * factor).astype(out[name].dtype)
    return out
```

```python
from contextlib import ExitStack

import numpy as np

import concourse.bass as bass
from concourse import mybir

F32 = mybir.dt.float32
BF16 = mybir.dt.bfloat16
I32 = mybir.dt.int32
ALU = mybir.AluOpType
ACT = mybir.ActivationFunctionType
AX_X = mybir.AxisListType.X

P = 128
NB, S, D = 8, 512, 256
NH, HD = 16, 16
TB = S // P
CD = D // P
GH = 4
NG = NH // GH
E0, I0, CAP = 7, 1024, 512
NE0 = E0 + 1
E1, F1, NE1 = 8, 512, 12
NTOK = NB * S
SEG = NTOK + P
ZROW = E1 * SEG
NBLK = 2 * NTOK // P + E1
LN_EPS, RMS_EPS, SUM_EPS = 1e-5, 1e-8, 1e-8
ATT_SCALE = 0.25
FAR = float(1 << 20)
LOW = -3.0e38
NPROD = 6
SK = NPROD * HD
RING = 4
RSQRT_MAGIC = 1597463007.0

PRODUCTS = [(0, 0), (0, 1), (1, 0), (1, 1), (0, 2), (2, 0)]

UNITS_CAUSAL = [
    [(3, 0, 256, 0)],
    [(2, 0, 256, 0)],
    [(1, 0, 256, 0)],
    [(3, 256, 256, 0)],
    [(0, 0, 128, 0), (2, 256, 128, 128)],
]
UNITS_FULL = [[(kb, qh * 256, 256, 0)] for qh in range(2) for kb in range(TB)]
DIAGONAL = {2: (128, 1), 3: (128, 1), 4: (0, 2)}


def wait(eng, sem, value):
    if isinstance(value, int) and value <= 0:
        return
    eng.wait_ge(sem, value)


class Turn:

    def __init__(self, kind, s, it=None):
        self.kind, self.s, self.it = kind, s, it

    def batch(self, d):
        if self.it is None:
            k = self.s - d
            return k, k % 2, k // 2
        k = self.s - d
        return self.it * 2 + k, k % 2, (self.it + (k // 2) if k // 2 else self.it)


def passes(eng, n, one):
    one(0)
    with eng.Fori(1, n) as it:
        one(it)


CHUNKS = (0, 2, 1, 3)

KINDS = ("first", "second", "body", "eighth", "ninth")


def slots(eng, emit):
    emit(Turn("first", 0))
    emit(Turn("second", 1))

    def two(it):
        emit(Turn("body", 2, it))
        emit(Turn("body", 3, it))
    passes(eng, (NB - 2) // 2, two)
    emit(Turn("eighth", NB))
    emit(Turn("ninth", NB + 1))


def schedule(causal, kind):
    prep = kind in ("first", "second", "body")
    attn = kind in ("second", "body", "eighth")
    route = kind in ("body", "eighth", "ninth")
    prep_steps = [("xT", c) for c in range(CD)]
    if causal:
        prep_steps += [("qk", j) for j in CHUNKS] + [("v", i) for i in range(2)]
    else:
        prep_steps += [("qk", 0), ("qk", 2), ("ro", 0), ("qk", 1), ("ro", 2), ("qk", 3), ("ro", 1), ("v", 0),
                       ("ro", 3), ("v", 1)]
    route_steps = [("rT", 0), ("rT", 1), ("lg", 0), ("ex", 0), ("rt", 0), ("ps", 0)]
    route_steps += [("sc", i) for i in range(2 * TB)]
    others = []
    if causal:
        if prep:
            others += prep_steps + [("st_q", 0)]
        if route:
            others += route_steps
        if prep:
            others += [("mx", h) for h in range(NH)] + [("mr", 0)]
    else:
        if prep:
            others += [("gi", 0)] + [("ga", i) for i in range(2 * TB)] + [("cb", 0)]
        if route:
            others += route_steps
        if prep:
            others += prep_steps + [("st_q", 0)]
    units = []
    per_group = 5 if causal else 8
    n_units = NG * per_group
    if attn:
        for n in range(n_units + 2):
            if n < n_units:
                units.append([("st", n)])
            else:
                units.append([])
            if n >= 2:
                units[-1].append(("av", n - 2))
                if (n - 2) % per_group == per_group - 1:
                    units[-1].append(("oe", (n - 2) // per_group))
            if n >= 4 and (n - 4) % per_group == per_group - 1:
                units[-1].append(("on", (n - 4) // per_group))
    out = [("xl", 0)] if prep else []
    out += [("xp", 0)] if attn else []
    if not units:
        return out + others
    done = 0
    for i, u in enumerate(units):
        upto = len(others) * (i + 1) // len(units)
        out += others[done:upto] + u
        done = upto
    out += [("on", NG - 1)]
    out += [("oT", 0), ("oT", 1), ("y", 0), ("y", 1), ("ln", 0)]
    return out


def bank_keys(causal, kind):
    keys = []
    for step, n in schedule(causal, kind):
        if step in ("xT", "qk", "ro", "v", "on", "oT", "y", "rT", "lg", "ps", "mr"):
            keys.append((step, n))
        elif step == "mx":
            keys += [("mx", (n, qb)) for qb in range(TB)]
    return keys


class Banks:

    def __init__(self, causal, ready, free, memory):
        self.ready, self.free, self.memory = ready, free, memory
        self.n = len(memory)
        self.place, self.uses = {}, {}
        for kind in KINDS:
            keys = bank_keys(causal, kind)
            self.place[kind] = {key: (i % self.n, i // self.n) for i, key in enumerate(keys)}
            self.uses[kind] = [sum(i % self.n == b for i in range(len(keys))) for b in range(self.n)]

    def base(self, turn, b):
        u = {kind: self.uses[kind][b] for kind in KINDS}
        if turn.kind == "first":
            return 0
        if turn.kind == "second":
            return u["first"]
        before = u["first"] + u["second"]
        if turn.kind == "body":
            return turn.it * (2 * u["body"]) + (before + (turn.s - 2) * u["body"])
        before += (NB - 2) * u["body"]
        return before if turn.kind == "eighth" else before + u["eighth"]

    def acquire(self, pe, turn, key):
        b, n = self.place[turn.kind][key]
        wait(pe, self.free[b], self.base(turn, b) + n)
        return self.memory[b], self.ready[b]

    def filled(self, eng, turn, key):
        b, n = self.place[turn.kind][key]
        eng.wait_ge(self.ready[b], self.base(turn, b) + (n + 1))
        return self.memory[b], self.free[b]

    def read(self, eng, turn, key):
        b, n = self.place[turn.kind][key]
        eng.wait_ge(self.free[b], self.base(turn, b) + (n + 1))

    def total(self, b):
        u = {kind: self.uses[kind][b] for kind in KINDS}
        return sum(u.values()) + (NB - 3) * u["body"]

    def all_before_read(self, eng, turn):
        for b in range(self.n):
            wait(eng, self.free[b], self.base(turn, b))


class Chain:

    def __init__(self, eng, sem, base):
        self.eng, self.sem, self.base, self.n = eng, sem, base, 0

    def __call__(self, instruction):
        self.n += 1
        instruction.then_inc(self.sem, 1)
        self.eng.wait_ge(self.sem, self.base + self.n)

    def unwaited(self, instruction):
        self.n += 1
        instruction.then_inc(self.sem, 1)

    def join(self):
        self.eng.wait_ge(self.sem, self.base + self.n)


RSQRT_STEPS = 13


def rsqrt(dve, chain, out, x, tmp):
    chain(dve.tensor_scalar(out.bitcast(I32), x.bitcast(I32), -0.5, RSQRT_MAGIC, ALU.mult, ALU.add))
    for _ in range(3):
        chain(dve.tensor_tensor(tmp, out, out, ALU.mult))
        chain(dve.tensor_tensor(tmp, tmp, x, ALU.mult))
        chain(dve.tensor_scalar(tmp, tmp, -0.5, 1.5, ALU.mult, ALU.add))
        chain(dve.tensor_tensor(out, out, tmp, ALU.mult))


def spread(ap, n):
    return ap.unsqueeze(2).broadcast_to([ap.shape[0], ap.shape[1], n])


def build(nc, a, out):
    with ExitStack() as ctx:
        def sb(name, shape, dt=F32):
            return ctx.enter_context(nc.sbuf_tensor(name, shape, dt))

        def psum(name, shape, dt=F32):
            return ctx.enter_context(nc.psum_tensor(name, shape, dt))

        def sem(name):
            return ctx.enter_context(nc.semaphore(name))

        def dram(name, shape, dt=F32):
            return nc.dram_tensor(name, shape, dt, kind="Internal").ap()

        parts = dram("qk_parts", [2, 2, 3, D, S], BF16)
        x1_dram = dram("x1_rows", [NTOK, D])
        x3_dram = dram("x3_rows", [NTOK, D])
        slot_x0 = dram("slot_x0", [E0 * CAP, D])
        slot_y0 = dram("slot_y0", [E0 * CAP, D])
        slot_x1 = dram("slot_x1", [ZROW + P, D])
        slot_y1 = dram("slot_y1", [NBLK * P, D])

        ident = sb("ident", [P, P])
        ident_b = sb("ident_b", [P, P], BF16)
        before = sb("before", [P, P], BF16)
        ones_b = sb("ones_b", [P, P], BF16)
        mask = sb("mask", [P, S])
        rot = sb("rot", [P, P])
        cos_t = sb("cos_t", [P, S])
        sin_t = sb("sin_t", [P, S])
        lane = sb("lane", [P, 304])
        zero = sb("zero", [P, D])

        arena = sb("arena", [P, 21504])
        stack_words = NH * S // 2
        Q = [arena[:, i * stack_words:(i + 1) * stack_words].bitcast(BF16).rearrange("p (h n) -> p h n", h=NH)
             for i in (0, 1)]
        K = [arena[:, i * stack_words:(i + 1) * stack_words].bitcast(BF16).rearrange("p (h n) -> p h n", h=NH)
             for i in (2, 3)]
        pt_at = 4 * stack_words
        PT = [arena[:, pt_at + i * 1024:pt_at + (i + 1) * 1024].rearrange("p (h n) -> p h n", h=GH)
              for i in range(RING)]

        w_qkv = sb("w_qkv", [P, CD, 3 * D])
        w_o = sb("w_o", [P, CD, D])
        w_r = sb("w_r", [P, CD, NE1])
        b_qk = sb("b_qk", [P, 4])
        b_v = sb("b_v", [P, D])
        b_o = sb("b_o", [P, D])
        rn_scale = sb("rn_scale", [P, 2, CD])
        x_in = [sb(f"x_in{i}", [P, TB, D]) for i in range(2)]
        xT = sb("xT", [P, CD, S])
        qk_src = [sb(f"qk_src{j}", [P, 3, S], BF16) for j in range(4)]
        qk_rest = [sb(f"qk_rest{i}", [P, S]) for i in range(2)]
        v_aug = [sb(f"v_aug{i}", [P, TB, NH, 32]) for i in range(2)]
        oT_raw = [sb(f"oT_raw{i}", [P, S]) for i in range(2)]
        o_nat = sb("o_nat", [P, TB, D])
        oT = sb("oT", [P, CD, S])
        x_res = sb("x_res", [P, TB, D])
        y_b = sb("y_b", [P, TB, D])
        x_out = [sb(f"x_out{i}", [P, TB, D]) for i in range(2)]
        rT = oT
        scratch = sb("scratch", [P, S])
        junk = [scratch[:, i * (S // 2):(i + 1) * (S // 2)].bitcast(BF16) for i in range(2)]
        mx = sb("mx", [P, NH * TB])
        mx_rest = sb("mx_rest", [P, NH * TB])
        mx_parts = sb("mx_parts", [P, 3, NH * TB], BF16)
        mx_rows = sb("mx_rows", [NH * TB, 3, P], BF16)
        o_sum = sb("o_sum", [P, TB * GH])
        stats = sb("stats", [P, TB, 6])
        mv = sb("mv", [P, TB, 2])
        small = sb("small", [P, 16, TB])
        NEM = NE1
        r_lg = sb("r_lg", [P, TB, NEM])
        r_w = sb("r_w", [P, TB, NEM])
        r_c = sb("r_c", [P, TB, NEM])
        r_oh = sb("r_oh", [P, 2, TB, NEM])
        r_pos = sb("r_pos", [P, TB, NEM])
        r_s = sb("r_s", [P, 24, TB])
        r_mask = sb("r_mask", [P, TB, NEM], BF16)
        r_before = sb("r_before", [P, TB + 1, NEM], BF16)
        row_to = [sb(f"row_to{i}", [P, TB, 2], I32) for i in range(2)]
        row_from0 = sb("row_from0", [P, NB, TB * 2], I32)
        gate0 = sb("gate0", [P, NB, TB * 3])
        row_now = [sb(f"row_now{i}", [P, TB * 2], I32) for i in range(2)]

        ST = [psum(f"ST{i}", [P, 1024]) for i in range(2)]
        OT = psum("OT", [P, 512])
        shared = [psum(f"shared{i}", [P, 512]) for i in range(3)]

        s_const = sem("s_const")
        s_fill = sem("s_fill")
        s_fill2 = sem("s_fill2")
        s_zero = sem("s_zero")
        s_tick = sem("s_tick")

        def settle(eng):
            eng.sem_inc(s_tick, 1)

        def layer_sems(t):
            names = dict(
                weights="weights", xp="residual_ready", q1="first_part", q2="second_part", q3="third_part",
                rest="rest_ready", parts_saved="parts_saved",
                st="scores_ready", exp="weights_ready", sel="masked", av="unit_used", oe="out_saved",
                osum="out_sum_ready", ttr="max_taken", mchain="max_split", mrow="max_rows_saved",
                lnc="norm_chain", x_out="x_out_ready", rc="route_chain", ex="route_exp", ga_idx="rows_known",
                comb="combine_chain", xn="xn_ready", rot="rotated", rope="rope_chain", qf="qk_biased",
                wprep="weights_scaled")
            d = {k: sem(f"{t}_{v}") for k, v in names.items()}
            for k in ("x_load", "stacked", "scattered", "x_saved", "gathered"):
                d[k] = [sem(f"{t}_{k}{i}") for i in range(2)]
            d["ready"] = [sem(f"{t}_bank_ready{i}") for i in range(3)]
            d["free"] = [sem(f"{t}_bank_free{i}") for i in range(3)]
            return d

        LA = layer_sems("a")
        banks_a = Banks(True, LA["ready"], LA["free"], shared)
        U0 = NG * len(UNITS_CAUSAL)

        ROUTE0 = 46
        LN_CHAIN = TB + TB + 1 + RSQRT_STEPS

        block = ctx.enter_context(nc.Block())

        def a_sp(sp):
            L = LA

            def emit(turn):
                for step, n in schedule(True, turn.kind):
                    if step == "xl":
                        k, par, half = turn.batch(0)
                        wait(sp, L["xp"], k - 1)
                        settle(sp)
                        sp.dma_start(x_in[par][:, :, :],
                                     a["x"][bass.ds(k * S, S), :].rearrange("(t p) d -> p t d", p=P)
                                     ).then_inc(L["x_load"][par], 16)
                    elif step == "qk":
                        k, par, half = turn.batch(0)
                        order = CHUNKS.index(n)
                        wait(sp, L["stacked"][par], half * (192))
                        settle(sp)
                        sp.wait_ge(L["q3"], k * 4 + (order + 1))
                        settle(sp)
                        sp.dma_start(parts[par, n // 2, :, (n % 2) * P:(n % 2 + 1) * P, :].rearrange("j p n -> p j n"),
                                     qk_src[n][:, :, :]).then_inc(L["parts_saved"], 16)
                    elif step == "st_q":
                        k, par, half = turn.batch(0)
                        sp.wait_ge(L["parts_saved"], k * 64 + 64)
                        settle(sp)
                        wait(sp, L["exp"], (k - 1) * U0)
                        settle(sp)
                        for t, (i, j) in enumerate(PRODUCTS):
                            for side, part, stack in ((0, i, Q), (1, j, K)):
                                sp.dma_start(stack[par][t * HD:(t + 1) * HD, :, :],
                                             parts[par, side, part].rearrange("(h d) n -> d h n", d=HD)
                                             ).then_inc(L["stacked"][par], 16)
                    elif step == "mr":
                        k, par, half = turn.batch(0)
                        banks_a.read(sp, turn, ("mr", 0))
                        for j in range(3):
                            sp.dma_start(Q[par][SK + j:SK + j + 1, :, :].rearrange("p h (b n) -> p (h b) n", b=TB),
                                         mx_rows[:, j, :]).then_inc(L["mrow"], 16)
                    elif step == "ln":
                        k, par, half = turn.batch(1)
                        sp.wait_ge(L["x_out"], k * TB + TB)
                        settle(sp)
                        sp.dma_start(x1_dram[bass.ds(k * S, S), :].rearrange("(t p) d -> p t d", p=P),
                                     x_out[par][:, :, :]).then_inc(L["x_saved"][par], 16)
            slots(sp, emit)

        def attention_pe(pe, L, banks, causal, turn, step, n, U):
            k, par, half = turn.batch(1)
            units = UNITS_CAUSAL if causal else UNITS_FULL
            per = len(units)
            rows = SK + 3 if causal else SK
            if step == "st":
                if n == 0:
                    banks.all_before_read(pe, turn)
                    if causal:
                        pe.wait_ge(L["mrow"], k * 48 + 48)
                    else:
                        pe.wait_ge(L["stacked"][par], half * 192 + 192)
                wait(pe, L["exp"], k * U + (n - 1))
                g, u = n // per, n % per
                for i in range(GH):
                    h = g * GH + i
                    for kb, q0, nq, at in units[u]:
                        mm = pe.matmul(ST[n % 2][:, i * 256 + at:i * 256 + at + nq],
                                       K[par][0:rows, h, kb * P:(kb + 1) * P],
                                       Q[par][0:rows, h, q0:q0 + nq], start=True, stop=True)
                mm.then_inc(L["st"], 1)
            elif step == "av":
                g, u = n // per, n % per
                if u == 0:
                    wait(pe, L["oe"], k * NG + g)
                if causal and u in DIAGONAL:
                    pe.wait_ge(L["sel"], k * (3 * NG) + (g * 3 + sorted(DIAGONAL).index(u) + 1))
                else:
                    pe.wait_ge(L["exp"], k * U + (n + 1))
                for piece, (kb, q0, nq, at) in enumerate(units[u]):
                    for i in range(GH):
                        mm = pe.matmul(OT[32 * i:32 * i + 32, q0:q0 + nq],
                                       v_aug[par][:, kb, g * GH + i, :],
                                       PT[n % RING][:, i, at:at + nq],
                                       start=(u == 0), stop=(u == per - 1),
                                       skip_group_check=True, tile_position=(0, 32 * i))
                mm.then_inc(L["av"], 1)
            elif step == "on":
                bank, ready = banks.acquire(pe, turn, ("on", n))
                pe.wait_ge(L["oe"], k * NG + (n + 1))
                for t in range(TB):
                    mm = pe.transpose(bank[:, t * P:(t + 1) * P], oT_raw[n % 2][:, t * P:(t + 1) * P], ident[:, :])
                mm.then_inc(ready, 1)
            elif step == "oT":
                bank, ready = banks.acquire(pe, turn, ("oT", n))
                if n == 0:
                    banks.read(pe, turn, ("on", NG - 1))
                for t in range(TB):
                    mm = pe.transpose(bank[:, t * P:(t + 1) * P], o_nat[:, t, n * P:(n + 1) * P], ident[:, :])
                mm.then_inc(ready, 1)
            elif step == "y":
                bank, ready = banks.acquire(pe, turn, ("y", n))
                if n == 0:
                    banks.read(pe, turn, ("oT", 0))
                    banks.read(pe, turn, ("oT", 1))
                for t in (2 * n, 2 * n + 1):
                    for c in range(CD):
                        mm = pe.matmul(bank[:, (t % 2) * D:(t % 2 + 1) * D], oT[:, c, t * P:(t + 1) * P],
                                       w_o[:, c, :], start=(c == 0), stop=(c == CD - 1))
                mm.then_inc(ready, 1)

        def route_pe(pe, L, banks, turn, step, n, ne, chain_len, mask_at):
            k, par, half = turn.batch(2)
            if step == "rT":
                bank, ready = banks.acquire(pe, turn, ("rT", n))
                pe.wait_ge(L["x_out"], k * TB + TB)
                for t in range(TB):
                    mm = pe.transpose(bank[:, t * P:(t + 1) * P], x_out[par][:, t, n * P:(n + 1) * P], ident[:, :])
                mm.then_inc(ready, 1)
            elif step == "lg":
                bank, ready = banks.acquire(pe, turn, ("lg", 0))
                banks.read(pe, turn, ("rT", 0))
                banks.read(pe, turn, ("rT", 1))
                for t in range(TB):
                    for c in range(CD):
                        mm = pe.matmul(bank[:, t * ne:(t + 1) * ne], rT[:, c, t * P:(t + 1) * P],
                                       w_r[:, c, 0:ne], start=(c == 0), stop=(c == CD - 1))
                mm.then_inc(ready, 1)
            elif step == "ps":
                bank, ready = banks.acquire(pe, turn, ("ps", 0))
                pe.wait_ge(L["rc"], k * chain_len + mask_at)
                for t in range(TB):
                    pe.matmul(bank[:, t * ne:(t + 1) * ne], before[:, :], r_mask[:, t, 0:ne],
                              start=True, stop=False)
                    mm = pe.matmul(bank[:, t * ne:(t + 1) * ne], ones_b[:, :], r_before[:, t, 0:ne],
                                   start=False, stop=True)
                mm.then_inc(ready, 1)

        def a_pe(pe):
            L, banks = LA, banks_a
            pe.wait_ge(s_const, CONST_DMAS * 16)
            pe.wait_ge(s_fill2, 1)

            def emit(turn):
                for step, n in schedule(True, turn.kind):
                    k, par, half = turn.batch(0)
                    if step == "xT":
                        bank, ready = banks.acquire(pe, turn, ("xT", n))
                        if n == 0:
                            pe.wait_ge(L["x_load"][par], half * 16 + 16)
                        for t in range(TB):
                            mm = pe.transpose(bank[:, t * P:(t + 1) * P], x_in[par][:, t, n * P:(n + 1) * P],
                                              ident[:, :])
                        mm.then_inc(ready, 1)
                    elif step == "qk":
                        bank, ready = banks.acquire(pe, turn, ("qk", n))
                        if n == 0:
                            banks.read(pe, turn, ("xT", 0))
                            banks.read(pe, turn, ("xT", 1))
                        for c in range(CD):
                            mm = pe.matmul(bank[:, :], w_qkv[:, c, n * P:(n + 1) * P], xT[:, c, :],
                                           start=(c == 0), stop=(c == CD - 1))
                        mm.then_inc(ready, 1)
                    elif step == "v":
                        bank, ready = banks.acquire(pe, turn, ("v", n))
                        for t in (2 * n, 2 * n + 1):
                            for c in range(CD):
                                mm = pe.matmul(bank[:, (t % 2) * D:(t % 2 + 1) * D], xT[:, c, t * P:(t + 1) * P],
                                               w_qkv[:, c, 2 * D:3 * D], start=(c == 0), stop=(c == CD - 1))
                        mm.then_inc(ready, 1)
                    elif step == "mx":
                        if n == 0:
                            pe.wait_ge(L["stacked"][par], half * 192 + 192)
                        for qb in range(TB):
                            bank, ready = banks.acquire(pe, turn, ("mx", (n, qb)))
                            pe.matmul(bank[:, 0:S - qb * P], Q[par][0:SK, n, qb * P:(qb + 1) * P],
                                      K[par][0:SK, n, qb * P:S], start=True, stop=True).then_inc(ready, 1)
                    elif step == "mr":
                        bank, ready = banks.acquire(pe, turn, ("mr", 0))
                        pe.wait_ge(L["mchain"], k * 5 + 5)
                        settle(pe)
                        for j in range(3):
                            mm = pe.transpose(bank[0:NH * TB, j * 64:(j + 1) * 64].bitcast(BF16),
                                              mx_parts[:, j, :], ident_b[:, :])
                        mm.then_inc(ready, 1)
                    elif step in ("st", "av", "on", "oT", "y"):
                        attention_pe(pe, L, banks, True, turn, step, n, U0)
                    elif step in ("rT", "lg", "ps"):
                        route_pe(pe, L, banks, turn, step, n, NE0, ROUTE0, MASK0)
            slots(pe, emit)

        def attention_act(act, L, causal, turn, step, n, U, func):
            k, par, half = turn.batch(1)
            if step == "st":
                act.wait_ge(L["st"], k * U + (n + 1))
                wait(act, L["av"], k * U + (n + 1 - RING))
                act.activation(PT[n % RING][:, :, :], ST[n % 2][:, :].rearrange("p (h n) -> p h n", h=GH),
                               func, scale=ATT_SCALE).then_inc(L["exp"], 1)
            elif step == "oe":
                per = U // NG
                act.wait_ge(L["av"], k * U + (n + 1) * per)
                act.activation(oT_raw[n % 2][:, :], OT[:, :], ACT.Identity).then_inc(L["oe"], 1)

        def copy_bank(act, banks, turn, key, to):
            bank, free = banks.filled(act, turn, key)
            act.activation(to, bank[:, :], ACT.Identity).then_inc(free, 1)

        def a_act(act):
            L, banks = LA, banks_a
            act.wait_ge(s_const, CONST_DMAS * 16)

            def emit(turn):
                for step, n in schedule(True, turn.kind):
                    k, par, half = turn.batch(0)
                    if step == "xT":
                        copy_bank(act, banks, turn, ("xT", n), xT[:, n, :])
                    elif step == "qk":
                        bank, free = banks.filled(act, turn, ("qk", n))
                        wait(act, L["parts_saved"], k * 64)
                        act.activation(qk_src[n][:, 0, :], bank[:, :], ACT.Identity,
                                       bias=b_qk[:, n:n + 1]).then_inc(L["q1"], 1)
                    elif step in ("st", "oe"):
                        attention_act(act, L, True, turn, step, n, U0, ACT.Exp)
                    elif step == "oT":
                        copy_bank(act, banks, turn, ("oT", n), oT[:, n, :])
                    elif step == "rT":
                        copy_bank(act, banks, turn, ("rT", n), rT[:, n, :])
                    elif step == "ex":
                        k, par, half = turn.batch(2)
                        act.wait_ge(L["rc"], k * ROUTE0 + 3)
                        act.activation(r_w[:, :, 0:NE0], r_w[:, :, 0:NE0], ACT.Exp).then_inc(L["ex"], 1)
            slots(act, emit)

        def norm_dve(dve, L, k, src, dst, chain):
            for t in range(TB):
                chain.unwaited(dve.bn_stats(stats[:, t, :], src[:, t, :]))
            chain.join()
            settle(dve)
            for t in range(TB):
                chain.unwaited(dve.bn_aggr(mv[:, t, :], stats[:, t, :]))
            chain.join()
            chain(dve.tensor_scalar(small[:, 0, :], mv[:, :, 1], LN_EPS, None, ALU.add))
            rsqrt(dve, chain, small[:, 1, :], small[:, 0, :], small[:, 2, :])

        def attention_dve(dve, L, banks, turn, step, n, eps):
            k, par, half = turn.batch(1)
            if step == "on":
                bank, free = banks.filled(dve, turn, ("on", n))
                view = bank[:, :].rearrange("p (th c) -> p th c", c=32)
                if n:
                    banks.read(dve, turn, ("on", n - 1))
                if eps:
                    dve.tensor_scalar(o_sum[:, :], view[:, :, HD], eps, None, ALU.add).then_inc(L["osum"], 1)
                    dve.wait_ge(L["osum"], k * (2 * NG) + (2 * n + 1))
                    dve.reciprocal(o_sum[:, :], o_sum[:, :]).then_inc(L["osum"], 1)
                    dve.wait_ge(L["osum"], k * (2 * NG) + (2 * n + 2))
                else:
                    dve.reciprocal(o_sum[:, :], view[:, :, HD]).then_inc(L["osum"], 1)
                    dve.wait_ge(L["osum"], k * NG + (n + 1))
                dve.tensor_tensor(
                    o_nat[:, :, n * GH * HD:(n + 1) * GH * HD].rearrange("p t (h d) -> p t h d", h=GH),
                    view[:, :, 0:HD].rearrange("p (t h) d -> p t h d", t=TB),
                    spread(o_sum[:, :], HD).rearrange("p (t h) d -> p t h d", t=TB),
                    ALU.mult).then_inc(free, 1)
            elif step == "y":
                bank, free = banks.filled(dve, turn, ("y", n))
                wait(dve, L["x_out"], k * TB)
                dve.wait_ge(L["xp"], k + 1)
                dve.tensor_tensor(y_b[:, 2 * n:2 * n + 2, :], bank[:, :].rearrange("p (t d) -> p t d", t=2),
                                  x_res[:, 2 * n:2 * n + 2, :], ALU.add).then_inc(free, 1)
            elif step == "ln":
                for i in range(2):
                    banks.read(dve, turn, ("y", i))
                chain = Chain(dve, L["lnc"], k * LN_CHAIN)
                norm_dve(dve, L, k, y_b, None, chain)
                assert chain.n == LN_CHAIN
                wait(dve, L["x_saved"][par], half * 16)
                wait(dve, L["scattered"][par], half * (16 * 2 * TB))
                for t in range(TB):
                    dve.tensor_scalar(x_out[par][:, t, :], y_b[:, t, :], mv[:, t, 0:1], small[:, 1, t:t + 1],
                                      ALU.subtract, ALU.mult).then_inc(L["x_out"], 1)

        def first_choice(dve, chain, w, ne, best, rank, oh):
            chain(dve.tensor_reduce(best, w, AX_X, ALU.max))
            chain(dve.tensor_tensor(r_c[:, :, 0:ne], w, spread(best, ne), ALU.is_ge))
            chain(dve.tensor_tensor(r_c[:, :, 0:ne], r_c[:, :, 0:ne],
                                    rank.unsqueeze(1).broadcast_to([P, TB, ne]), ALU.mult))
            chain(dve.tensor_reduce(r_s[:, 0, :], r_c[:, :, 0:ne], AX_X, ALU.max))
            chain(dve.tensor_tensor(oh, r_c[:, :, 0:ne], spread(r_s[:, 0, :], ne), ALU.is_equal))

        def count_before(dve, chain, ne):
            chain(dve.tensor_copy(r_before[:, 0, 0:ne], r_before[:, TB, 0:ne]))
            for t in range(TB):
                chain(dve.tensor_tensor(r_before[:, t + 1, 0:ne], r_before[:, t, 0:ne], r_mask[:, t, 0:ne],
                                        ALU.add))

        def lanes(at, n):
            return lane[:, at:at + n].unsqueeze(1).broadcast_to([P, TB, n])

        def a_route_dve(dve, banks, turn, step):
            L, ne = LA, NE0
            k, par, half = turn.batch(2)
            w = r_w[:, :, 0:ne]
            oh = [r_oh[:, i, :, 0:ne] for i in range(2)]
            if step == "lg":
                chain = Chain(dve, L["rc"], k * ROUTE0)
                bank, free = banks.filled(dve, turn, ("lg", 0))
                dve.tensor_tensor(r_lg[:, :, 0:ne], bank[:, 0:TB * ne].rearrange("p (t e) -> p t e", t=TB),
                                  lanes(LANE_RB0, ne), ALU.add).then_inc(free, 1)
                banks.read(dve, turn, ("lg", 0))
                chain(dve.tensor_reduce(r_s[:, 1, :], r_lg[:, :, 0:ne], AX_X, ALU.max))
                chain(dve.tensor_tensor(w, r_lg[:, :, 0:ne], spread(r_s[:, 1, :], ne), ALU.subtract))
                chain.unwaited(dve.memset(r_s[:, 2, :], 0.0))
                assert chain.n == 3
            elif step == "rt":
                chain = Chain(dve, L["rc"], k * ROUTE0)
                chain.n = 3
                dve.wait_ge(L["ex"], k + 1)
                chain(dve.tensor_reduce(r_s[:, 2, :], w, AX_X, ALU.add))
                chain(dve.reciprocal(r_s[:, 3, :], r_s[:, 2, :]))
                chain(dve.tensor_tensor(w, w, spread(r_s[:, 3, :], ne), ALU.mult))
                first_choice(dve, chain, w, ne, r_s[:, 4, :], lane[:, LANE_RANK0:LANE_RANK0 + ne], oh[0])
                chain(dve.scalar_tensor_tensor(out=r_lg[:, :, 0:ne].rearrange("p t e -> p t e"), in0=oh[0],
                                               scalar=-2.0, in1=w, op0=ALU.mult, op1=ALU.add))
                first_choice(dve, chain, r_lg[:, :, 0:ne], ne, r_s[:, 5, :],
                             lane[:, LANE_RANK0:LANE_RANK0 + ne], oh[1])
                chain(dve.tensor_scalar(r_s[:, 6, :], r_s[:, 5, :], 0.0, None, ALU.is_gt))
                chain(dve.tensor_tensor(oh[1], oh[1], spread(r_s[:, 6, :], ne), ALU.mult))
                chain(dve.tensor_tensor(r_mask[:, :, 0:ne], oh[0], oh[1], ALU.add))
                count_before(dve, chain, ne)
                assert chain.n == MASK0, chain.n
            elif step == "ps":
                chain = Chain(dve, L["rc"], k * ROUTE0)
                chain.n = MASK0
                bank, free = banks.filled(dve, turn, ("ps", 0))
                pos = bank[:, 0:TB * ne].rearrange("p (t e) -> p t e", t=TB)
                chain(dve.tensor_tensor(r_c[:, :, 0:ne], pos, lanes(LANE_CAP, ne), ALU.is_lt))
                dve.tensor_tensor(r_pos[:, :, 0:ne], pos, lanes(LANE_SEG0, ne), ALU.add).then_inc(free, 1)
                banks.read(dve, turn, ("ps", 0))
                chain(dve.tensor_tensor(r_s[:, 7, :], oh[0][:, :, E0], r_s[:, 4, :], ALU.mult))
                chain(dve.tensor_tensor(r_s[:, 8, :], oh[1][:, :, E0], r_s[:, 5, :], ALU.mult))
                chain(dve.tensor_tensor(r_s[:, 7, :], r_s[:, 7, :], r_s[:, 8, :], ALU.add))
                g = gate0[:, bass.ds(k, 1), :].rearrange("p b (t c) -> p (b t) c", c=3)
                rows = row_from0[:, bass.ds(k, 1), :].rearrange("p b (t c) -> p (b t) c", c=2)
                chain(dve.tensor_scalar(g[:, :, 2], r_s[:, 7, :], 1.0, None, ALU.add))
                wait(dve, L["scattered"][par], half * (16 * 2 * TB))
                for i in range(2):
                    chain(dve.tensor_tensor(oh[i], oh[i], r_c[:, :, 0:ne], ALU.mult))
                    chain(dve.tensor_reduce(r_s[:, 9, :], oh[i], AX_X, ALU.add))
                    chain(dve.tensor_tensor(oh[i], oh[i], r_pos[:, :, 0:ne], ALU.mult))
                    chain(dve.tensor_reduce(r_s[:, 10, :], oh[i], AX_X, ALU.add))
                    chain(dve.tensor_tensor(g[:, :, i], r_s[:, 4 + i, :], r_s[:, 9, :], ALU.mult))
                    chain(dve.tensor_copy(rows[:, :, i], r_s[:, 10, :]))
                    chain(dve.tensor_scalar(r_s[:, 11, :], r_s[:, 9, :], -FAR, FAR, ALU.mult, ALU.add))
                    chain(dve.tensor_tensor(row_to[par][:, :, i], r_s[:, 10, :], r_s[:, 11, :], ALU.add))
                assert chain.n == ROUTE0, chain.n

        def a_dve(dve):
            L, banks = LA, banks_a
            dve.wait_ge(s_const, CONST_DMAS * 16)
            dve.memset(zero[:, :], 0.0).then_inc(s_zero, 1)
            dve.tensor_copy(ident_b[:, :], ident[:, :]).then_inc(s_fill, 1)
            dve.tensor_copy(before[:, :], scratch[:, 0:P]).then_inc(s_fill, 1)
            dve.memset(ones_b[:, :], 1.0).then_inc(s_fill, 1)
            for i in range(2):
                dve.memset(v_aug[i][:, :, :, :], 0.0).then_inc(s_fill, 1)
            dve.memset(r_before[:, :, :], 0.0).then_inc(s_fill, 1)
            dve.wait_ge(s_fill, 6)
            for i in range(2):
                dve.memset(v_aug[i][:, :, :, HD], 1.0).then_inc(s_fill, 1)
                dve.memset(K[i][SK:SK + 3, :, :], 1.0).then_inc(s_fill, 1)
            dve.wait_ge(s_fill, 10)
            dve.memset(junk[0][:, 0:2], 0.0).then_inc(s_fill2, 1)
            dve.wait_ge(s_fill2, 1)

            def emit(turn):
                for step, n in schedule(True, turn.kind):
                    k, par, half = turn.batch(0)
                    if step == "qk":
                        order = CHUNKS.index(n)
                        bank, free = banks.filled(dve, turn, ("qk", n))
                        dve.wait_ge(L["q1"], k * 4 + (order + 1))
                        wait(dve, L["q3"], k * 4 + (order - 1))
                        dve.scalar_tensor_tensor(out=qk_rest[order % 2][:, :], in0=bank[:, :],
                                                 scalar=b_qk[:, n:n + 1], in1=qk_src[n][:, 0, :],
                                                 op0=ALU.add, op1=ALU.subtract).then_inc(free, 1)
                        banks.read(dve, turn, ("qk", n))
                        dve.tensor_copy(qk_src[n][:, 1, :], qk_rest[order % 2][:, :]).then_inc(L["q2"], 1)
                    elif step == "v":
                        bank, free = banks.filled(dve, turn, ("v", n))
                        wait(dve, L["av"], (k - 1) * U0)
                        dve.tensor_tensor(
                            v_aug[par][:, 2 * n:2 * n + 2, :, 0:HD],
                            bank[:, :].rearrange("p (t h d) -> p t h d", t=2, h=NH),
                            b_v[:, :].rearrange("p (h d) -> p h d", h=NH).unsqueeze(1).broadcast_to([P, 2, NH, HD]),
                            ALU.add).then_inc(free, 1)
                    elif step == "mx":
                        for qb in range(TB):
                            i = n * TB + qb
                            bank, free = banks.filled(dve, turn, ("mx", (n, qb)))
                            if i >= 2:
                                self_bank_wait(dve, banks, turn, i - 2)
                            elif turn.kind != "first":
                                banks.all_before_read(dve, turn)
                            m = S - qb * P
                            settle(dve)
                            dve.tensor_tensor_reduce(out=junk[i % 2][:, 0:m], in0=bank[:, 0:m], in1=mask[:, 0:m],
                                                     scale=1.0, scalar=LOW, op0=ALU.add, op1=ALU.max,
                                                     accum_out=mx[:, i:i + 1]).then_inc(free, 1)
                    elif step == "mr":
                        for i in (62, 63):
                            self_bank_wait(dve, banks, turn, i)
                        chain = Chain(dve, L["mchain"], k * 5)
                        chain(dve.tensor_scalar(mx_parts[:, 0, :], mx[:, :], -1.0, None, ALU.mult))
                        chain(dve.scalar_tensor_tensor(out=mx_rest[:, :], in0=mx[:, :], scalar=-1.0,
                                                       in1=mx_parts[:, 0, :], op0=ALU.mult, op1=ALU.subtract))
                        chain(dve.tensor_copy(mx_parts[:, 1, :], mx_rest[:, :]))
                        chain(dve.tensor_tensor(mx_parts[:, 2, :], mx_rest[:, :], mx_parts[:, 1, :], ALU.subtract))
                        chain.unwaited(dve.memset(r_s[:, 23, :], 0.0))
                        bank, free = banks.filled(dve, turn, ("mr", 0))
                        wait(dve, L["mrow"], k * 48)
                        dve.tensor_copy(mx_rows[:, :, :],
                                        bank[0:NH * TB, 0:192].bitcast(BF16).rearrange("p (j n) -> p j n", j=3)
                                        ).then_inc(free, 1)
                    elif step in ("on", "y", "ln"):
                        attention_dve(dve, L, banks, turn, step, n, 0)
                    elif step in ("lg", "rt", "ps"):
                        a_route_dve(dve, banks, turn, step)
            slots(dve, emit)

        def self_bank_wait(dve, banks, turn, i):
            banks.read(dve, turn, ("mx", (i // TB, i % TB)))

        def a_pool(pool):
            L = LA
            pool.wait_ge(s_const, CONST_DMAS * 16)

            def emit(turn):
                for step, n in schedule(True, turn.kind):
                    k, par, half = turn.batch(0)
                    if step == "xp":
                        k, par, half = turn.batch(1)
                        pool.wait_ge(L["x_load"][par], half * 16 + 16)
                        wait(pool, L["x_out"], k * TB)
                        pool.tensor_tensor(out=x_res[:, :, :], in0=x_in[par][:, :, :],
                                           in1=b_o[:, :].unsqueeze(1).broadcast_to([P, TB, D]),
                                           op=ALU.add).then_inc(L["xp"], 1)
                    elif step == "qk":
                        order = CHUNKS.index(n)
                        pool.wait_ge(L["q2"], k * 4 + (order + 1))
                        pool.tensor_tensor(out=qk_src[n][:, 2, :], in0=qk_rest[order % 2][:, :],
                                           in1=qk_src[n][:, 1, :], op=ALU.subtract).then_inc(L["q3"], 1)
                    elif step == "st":
                        k, par, half = turn.batch(1)
                        u = n % len(UNITS_CAUSAL)
                        if u not in DIAGONAL:
                            continue
                        at, blocks = DIAGONAL[u]
                        pool.wait_ge(L["exp"], k * U0 + (n + 1))
                        settle(pool)
                        v = PT[n % RING][:, :, at:at + blocks * P].rearrange("p h (b q) -> p h b q", q=P)
                        pool.affine_select(out=v, in_=v, compare_op=ALU.is_ge, fill=0.0, base=0,
                                           pattern=[[0, GH], [0, blocks], [-1, P]],
                                           channel_multiplier=1).then_inc(L["sel"], 1)
                    elif step == "sc":
                        k, par, half = turn.batch(2)
                        if n == 0:
                            pool.wait_ge(L["rc"], k * ROUTE0 + ROUTE0)
                            pool.wait_ge(s_filled_rows, 16)
                            settle(pool)
                        t, i = n // 2, n % 2
                        pool.indirect_dma_start(
                            out=slot_x0, out_offset=bass.IndirectOffsetOnAxis(ap=row_to[par][:, t, i:i + 1], axis=0),
                            in_=x_out[par][:, t, :], in_offset=None, bounds_check=E0 * CAP - 1,
                            oob_is_err=False).then_inc(L["scattered"][par], 16)
            slots(pool, emit)

        MASK0 = 3 + 3 + 5 + 1 + 5 + 3 + 5
        LANE_RANK0, LANE_CAP, LANE_SEG0, LANE_RB0 = 0, 16, 32, 48
        LANE_RANK1, LANE_FFN, LANE_SEG1, LANE_RB1 = 64, 80, 96, 112
        LANE_STEP, LANE_TRI, LANE_BLK, LANE_IOTA = 128, 160, 224, 296
        CONST_DMAS = 16
        s_filled_rows = sem("s_filled_rows")

        wi = [arena[:, i * 2048:(i + 1) * 2048].rearrange("p (c n) -> p c n", c=CD) for i in (0, 1)]
        wo = [arena[:, 4096 + i * 2048:4096 + (i + 1) * 2048].rearrange("p (c n) -> p c n", c=I0 // P)
              for i in (0, 1)]
        xg = [arena[:, 8192 + i * 1024:8192 + (i + 1) * 1024].rearrange("p (t d) -> p t d", t=TB) for i in (0, 1)]
        xgT = arena[:, 10240:11264].rearrange("p (c n) -> p c n", c=CD)
        hT = arena[:, 11264:15360].rearrange("p (c n) -> p c n", c=I0 // P)
        yo = [arena[:, 15360 + i * 1024:15360 + (i + 1) * 1024].rearrange("p (t d) -> p t d", t=TB) for i in (0, 1)]
        b_load = [sem(f"b_load{i}") for i in range(2)]
        b_turned, b_turned_out = sem("b_turned"), sem("b_turned_out")
        b_up = sem("b_up")
        b_relu = [sem("b_relu_act"), sem("b_relu_dve")]
        b_down, b_down_out = sem("b_down"), sem("b_down_out")
        b_saved = [sem(f"b_saved{i}") for i in range(2)]
        MI = I0 // P
        up_banks = [ST[m // 2][:, (m % 2) * 512:(m % 2 + 1) * 512] for m in range(4)]
        down_banks = [shared[2], OT]

        def experts(eng, emit, pairs):
            def two(it):
                emit(it * 2, 0, it)
                emit(it * 2 + 1, 1, it)
            passes(eng, pairs, two)
            for e in range(2 * pairs, E0):
                emit(e, e % 2, e // 2)

        def b_sp(sp):
            def load(e, par):
                settle(sp)
                sp.dma_start(wi[par], a["experts_inter"][bass.ds(e * D, D), :].rearrange("(c p) n -> p c n", p=P)
                             ).then_inc(b_load[par], 16)
                sp.dma_start(wo[par], a["experts_out"][bass.ds(e * I0, I0), :].rearrange("(c p) n -> p c n", p=P)
                             ).then_inc(b_load[par], 16)
                sp.dma_start(xg[par], slot_x0[bass.ds(e * CAP, CAP), :].rearrange("(t p) d -> p t d", p=P)
                             ).then_inc(b_load[par], 16)

            sp.wait_ge(LA["oe"], NB * NG)
            for i in range(2):
                sp.wait_ge(LA["scattered"][i], NB // 2 * 16 * 2 * TB)
            load(0, 0)
            load(1, 1)

            def emit(e, par, half):
                sp.wait_ge(b_down_out, e * 2 + 2)
                settle(sp)
                sp.dma_start(slot_y0[bass.ds(e * CAP, CAP), :].rearrange("(t p) d -> p t d", p=P), yo[par]
                             ).then_inc(b_saved[par], 16)
                if not isinstance(e, int) or e + 2 < E0:
                    load(e + 2, par)
            experts(sp, emit, 2)
            sp.wait_ge(b_saved[0], 4 * 16)
            sp.wait_ge(b_saved[1], 3 * 16)

        def b_pe(pe):
            for b in range(3):
                pe.wait_ge(banks_a.free[b], banks_a.total(b))
            pe.wait_ge(LA["exp"], NB * U0)
            pe.wait_ge(LA["oe"], NB * NG)

            def emit(e, par, half):
                pe.wait_ge(b_load[par], half * 48 + 48)
                wait(pe, b_turned_out, e * CD)
                for c in range(CD):
                    for t in range(TB):
                        mm = pe.transpose(shared[c][:, t * P:(t + 1) * P], xg[par][:, t, c * P:(c + 1) * P],
                                          ident[:, :])
                    mm.then_inc(b_turned, 1)
                pe.wait_ge(b_turned_out, e * CD + CD)
                for m in range(MI):
                    wait(pe, b_relu[m % 2], e * (MI // 2) + (m // 2 - 1) if m >= 4 else e * (MI // 2))
                    for c in range(CD):
                        mm = pe.matmul(up_banks[m % 4], wi[par][:, c, m * P:(m + 1) * P], xgT[:, c, :],
                                       start=(c == 0), stop=(c == CD - 1))
                    mm.then_inc(b_up, 1)
                wait(pe, b_down_out, e * 2)
                for t in range(TB):
                    for m in range(MI):
                        if t == 0:
                            pe.wait_ge(b_relu[m % 2], e * (MI // 2) + (m // 2 + 1))
                        mm = pe.matmul(down_banks[t // 2][:, (t % 2) * D:(t % 2 + 1) * D],
                                       hT[:, m, t * P:(t + 1) * P], wo[par][:, m, :],
                                       start=(m == 0), stop=(m == MI - 1))
                    if t % 2:
                        mm.then_inc(b_down, 1)
            experts(pe, emit, 3)

        def b_act(act):
            def emit(e, par, half):
                for c in range(CD):
                    act.wait_ge(b_turned, e * CD + (c + 1))
                    act.activation(xgT[:, c, :], shared[c][:, :], ACT.Identity).then_inc(b_turned_out, 1)
                for m in range(0, MI, 2):
                    act.wait_ge(b_up, e * MI + (m + 1))
                    act.activation(hT[:, m, :], up_banks[m % 4], ACT.Relu).then_inc(b_relu[0], 1)
            experts(act, emit, 3)

        def b_dve(dve):
            def emit(e, par, half):
                for m in range(1, MI, 2):
                    dve.wait_ge(b_up, e * MI + (m + 1))
                    dve.tensor_scalar(hT[:, m, :], up_banks[m % 4], 0.0, None, ALU.max).then_inc(b_relu[1], 1)
                wait(dve, b_saved[par], half * 16)
                for i in range(2):
                    dve.wait_ge(b_down, e * 2 + (i + 1))
                    dve.tensor_copy(yo[par][:, 2 * i:2 * i + 2, :],
                                    down_banks[i][:, :].rearrange("p (t d) -> p t d", t=2)).then_inc(b_down_out, 1)
            experts(dve, emit, 3)

        LC = layer_sems("c")
        banks_c = Banks(False, LC["ready"], LC["free"], shared)
        U1 = NG * len(UNITS_FULL)
        gath = sb("gath", [P, 2 * TB, D])
        xn = y_b
        gate_now = [sb(f"gate_now{i}", [P, TB * 3]) for i in range(2)]
        qk_flat = [sb(f"qk_flat{i}", [P, S]) for i in range(2)]
        qk_cos = [sb("qk_cos", [P, S]), scratch]
        qk_sin = mask
        chosen1 = sb("chosen1", [P, NB, 2, TB * E1])
        row1 = sb("row1", [P, NB, 2 * TB])
        gate1 = sb("gate1", [P, NB, TB * 3])
        row_from1 = sb("row_from1", [P, NB, TB * 2], I32)
        s_w1, s_w1s = sem("s_w1"), sem("s_w1s")
        W1_DMAS = 8
        NORM = TB + TB + 1 + RSQRT_STEPS
        COMB_E = 3 * TB + NORM
        COMB = COMB_E + TB + TB + TB + 2 + RSQRT_STEPS + 1 + TB + 1
        MASK1 = 5 + 1 + 5 + 2 + 5
        ROUTE1 = MASK1 + 2 * 9 + 2 + 2
        ROPE = 3

        def gather_index_dve(dve, L, k, par, half, row_from, gate):
            wait(dve, L["gathered"][par], half * (16 * 2 * TB))
            dve.tensor_copy(row_now[par][:, :], row_from[:, bass.ds(k, 1), :].rearrange("p b n -> p (b n)")
                            ).then_inc(L["ga_idx"], 1)
            dve.tensor_copy(gate_now[par][:, :], gate[:, bass.ds(k, 1), :].rearrange("p b n -> p (b n)")
                            ).then_inc(L["ga_idx"], 1)

        def gather_pool(pool, L, k, par, n, table, rows, to):
            settle(pool)
            pool.indirect_dma_start(out=to[:, n, :], out_offset=None, in_=table,
                                    in_offset=bass.IndirectOffsetOnAxis(ap=row_now[par][:, n:n + 1], axis=0),
                                    bounds_check=rows - 1, oob_is_err=False).then_inc(L["gathered"][par], 16)

        def combine_dve(dve, chain, x, rows, gates):
            for t in range(TB):
                chain.unwaited(dve.tensor_scalar(x[:, t, :], x[:, t, :], gates[:, 3 * t + 2:3 * t + 3], None,
                                                 ALU.mult))
            chain.join()
            for i in range(2):
                for t in range(TB):
                    chain.unwaited(dve.scalar_tensor_tensor(
                        out=x[:, t, :], in0=rows[:, 2 * t + i, :], scalar=gates[:, 3 * t + i:3 * t + i + 1],
                        in1=x[:, t, :], op0=ALU.mult, op1=ALU.add))
                chain.join()
            norm_dve(dve, None, None, x, None, chain)

        def c_combine_dve(dve, L, turn):
            k, par, half = turn.batch(0)
            dve.wait_ge(L["x_load"][par], half * 16 + 16)
            dve.wait_ge(L["gathered"][par], half * (16 * 2 * TB) + 16 * 2 * TB)
            dve.wait_ge(L["ga_idx"], k * 2 + 2)
            wait(dve, L["x_out"], (k - 1) * TB)
            chain = Chain(dve, L["comb"], k * COMB)
            x = x_in[par]
            combine_dve(dve, chain, x, gath, gate_now[par])
            for t in range(TB):
                chain.unwaited(dve.tensor_scalar(x[:, t, :], x[:, t, :], mv[:, t, 0:1], small[:, 1, t:t + 1],
                                                 ALU.subtract, ALU.mult))
            chain.join()
            for t in range(TB):
                chain.unwaited(dve.bn_stats(stats[:, t, :], x[:, t, :]))
            chain.join()
            settle(dve)
            for t in range(TB):
                chain.unwaited(dve.bn_aggr(mv[:, t, :], stats[:, t, :]))
            chain.join()
            chain(dve.tensor_tensor(small[:, 3, :], mv[:, :, 0], mv[:, :, 0], ALU.mult))
            chain(dve.scalar_tensor_tensor(out=small[:, 3, :], in0=mv[:, :, 1], scalar=RMS_EPS, in1=small[:, 3, :],
                                           op0=ALU.add, op1=ALU.add))
            rsqrt(dve, chain, small[:, 4, :], small[:, 3, :], small[:, 2, :])
            chain(dve.tensor_tensor(small[:, 5, :], small[:, 3, :], small[:, 4, :], ALU.mult))
            for t in range(TB):
                chain.unwaited(dve.tensor_scalar(xn[:, t, :], x[:, t, :], small[:, 4, t:t + 1], None, ALU.mult))
            chain.unwaited(dve.memset(small[:, 15, :], 0.0))
            chain.join()
            assert chain.n == COMB, chain.n

        def c_sp(sp):
            L = LC

            def emit(turn):
                for step, n in schedule(False, turn.kind):
                    k, par, half = turn.batch(0)
                    if step == "xl":
                        wait(sp, L["xp"], k - 1)
                        settle(sp)
                        sp.dma_start(x_in[par][:, :, :],
                                     x1_dram[bass.ds(k * S, S), :].rearrange("(t p) d -> p t d", p=P)
                                     ).then_inc(L["x_load"][par], 16)
                    elif step == "ro":
                        order = CHUNKS.index(n)
                        wait(sp, L["stacked"][par], half * 192)
                        settle(sp)
                        sp.wait_ge(L["q3"], k * 4 + (order + 1))
                        settle(sp)
                        sp.dma_start(parts[par, n // 2, :, (n % 2) * P:(n % 2 + 1) * P, :].rearrange("j p n -> p j n"),
                                     qk_src[n][:, :, :]).then_inc(L["parts_saved"], 16)
                    elif step == "st_q":
                        sp.wait_ge(L["parts_saved"], k * 64 + 64)
                        settle(sp)
                        wait(sp, L["exp"], (k - 1) * U1)
                        settle(sp)
                        for t, (i, j) in enumerate(PRODUCTS):
                            for side, part, stack in ((0, i, Q), (1, j, K)):
                                sp.dma_start(stack[par][t * HD:(t + 1) * HD, :, :],
                                             parts[par, side, part].rearrange("(h d) n -> d h n", d=HD)
                                             ).then_inc(L["stacked"][par], 16)
                    elif step == "ln":
                        k, par, half = turn.batch(1)
                        sp.wait_ge(L["x_out"], k * TB + TB)
                        settle(sp)
                        sp.dma_start(x3_dram[bass.ds(k * S, S), :].rearrange("(t p) d -> p t d", p=P),
                                     x_out[par][:, :, :]).then_inc(L["x_saved"][par], 16)
            slots(sp, emit)
            for i in range(2):
                sp.wait_ge(L["x_saved"][i], NB // 2 * 16)

        def c_pe(pe):
            L, banks = LC, banks_c
            pe.wait_ge(s_w1, W1_DMAS * 16)
            pe.wait_ge(s_w1s, 2 * CD)
            pe.wait_ge(b_down_out, E0 * 2)
            pe.wait_ge(b_turned_out, E0 * CD)
            for i in range(2):
                pe.wait_ge(b_relu[i], E0 * MI // 2)

            def emit(turn):
                for step, n in schedule(False, turn.kind):
                    k, par, half = turn.batch(0)
                    if step == "xT":
                        bank, ready = banks.acquire(pe, turn, ("xT", n))
                        if n == 0:
                            pe.wait_ge(L["comb"], k * COMB + COMB)
                        for t in range(TB):
                            mm = pe.transpose(bank[:, t * P:(t + 1) * P], xn[:, t, n * P:(n + 1) * P], ident[:, :])
                        mm.then_inc(ready, 1)
                    elif step == "qk":
                        bank, ready = banks.acquire(pe, turn, ("qk", n))
                        if n == 0:
                            banks.read(pe, turn, ("xT", 0))
                            banks.read(pe, turn, ("xT", 1))
                        for c in range(CD):
                            mm = pe.matmul(bank[:, :], w_qkv[:, c, n * P:(n + 1) * P], xT[:, c, :],
                                           start=(c == 0), stop=(c == CD - 1))
                        mm.then_inc(ready, 1)
                    elif step == "ro":
                        bank, ready = banks.acquire(pe, turn, ("ro", n))
                        banks.read(pe, turn, ("qk", n))
                        pe.matmul(bank[:, :], rot[:, :], qk_flat[CHUNKS.index(n) % 2][:, :],
                                  start=True, stop=True).then_inc(ready, 1)
                    elif step == "v":
                        bank, ready = banks.acquire(pe, turn, ("v", n))
                        for t in (2 * n, 2 * n + 1):
                            for c in range(CD):
                                mm = pe.matmul(bank[:, (t % 2) * D:(t % 2 + 1) * D], xT[:, c, t * P:(t + 1) * P],
                                               w_qkv[:, c, 2 * D:3 * D], start=(c == 0), stop=(c == CD - 1))
                        mm.then_inc(ready, 1)
                    elif step in ("st", "av", "on", "oT", "y"):
                        attention_pe(pe, L, banks, False, turn, step, n, U1)
                    elif step in ("rT", "lg", "ps"):
                        route_pe(pe, L, banks, turn, step, n, NE1, ROUTE1, MASK1)
            slots(pe, emit)

        def c_act(act):
            L, banks = LC, banks_c
            act.wait_ge(s_w1, W1_DMAS * 16)

            def emit(turn):
                for step, n in schedule(False, turn.kind):
                    k, par, half = turn.batch(0)
                    if step == "xT":
                        copy_bank(act, banks, turn, ("xT", n), xT[:, n, :])
                    elif step == "qk":
                        order = CHUNKS.index(n)
                        bank, free = banks.filled(act, turn, ("qk", n))
                        wait(act, L["rope"], k * (4 * ROPE) + (ROPE * (order - 1) - 2))
                        act.activation(qk_flat[order % 2][:, :], bank[:, :], ACT.Identity,
                                       bias=b_qk[:, n:n + 1]).then_inc(free, 1)
                    elif step in ("st", "oe"):
                        attention_act(act, L, False, turn, step, n, U1, ACT.Sigmoid)
                    elif step == "oT":
                        copy_bank(act, banks, turn, ("oT", n), oT[:, n, :])
                    elif step == "rT":
                        copy_bank(act, banks, turn, ("rT", n), rT[:, n, :])
                    elif step == "ex":
                        k, par, half = turn.batch(2)
                        act.wait_ge(L["rc"], k * ROUTE1 + MASK1 - 5)
                        act.activation(r_s[:, 12, :], r_s[:, 2, :], ACT.Sigmoid, scale=-1.0).then_inc(L["ex"], 1)
                        act.activation(r_s[:, 13, :], r_s[:, 2, :], ACT.Sigmoid).then_inc(L["ex"], 1)
            slots(act, emit)

        def c_route_dve(dve, banks, turn, step):
            L, ne = LC, NE1
            k, par, half = turn.batch(2)
            oh = [r_oh[:, i, :, 0:ne] for i in range(2)]
            lg = r_lg[:, :, 0:ne]
            rank = lane[:, LANE_RANK1:LANE_RANK1 + ne]
            if step == "lg":
                chain = Chain(dve, L["rc"], k * ROUTE1)
                bank, free = banks.filled(dve, turn, ("lg", 0))
                dve.tensor_tensor(lg, bank[:, 0:TB * ne].rearrange("p (t e) -> p t e", t=TB),
                                  lanes(LANE_RB1, ne), ALU.add).then_inc(free, 1)
                banks.read(dve, turn, ("lg", 0))
                first_choice(dve, chain, lg, ne, r_s[:, 4, :], rank, oh[0])
                chain(dve.scalar_tensor_tensor(out=r_w[:, :, 0:ne], in0=oh[0], scalar=LOW, in1=lg,
                                               op0=ALU.mult, op1=ALU.add))
                first_choice(dve, chain, r_w[:, :, 0:ne], ne, r_s[:, 5, :], rank, oh[1])
                chain(dve.tensor_tensor(r_s[:, 2, :], r_s[:, 5, :], r_s[:, 4, :], ALU.subtract))
                chain(dve.tensor_tensor(r_mask[:, :, 0:ne], oh[0], oh[1], ALU.add))
            elif step == "rt":
                chain = Chain(dve, L["rc"], k * ROUTE1)
                chain.n = MASK1 - 5
                count_before(dve, chain, ne)
                assert chain.n == MASK1, chain.n
            elif step == "ps":
                chain = Chain(dve, L["rc"], k * ROUTE1)
                chain.n = MASK1
                bank, free = banks.filled(dve, turn, ("ps", 0))
                dve.tensor_tensor(r_pos[:, :, 0:ne], bank[:, 0:TB * ne].rearrange("p (t e) -> p t e", t=TB),
                                  lanes(LANE_SEG1, ne), ALU.add).then_inc(free, 1)
                banks.read(dve, turn, ("ps", 0))
                dve.wait_ge(L["ex"], k * 2 + 2)
                g = gate1[:, bass.ds(k, 1), :].rearrange("p b (t c) -> p (b t) c", c=3)
                rows = row1[:, bass.ds(k, 1), :].rearrange("p b (t c) -> p (b t) c", c=2)
                wait(dve, L["scattered"][par], half * (16 * 2 * TB))
                for i in range(2):
                    chain(dve.tensor_tensor(oh[i], oh[i], lanes(LANE_FFN, ne), ALU.mult))
                    chain(dve.tensor_reduce(r_s[:, 9, :], oh[i], AX_X, ALU.add))
                    chain(dve.tensor_tensor(r_c[:, :, 0:ne], oh[i], r_pos[:, :, 0:ne], ALU.mult))
                    chain(dve.tensor_reduce(r_s[:, 10, :], r_c[:, :, 0:ne], AX_X, ALU.add))
                    chain(dve.tensor_tensor(g[:, :, i], r_s[:, 12 + i, :], r_s[:, 9, :], ALU.mult))
                    chain(dve.tensor_copy(rows[:, :, i], r_s[:, 10, :]))
                    chain(dve.tensor_scalar(r_s[:, 11, :], r_s[:, 9, :], -FAR, FAR, ALU.mult, ALU.add))
                    chain(dve.tensor_tensor(row_to[par][:, :, i], r_s[:, 10, :], r_s[:, 11, :], ALU.add))
                    chain(dve.tensor_copy(
                        chosen1[:, bass.ds(k, 1), i, :].rearrange("p b (t e) -> p (b t) e", e=E1),
                        oh[i][:, :, 0:E1]))
                chain(dve.tensor_tensor(r_s[:, 14, :], g[:, :, 0], g[:, :, 1], ALU.add))
                chain(dve.tensor_tensor(r_s[:, 15, :], r_s[:, 12, :], r_s[:, 13, :], ALU.add))
                chain(dve.tensor_tensor(r_s[:, 14, :], r_s[:, 15, :], r_s[:, 14, :], ALU.subtract))
                chain(dve.tensor_scalar(g[:, :, 2], r_s[:, 14, :], 1.0, None, ALU.add))
                assert chain.n == ROUTE1, chain.n

        def c_dve(dve):
            L, banks = LC, banks_c
            dve.wait_ge(s_w1, W1_DMAS * 16)
            for c in range(CD):
                for side in range(2):
                    dve.tensor_scalar(w_qkv[:, c, side * D:(side + 1) * D], w_qkv[:, c, side * D:(side + 1) * D],
                                      rn_scale[:, side, c:c + 1], None, ALU.mult).then_inc(s_w1s, 1)
            dve.memset(r_before[:, TB, :], 0.0).then_inc(s_fill2, 1)
            dve.wait_ge(s_fill2, 2)

            def emit(turn):
                for step, n in schedule(False, turn.kind):
                    k, par, half = turn.batch(0)
                    if step == "gi":
                        gather_index_dve(dve, L, k, par, half, row_from0, gate0)
                    elif step == "cb":
                        c_combine_dve(dve, L, turn)
                    elif step == "ro":
                        order = CHUNKS.index(n)
                        bank, free = banks.filled(dve, turn, ("ro", n))
                        rest = qk_rest[order % 2]
                        chain = Chain(dve, L["rope"], k * (4 * ROPE))
                        chain.n = order * ROPE
                        dve.tensor_tensor(qk_sin[:, :], bank[:, :], sin_t[:, :], ALU.mult).then_inc(free, 1)
                        banks.read(dve, turn, ("ro", n))
                        dve.wait_ge(L["qf"], k * 4 + (order + 1))
                        wait(dve, L["q3"], k * 4 + (order - 1))
                        chain(dve.tensor_tensor(rest[:, :], qk_cos[order % 2][:, :], qk_sin[:, :], ALU.add))
                        wait(dve, L["parts_saved"], k * 64)
                        chain(dve.tensor_copy(qk_src[n][:, 0, :], rest[:, :]))
                        chain(dve.tensor_tensor(rest[:, :], rest[:, :], qk_src[n][:, 0, :], ALU.subtract))
                        dve.tensor_copy(qk_src[n][:, 1, :], rest[:, :]).then_inc(L["q2"], 1)
                    elif step == "v":
                        bank, free = banks.filled(dve, turn, ("v", n))
                        wait(dve, L["av"], (k - 1) * U1)
                        dve.wait_ge(L["comb"], k * COMB + COMB)
                        for t in (2 * n, 2 * n + 1):
                            v = dve.scalar_tensor_tensor(
                                out=v_aug[par][:, t, :, 0:HD],
                                in0=bank[:, (t % 2) * D:(t % 2 + 1) * D].rearrange("p (h d) -> p h d", h=NH),
                                scalar=small[:, 5, t:t + 1], in1=b_v[:, :].rearrange("p (h d) -> p h d", h=NH),
                                op0=ALU.mult, op1=ALU.add)
                        v.then_inc(free, 1)
                    elif step in ("on", "y", "ln"):
                        attention_dve(dve, L, banks, turn, step, n, SUM_EPS)
                    elif step in ("lg", "rt", "ps"):
                        c_route_dve(dve, banks, turn, step)
            slots(dve, emit)

        def c_pool(pool):
            L = LC
            pool.wait_ge(s_w1, W1_DMAS * 16)

            def emit(turn):
                for step, n in schedule(False, turn.kind):
                    k, par, half = turn.batch(0)
                    if step == "ga":
                        if n == 0:
                            pool.wait_ge(L["ga_idx"], k * 2 + 2)
                            wait(pool, L["comb"], k * COMB)
                            pool.wait_ge(b_saved[0], 4 * 16)
                            pool.wait_ge(b_saved[1], 3 * 16)
                        gather_pool(pool, L, k, par, n, slot_y0, E0 * CAP, gath)
                    elif step == "ro":
                        order = CHUNKS.index(n)
                        banks_c.read(pool, turn, ("qk", n))
                        wait(pool, L["rope"], k * (4 * ROPE) + (ROPE * (order - 1) - 2))
                        pool.tensor_tensor(out=qk_cos[order % 2][:, :], in0=qk_flat[order % 2][:, :],
                                           in1=cos_t[:, :], op=ALU.mult).then_inc(L["qf"], 1)
                        pool.wait_ge(L["q2"], k * 4 + (order + 1))
                        pool.tensor_tensor(out=qk_src[n][:, 2, :], in0=qk_rest[order % 2][:, :],
                                           in1=qk_src[n][:, 1, :], op=ALU.subtract).then_inc(L["q3"], 1)
                    elif step == "xp":
                        k, par, half = turn.batch(1)
                        pool.wait_ge(L["comb"], k * COMB + COMB)
                        wait(pool, L["x_out"], k * TB)
                        pool.tensor_tensor(out=x_res[:, :, :], in0=x_in[par][:, :, :],
                                           in1=b_o[:, :].unsqueeze(1).broadcast_to([P, TB, D]),
                                           op=ALU.add).then_inc(L["xp"], 1)
                    elif step == "sc":
                        k, par, half = turn.batch(2)
                        if n == 0:
                            pool.wait_ge(L["rc"], k * ROUTE1 + ROUTE1)
                            settle(pool)
                        t, i = n // 2, n % 2
                        pool.indirect_dma_start(
                            out=slot_x1, out_offset=bass.IndirectOffsetOnAxis(ap=row_to[par][:, t, i:i + 1], axis=0),
                            in_=x_out[par][:, t, :], in_offset=None, bounds_check=ZROW - 1,
                            oob_is_err=False).then_inc(L["scattered"][par], 16)
            slots(pool, emit)

        w1t = arena[:, 0:8192]
        w2t = arena[:, 8192:16384]
        free_at = [16384]

        def carve(n):
            free_at[0] += n
            return arena[:, free_at[0] - n:free_at[0]]

        RX = 4
        bx = [gath[:, i, :] for i in range(RX)]
        bxT = [carve(D) for _ in range(2)]
        bh = [carve(F1) for _ in range(2)]
        bhT = [carve(F1) for _ in range(2)]
        by = [carve(D) for _ in range(2)]
        KF = F1 // P
        t_tab = sb("t_tab", [1, 2, NBLK], I32)
        t_cnt = sb("t_cnt", [P, E1])
        t_a = carve(E1 * 32).rearrange("p (e n) -> p e n", e=E1)
        t_nb = sb("t_nb", [P, E1])
        t_tri = carve(E1 * E1).rearrange("p (a b) -> p a b", a=E1)
        t_start = sb("t_start", [P, E1])
        t_end = sb("t_end", [P, E1])
        t_delta = sb("t_delta", [P, E1])
        t_rowf = carve(2 * TB * NB)
        t_pad = sb("t_pad", [P, E1], I32)
        t_b8 = carve(NBLK * E1)[0:1, :].rearrange("p (b e) -> p b e", e=E1)
        t_b8b = carve(NBLK * E1)[0:1, :].rearrange("p (b e) -> p b e", e=E1)
        t_bf = sb("t_bf", [1, 6, NBLK])
        d_cnt, d_chain, d_tab = sem("d_counts"), sem("d_chain"), sem("d_tables")
        d_w = sem("d_weights")
        d_pad = sem("d_padded")
        d_zero = sem("d_zero_rows")
        d_load = [sem(f"d_load{i}") for i in range(RX)]
        d_saved = [sem(f"d_saved{i}") for i in range(2)]
        d_t, d_tout, d_up, d_h, d_ht, d_htout, d_y, d_yout = (
            sem(x) for x in ("d_turned", "d_turned_out", "d_up", "d_hidden", "d_hidden_turned", "d_hidden_out",
                             "d_down", "d_down_out"))
        D_CHAIN = 25

        def tables_dve(dve):
            chain = Chain(dve, d_chain, 0)
            dve.wait_ge(d_cnt, 1)
            chain(dve.tensor_copy(t_cnt[:, :], shared[0][:, 0:E1]))
            chain(dve.tensor_tensor(t_a[:, :, :], spread(t_cnt[:, :], 32),
                                    lane[:, LANE_STEP:LANE_STEP + 32].unsqueeze(1).broadcast_to([P, E1, 32]),
                                    ALU.is_gt))
            chain(dve.tensor_reduce(t_nb[:, :], t_a[:, :, :], AX_X, ALU.add))
            chain(dve.tensor_tensor(t_tri[:, :, :], t_nb[:, :].unsqueeze(1).broadcast_to([P, E1, E1]),
                                    lane[:, LANE_TRI:LANE_TRI + 64].rearrange("p (a b) -> p a b", a=E1), ALU.mult))
            chain(dve.tensor_reduce(t_start[:, :], t_tri[:, :, :], AX_X, ALU.add))
            chain(dve.tensor_tensor(t_end[:, :], t_start[:, :], t_nb[:, :], ALU.add))
            chain(dve.scalar_tensor_tensor(out=t_delta[:, :], in0=t_start[:, :], scalar=float(P),
                                           in1=lane[:, LANE_SEG1:LANE_SEG1 + E1], op0=ALU.mult, op1=ALU.subtract))
            seg = lane[:, LANE_SEG1:LANE_SEG1 + E1]
            chain(dve.tensor_tensor(t_start[:, :], t_cnt[:, :], seg, ALU.add))
            chain(dve.tensor_scalar(t_pad[:, :], t_start[:, :], lane[:, LANE_IOTA:LANE_IOTA + 1], None, ALU.add))
            blk = lane[0:1, LANE_BLK:LANE_BLK + NBLK]
            chain(dve.tensor_tensor(t_b8[:, :, :], spread(blk, E1),
                                    t_end[0:1, :].unsqueeze(1).broadcast_to([1, NBLK, E1]), ALU.is_ge))
            chain(dve.tensor_reduce(t_bf[:, 0, :], t_b8[:, :, :], AX_X, ALU.add))
            chain(dve.tensor_tensor(t_b8[:, :, :], spread(t_bf[:, 0, :], E1),
                                    lane[0:1, LANE_BLK:LANE_BLK + E1].unsqueeze(1).broadcast_to([1, NBLK, E1]),
                                    ALU.is_equal))
            chain(dve.tensor_tensor(t_b8b[:, :, :], t_b8[:, :, :],
                                    t_delta[0:1, :].unsqueeze(1).broadcast_to([1, NBLK, E1]), ALU.mult))
            chain(dve.tensor_reduce(t_bf[:, 1, :], t_b8b[:, :, :], AX_X, ALU.add))
            chain(dve.tensor_reduce(t_bf[:, 2, :], t_b8[:, :, :], AX_X, ALU.add))
            chain(dve.scalar_tensor_tensor(out=t_bf[:, 3, :], in0=blk, scalar=float(P), in1=t_bf[:, 1, :],
                                           op0=ALU.mult, op1=ALU.subtract))
            chain(dve.tensor_tensor(t_bf[:, 3, :], t_bf[:, 3, :], t_bf[:, 2, :], ALU.mult))
            chain(dve.tensor_scalar(t_bf[:, 4, :], t_bf[:, 2, :], -float(ZROW), float(ZROW), ALU.mult, ALU.add))
            chain(dve.tensor_tensor(t_tab[:, 0, :], t_bf[:, 3, :], t_bf[:, 4, :], ALU.add))
            chain(dve.tensor_scalar(t_bf[:, 5, :], t_bf[:, 0, :], float(E1 - 1), None, ALU.min))
            chain(dve.tensor_copy(t_tab[:, 1, :], t_bf[:, 5, :]))
            c2 = chosen1[:, :, :, :].rearrange("p b i (t e) -> p (b i t) e", e=E1)
            chain(dve.tensor_tensor(c2, c2, t_delta[:, :].unsqueeze(1).broadcast_to([P, 2 * TB * NB, E1]), ALU.mult))
            chain(dve.tensor_reduce(t_rowf[:, :], c2, AX_X, ALU.add))
            for i in range(2):
                chain(dve.tensor_tensor(
                    row_from1[:, :, :].rearrange("p b (t c) -> p b t c", c=2)[:, :, :, i],
                    row1[:, :, :].rearrange("p b (t c) -> p b t c", c=2)[:, :, :, i],
                    t_rowf[:, :].rearrange("p (b i t) -> p b i t", i=2, t=TB)[:, :, i, :], ALU.add))
            assert chain.n == D_CHAIN, chain.n

        def d_sp(sp):
            sp.wait_ge(LC["oe"], NB * NG)
            for e in range(E1):
                sp.dma_start(w1t[:, e * 1024:(e + 1) * 1024].rearrange("p (c n) -> p c n", c=CD),
                             a["w1T"][e * D:(e + 1) * D, :].rearrange("(c p) n -> p c n", p=P)).then_inc(d_w, 16)
                sp.dma_start(w2t[:, e * 1024:(e + 1) * 1024].rearrange("p (c n) -> p c n", c=KF),
                             a["w2T"][e * F1:(e + 1) * F1, :].rearrange("(c p) n -> p c n", p=P)).then_inc(d_w, 16)
            sp.wait_ge(d_chain, 21)
            for i in range(2):
                sp.wait_ge(LC["scattered"][i], NB // 2 * 16 * 2 * TB)
            sp.wait_ge(d_pad, 16 * E1)
            sp.wait_ge(d_zero, 16)

            def load(j, buffer):
                row = sp.value_load(t_tab[0:1, 0, bass.ds(j, 1)], min_val=0, max_val=ZROW)
                sp.dma_start(bx[buffer], slot_x1[bass.ds(row, P), :]).then_inc(d_load[buffer], 16)

            for j in range(RX):
                load(j, j)

            def step(j, buffer, more):
                if more:
                    sp.wait_ge(d_t, j + 1)
                    settle(sp)
                    load(j + RX, buffer)
                sp.wait_ge(d_yout, j + 1)
                settle(sp)
                sp.dma_start(slot_y1[bass.ds(j * P, P), :], by[buffer % 2]).then_inc(d_saved[buffer % 2], 16)

            with sp.Fori(0, NBLK // RX - 1) as it:
                for i in range(RX):
                    step(it * RX + i, i, True)
            for i in range(RX):
                step(NBLK - RX + i, i, False)
            for i in range(2):
                sp.wait_ge(d_saved[i], NBLK // 2 * 16)

        T_BANK = shared[0]
        UP = [ST[0][:, 0:512], ST[0][:, 512:1024]]
        HT_BANK = [ST[1][:, 0:512], ST[1][:, 512:1024]]
        Y_BANK = [shared[1], shared[2]]

        def d_pe(pe):
            for b in range(3):
                pe.wait_ge(banks_c.free[b], banks_c.total(b))
            pe.wait_ge(LC["rc"], NB * ROUTE1)
            pe.wait_ge(LC["exp"], NB * U1)
            pe.wait_ge(LC["oe"], NB * NG)
            pe.matmul(shared[0][:, 0:E1], ones_b[:, :], r_before[:, TB, 0:E1], start=True, stop=True
                      ).then_inc(d_cnt, 1)
            pe.wait_ge(d_chain, 21)
            pe.wait_ge(d_w, 2 * E1 * 16)

            def turn_rows(j, buffer, turns):
                wait(pe, d_tout, j)
                pe.wait_ge(d_load[buffer], turns * 16 + 16)
                for c in range(CD):
                    mm = pe.transpose(T_BANK[:, c * P:(c + 1) * P], bx[buffer][:, c * P:(c + 1) * P], ident[:, :])
                mm.then_inc(d_t, 1)

            def up(j, par):
                e = pe.value_load(t_tab[0:1, 1, bass.ds(j, 1)], min_val=0, max_val=E1 - 1)
                pe.wait_ge(d_tout, j + 1)
                for c in range(CD):
                    mm = pe.matmul(UP[par], bxT[par][:, c * P:(c + 1) * P],
                                   w1t[:, bass.ds(e * 1024 + c * F1, F1)], start=(c == 0), stop=(c == CD - 1))
                mm.then_inc(d_up, 1)

            def turn_hidden(j, par):
                pe.wait_ge(d_h, j + 1)
                for c in range(KF):
                    mm = pe.transpose(HT_BANK[par][:, c * P:(c + 1) * P], bh[par][:, c * P:(c + 1) * P],
                                      ident[:, :])
                mm.then_inc(d_ht, 1)

            def down(j, par, clear):
                e = pe.value_load(t_tab[0:1, 1, bass.ds(j, 1)], min_val=0, max_val=E1 - 1)
                pe.wait_ge(d_htout, j + 1)
                if clear is not None:
                    pe.wait_ge(d_yout, clear)
                for c in range(KF):
                    mm = pe.matmul(Y_BANK[par][:, 0:D], bhT[par][:, c * P:(c + 1) * P],
                                   w2t[:, bass.ds(e * 1024 + c * D, D)], start=(c == 0), stop=(c == KF - 1))
                mm.then_inc(d_y, 1)

            turn_rows(0, 0, 0)
            up(0, 0)
            turn_rows(1, 1, 0)
            turn_hidden(0, 0)
            up(1, 1)
            turn_rows(2, 2, 0)
            down(0, 0, None)
            with pe.Fori(0, NBLK // RX - 1) as it:
                for j0 in range(1, RX + 1):
                    par = j0 % 2
                    j = it * RX + j0
                    turn_hidden(j, par)
                    up(j + 1, 1 - par)
                    turn_rows(j + 2, (j0 + 2) % RX, it + (j0 + 2) // RX)
                    down(j, par, j - 1)
            for j in range(NBLK - 3, NBLK):
                turn_hidden(j, j % 2)
                if j + 1 < NBLK:
                    up(j + 1, (j + 1) % 2)
                if j + 2 < NBLK:
                    turn_rows(j + 2, (j + 2) % RX, (j + 2) // RX)
                down(j, j % 2, j - 1)

        def d_act(act):
            act.wait_ge(d_up, 1)
            act.activation(bh[0], UP[0], ACT.Silu).then_inc(d_h, 1)

            def emit_lag(j, par, half, last=False):
                if not last:
                    act.wait_ge(d_up, j + 2)
                    act.activation(bh[1 - par], UP[1 - par], ACT.Silu).then_inc(d_h, 1)
                act.wait_ge(d_y, j + 1)
                wait(act, d_saved[par], half * 16)
                act.activation(by[par], Y_BANK[par][:, 0:D], ACT.Identity).then_inc(d_yout, 1)
            def two(it):
                emit_lag(it * 2, 0, it)
                emit_lag(it * 2 + 1, 1, it)
            passes(act, NBLK // 2 - 1, two)
            emit_lag(NBLK - 2, 0, NBLK // 2 - 1)
            emit_lag(NBLK - 1, 1, NBLK // 2 - 1, True)

        def d_dve(dve):
            tables_dve(dve)

            def rows_out(j, par):
                dve.wait_ge(d_t, j + 1)
                dve.tensor_copy(bxT[par], T_BANK[:, 0:D]).then_inc(d_tout, 1)

            def hidden_out(j, par):
                dve.wait_ge(d_ht, j + 1)
                dve.tensor_copy(bhT[par], HT_BANK[par]).then_inc(d_htout, 1)

            rows_out(0, 0)
            rows_out(1, 1)
            with dve.Fori(0, NBLK // 2 - 1) as it:
                for par in range(2):
                    hidden_out(it * 2 + par, par)
                    rows_out(it * 2 + par + 2, par)
            hidden_out(NBLK - 2, 0)
            hidden_out(NBLK - 1, 1)

        def d_pool(pool):
            pool.wait_ge(d_chain, 9)
            pool.wait_ge(s_zero, 1)
            for e in range(E1):
                pool.indirect_dma_start(out=slot_x1,
                                        out_offset=bass.IndirectOffsetOnAxis(ap=t_pad[:, e:e + 1], axis=0),
                                        in_=zero[:, :], in_offset=None, bounds_check=ZROW + P - 1,
                                        oob_is_err=False).then_inc(d_pad, 16)

        LE = dict(gathered=[sem(f"e_gathered{i}") for i in range(2)], ga_idx=sem("e_rows_known"),
                  comb=sem("e_combine_chain"), x_load=[sem(f"e_load{i}") for i in range(2)],
                  out=[sem(f"e_out{i}") for i in range(2)], done=sem("e_rows_done"))
        egath = [arena[:, i * 2048:(i + 1) * 2048].rearrange("p (n d) -> p n d", n=2 * TB) for i in (0, 1)]

        def pairs(eng, emit):
            def two(it):
                emit(it * 2, 0, it)
                emit(it * 2 + 1, 1, it)
            passes(eng, NB // 2, two)

        def e_sp(sp):
            def load(k, par):
                settle(sp)
                sp.dma_start(x_in[par][:, :, :], x3_dram[bass.ds(k * S, S), :].rearrange("(t p) d -> p t d", p=P)
                             ).then_inc(LE["x_load"][par], 16)
            sp.wait_ge(LC["xp"], NB)
            load(0, 0)
            load(1, 1)

            def emit(k, par, half, more=True):
                sp.wait_ge(LE["done"], k * TB + TB)
                settle(sp)
                sp.dma_start(out[bass.ds(k * S, S), :].rearrange("(t p) d -> p t d", p=P), x_out[par][:, :, :]
                             ).then_inc(LE["out"][par], 16)
                if more:
                    load(k + 2, par)
            with sp.Fori(0, NB // 2 - 1) as it:
                emit(it * 2, 0, it)
                emit(it * 2 + 1, 1, it)
            emit(NB - 2, 0, NB // 2 - 1, False)
            emit(NB - 1, 1, NB // 2 - 1, False)
            for i in range(2):
                sp.wait_ge(LE["out"][i], NB // 2 * 16)

        def e_dve(dve):
            for i in range(2):
                dve.wait_ge(LC["gathered"][i], NB // 2 * 16 * 2 * TB)
                dve.wait_ge(LC["x_saved"][i], NB // 2 * 16)
                dve.wait_ge(LC["scattered"][i], NB // 2 * 16 * 2 * TB)

            def emit(k, par, half):
                gather_index_dve(dve, LE, k, par, half, row_from1, gate1)
                dve.wait_ge(LE["x_load"][par], half * 16 + 16)
                dve.wait_ge(LE["gathered"][par], half * (16 * 2 * TB) + 16 * 2 * TB)
                dve.wait_ge(LE["ga_idx"], k * 2 + 2)
                wait(dve, LE["done"], k * TB)
                chain = Chain(dve, LE["comb"], k * COMB_E)
                combine_dve(dve, chain, x_in[par], egath[par], gate_now[par])
                assert chain.n == COMB_E
                wait(dve, LE["out"][par], half * 16)
                for t in range(TB):
                    dve.tensor_scalar(x_out[par][:, t, :], x_in[par][:, t, :], mv[:, t, 0:1], small[:, 1, t:t + 1],
                                      ALU.subtract, ALU.mult).then_inc(LE["done"], 1)
            pairs(dve, emit)

        def e_pool(pool):
            for i in range(2):
                pool.wait_ge(d_saved[i], NBLK // 2 * 16)

            def emit(k, par, half):
                pool.wait_ge(LE["ga_idx"], k * 2 + 2)
                wait(pool, LE["comb"], k * COMB_E)
                for n in range(2 * TB):
                    gather_pool(pool, LE, k, par, n, slot_y1, NBLK * P, egath[par])
            pairs(pool, emit)

        @block.sync
        def _(sp):
            for dst, src in (
                (ident[:, :], a["c_ident"]), (scratch[:, 0:P], a["c_before"]), (mask[:, :], a["c_mask"]),
                (lane[:, 0:48], a["c_lane"][:, 0:48]), (lane[:, 64:112], a["c_lane"][:, 64:112]),
                (lane[:, 128:304], a["c_lane"][:, 128:304]), (rot[:, :], a["c_rot"]),
                (cos_t[:, :], a["c_cos"]), (sin_t[:, :], a["c_sin"]),
                (lane[:, LANE_RB0:LANE_RB0 + NE0], a["router_b"].partition_broadcast(P)),
                (w_qkv[:, :, :], a["w_qkv"].rearrange("(c p) n -> p c n", p=P)),
                (w_o[:, :, :], a["w_out"].rearrange("(c p) n -> p c n", p=P)),
                (w_r[:, :, 0:NE0], a["router_wT"].rearrange("(c p) n -> p c n", p=P)),
                (b_qk[:, :], a["b_qk_cols"]),
                (b_v[:, :], a["b_qkv"][2 * D:3 * D].partition_broadcast(P)),
                (b_o[:, :], a["b_out"].partition_broadcast(P)),
            ):
                sp.dma_start(dst, src).then_inc(s_const, 16)
            sp.wait_ge(s_zero, 1)
            sp.dma_start(slot_x0.rearrange("(a p) d -> p a d", p=P),
                         zero[:, :].unsqueeze(1).broadcast_to([P, E0 * CAP // P, D])).then_inc(s_filled_rows, 16)
            sp.dma_start(slot_x1[ZROW:ZROW + P, :], zero[:, :]).then_inc(d_zero, 16)
            a_sp(sp)
            for i in range(2):
                sp.wait_ge(LA["x_saved"][i], NB // 2 * 16)
            sp.wait_ge(LA["rc"], NB * ROUTE0)
            for dst, src in (
                (w_qkv[:, :, :], a["w_qkv1T"].rearrange("(c p) n -> p c n", p=P)),
                (w_o[:, :, :], a["w_o1T"].rearrange("(c p) n -> p c n", p=P)),
                (w_r[:, :, :], a["gate_wT"].rearrange("(c p) n -> p c n", p=P)),
                (b_qk[:, :], a["b_qk_cols1"]), (rn_scale[:, :, :], a["rn_cols"]),
                (b_v[:, :], a["b_v1"].partition_broadcast(P)),
                (b_o[:, :], a["b_o1"].partition_broadcast(P)),
                (lane[:, LANE_RB1:LANE_RB1 + NE1], a["expert_bias"].partition_broadcast(P)),
            ):
                sp.dma_start(dst, src).then_inc(s_w1, 16)
            b_sp(sp)
            c_sp(sp)
            d_sp(sp)
            e_sp(sp)

        @block.tensor
        def _(pe):
            a_pe(pe)
            b_pe(pe)
            c_pe(pe)
            d_pe(pe)

        @block.scalar
        def _(act):
            a_act(act)
            b_act(act)
            c_act(act)
            d_act(act)

        @block.vector
        def _(dve):
            a_dve(dve)
            b_dve(dve)
            c_dve(dve)
            d_dve(dve)
            e_dve(dve)

        @block.gpsimd
        def _(pool):
            a_pool(pool)
            c_pool(pool)
            d_pool(pool)
            e_pool(pool)


def shape_constants():
    lane = np.zeros((P, 304), np.float32)
    lane[:, 0:NE0] = NE0 - np.arange(NE0)
    lane[:, 16:16 + E0] = CAP
    lane[:, 32:32 + NE0] = CAP * np.arange(NE0)
    lane[:, 64:64 + NE1] = NE1 - np.arange(NE1)
    lane[:, 80:80 + E1] = 1.0
    lane[:, 96:96 + E1] = SEG * np.arange(E1)
    lane[:, 128:160] = P * np.arange(32)
    lane[:, 160:224] = np.tril(np.ones((E1, E1), np.float32), -1).ravel()
    lane[:, 224:224 + NBLK] = np.arange(NBLK)
    lane[:, 296] = np.arange(P)
    mask = np.zeros((P, S), np.float32)
    mask[:, 0:P] = np.where(np.arange(P)[None, :] >= np.arange(P)[:, None], 0.0, LOW)
    inv = (np.float32(1.0) / np.float32(10000.0) ** (np.arange(0, HD, 2, dtype=np.float32) / np.float32(HD)))
    freqs = np.arange(S, dtype=np.float32)[:, None] * inv.astype(np.float32)[None, :]
    emb = np.concatenate([freqs, freqs], axis=-1)
    cos = np.tile(np.cos(emb).astype(np.float32).T, (P // HD, 1))
    sin = np.tile(np.sin(emb).astype(np.float32).T, (P // HD, 1))
    rot = np.zeros((P, P), np.float32)
    for i in range(0, P, 2):
        rot[i + 1, i] = -1.0
        rot[i, i + 1] = 1.0
    return {
        "c_ident": np.eye(P, dtype=np.float32), "c_before": np.triu(np.ones((P, P), np.float32), 1),
        "c_mask": mask, "c_lane": lane, "c_rot": rot, "c_cos": cos, "c_sin": sin,
    }


def laid_out(i):
    c = np.ascontiguousarray
    i = {k: np.asarray(v) for k, v in i.items()}
    cols = lambda v, n: c(v.reshape(n, P).T)
    return {
        "x": c(i["L0_attn_x"].reshape(NTOK, D)),
        "w_qkv": c(i["L0_attn_w_qkv"]), "b_qkv": c(i["L0_attn_b_qkv"]),
        "b_qk_cols": cols(i["L0_attn_b_qkv"][0:2 * D], 4),
        "w_out": c(i["L0_attn_w_out"]), "b_out": c(i["L0_attn_b_out"]),
        "router_wT": c(i["L0_ffn_router_w"].T), "router_b": c(i["L0_ffn_router_b"]),
        "experts_inter": c(i["L0_ffn_experts_inter"].reshape(E0 * D, I0)),
        "experts_out": c(i["L0_ffn_experts_out"].reshape(E0 * I0, D)),
        "w_qkv1T": c(np.concatenate([i["L1_attn_q_w"].T, i["L1_attn_k_w"].T, i["L1_attn_v_w"].T], axis=1)),
        "w_o1T": c(i["L1_attn_o_w"].T),
        "b_qk_cols1": c(np.concatenate([cols(i["L1_attn_q_b"], 2), cols(i["L1_attn_k_b"], 2)], axis=1)),
        "b_v1": c(i["L1_attn_v_b"]), "b_o1": c(i["L1_attn_o_b"]),
        "rn_cols": c(np.stack([cols(i["L1_attn_qn_scale"], 2), cols(i["L1_attn_kn_scale"], 2)], axis=1)),
        "gate_wT": c(i["L1_ffn_gate_w"].T), "expert_bias": c(i["L1_ffn_expert_bias"]),
        "w1T": c(i["L1_ffn_w1"].transpose(0, 2, 1).reshape(E1 * D, F1)),
        "w2T": c(i["L1_ffn_w2"].transpose(0, 2, 1).reshape(E1 * F1, D)),
    }


def kernel(**inputs):
    import concourse.bacc as bacc
    from concourse.bass_utils import run_bass_kernel_spmd

    nc = bacc.Bacc("TRN2", target_bir_lowering=False, num_devices=1)
    arrays = {f"in_{k}": v for k, v in {**laid_out(inputs), **shape_constants()}.items()}
    a = {k[3:]: nc.dram_tensor(k, v.shape, mybir.dt.from_np(v.dtype), kind="ExternalInput").ap()
         for k, v in arrays.items()}
    out = nc.dram_tensor("out_rows", (NTOK, D), F32, kind="ExternalOutput").ap()
    build(nc, a, out)
    r = run_bass_kernel_spmd(nc, [arrays], core_ids=[0])
    return r.results[0]["out_rows"].reshape(NB, S, D)
```

```python
from contextlib import ExitStack

import numpy as np

import concourse.bass as bass
from concourse import mybir

F32 = mybir.dt.float32
BF16 = mybir.dt.bfloat16
I32 = mybir.dt.int32
ALU = mybir.AluOpType
ACT = mybir.ActivationFunctionType
AX_X = mybir.AxisListType.X

P = 128
NB, S, D = 8, 512, 256
NH, HD = 16, 16
TB = S // P
CD = D // P
GH = 4
NG = NH // GH
E0, I0, CAP = 7, 1024, 512
NE0 = E0 + 1
E1, F1, NE1 = 8, 512, 12
NTOK = NB * S
SEG = NTOK + P
ZROW = E1 * SEG
NBLK = 2 * NTOK // P + E1
LN_EPS, RMS_EPS, SUM_EPS = 1e-5, 1e-8, 1e-8
ATT_SCALE = 0.25
FAR = float(1 << 20)
LOW = -3.0e38
NPROD = 6
SK = NPROD * HD
STACK_DMAS = 2 * NPROD * 16
RING = 4
RSQRT_MAGIC = 1597463007.0

PRODUCTS = [(0, 0), (0, 1), (1, 0), (1, 1), (0, 2), (2, 0)]

UNITS_CAUSAL = [
    [(3, 0, 256, 0)],
    [(2, 0, 256, 0)],
    [(1, 0, 256, 0)],
    [(3, 256, 256, 0)],
    [(0, 0, 128, 0), (2, 256, 128, 128)],
]
UNITS_FULL = [[(kb, qh * 256, 256, 0)] for qh in range(2) for kb in range(TB)]
DIAGONAL = {2: (128, 1), 3: (128, 1), 4: (0, 2)}


def wait(eng, sem, value):
    if isinstance(value, int) and value <= 0:
        return
    eng.wait_ge(sem, value)


class Turn:

    def __init__(self, kind, s, it=None):
        self.kind, self.s, self.it = kind, s, it

    def batch(self, d):
        if self.it is None:
            k = self.s - d
            return k, k % 2, k // 2
        k = self.s - d
        return self.it * 2 + k, k % 2, (self.it + (k // 2) if k // 2 else self.it)


def passes(eng, n, one):
    one(0)
    with eng.Fori(1, n) as it:
        one(it)


CHUNKS = (0, 2, 1, 3)

KINDS = ("first", "second", "body", "eighth", "ninth")


def slots(eng, emit):
    emit(Turn("first", 0))
    emit(Turn("second", 1))

    def two(it):
        emit(Turn("body", 2, it))
        emit(Turn("body", 3, it))
    passes(eng, (NB - 2) // 2, two)
    emit(Turn("eighth", NB))
    emit(Turn("ninth", NB + 1))


COST = {
    True: dict(xT=0.5, qk=0.8, y=0.4, v=0.8, ln=0.1, mx=0.5, mr=1),
    False: dict(xT=0.5, qk=1.7, ro=1.5, v=1.7, y=0.4, ln=0.25, cb=0.56, l1=0.1, l2=0.1, l3=0.1),
}
N_LN = 23
N_COMBINE = 64
N_ROUTE = {True: (3, 22, 20), False: (13, 5, 22)}


def pieces(step, n, first=0):
    return [(step, i) for i in range(first, n)]


def mixed(a, b):
    out, at = [], 0
    for i, step in enumerate(a):
        out.append(step)
        upto = (i + 1) * len(b) // len(a)
        if upto > at and b[upto - 1][0] in ("lg", "ps"):
            upto += 1
        out += b[at:upto]
        at = max(at, upto)
    return out


def schedule(causal, kind):
    prep = kind in ("first", "second", "body")
    attn = kind in ("second", "body", "eighth")
    route = kind in ("body", "eighth", "ninth")
    n1, n2, n3 = N_ROUTE[causal]
    start = [("oT", 0), ("oT", 1)] if route else []
    y = [("y", 0), ("y", 1)] if route else []
    norm = pieces("ln", N_LN) if route else []
    save = ([("sv", 0)] if route else []) + ([("xp", 0)] if attn else [])
    rows = [("rT", 0), ("rT", 1)] if route else []
    route_1 = ([("lg", 0)] + pieces("l1", n1) + [("ex", 0)]) if route else []
    route_2 = pieces("l2", n2) if route else []
    route_3 = ([("ps", 0)] + pieces("l3", n3)) if route else []
    scatter = [("sc", i) for i in range(2 * TB)] if route else []
    if not prep:
        others = y + norm + save + rows + route_1 + route_2 + route_3 + scatter
    elif causal:
        start += [("xT", 0), ("xT", 1)]
        maxima = [("mx", i) for i in range(NH * TB)]
        maxima = maxima[0:32] + [("mr", 0), ("ms", 0)] + maxima[32:] + [("mr", 1)]
        others = ([("qk", CHUNKS[0]), ("qk", CHUNKS[1]), ("st_q", 0)] + y + [("qk", CHUNKS[2])]
                  + norm[0:4] + [("qk", CHUNKS[3])] + norm[4:8] + [("v", 0)] + norm[8:16] + [("v", 1), ("st_q", 1)]
                  + mixed(maxima, norm[16:] + save + rows + route_1 + route_2 + route_3 + scatter))
    else:
        combine = pieces("cb", N_COMBINE)
        ahead = [("gi", 0)] + [("ga", i) for i in range(2 * TB)]
        others = (combine[0:16] + ahead + y[0:1] + combine[16:24] + y[1:2] + mixed(combine[24:], norm) + save
                  + [("xT", 0), ("xT", 1), ("qk", 0), ("qk", 2), ("ro", 0)]
                  + mixed([("qk", 1), ("ro", 2), ("st_q", 0), ("qk", 3), ("ro", 1), ("v", 0), ("ro", 3), ("v", 1),
                           ("st_q", 1)], rows + route_1 + route_2 + route_3) + scatter)
    out = [("xl", 0)] if prep else []
    if attn and causal:
        out.append(("ms", 1))
    out += start
    if not attn:
        return out + others
    per_group = len(UNITS_CAUSAL if causal else UNITS_FULL)
    n_units = NG * per_group
    cost = COST[causal]
    total, at = sum(cost.get(step, 0) for step, _ in others), 0
    others = list(others)
    for half in range(2 * (n_units + 2)):
        n = half // 2
        if half % 2 == 0:
            if n < n_units:
                out.append(("st", n))
            if n >= 4 and (n - 4) % per_group == per_group - 1:
                out.append(("on", (n - 4) // per_group))
        elif n >= 2:
            out.append(("av", n - 2))
            if (n - 2) % per_group == per_group - 1:
                out.append(("oe", (n - 2) // per_group))
        while others and (at + cost.get(others[0][0], 0) / 2) * 2 * (n_units + 2) <= total * (half + 1):
            at += cost.get(others[0][0], 0)
            out.append(others.pop(0))
    return out + others + [("on", NG - 1)]


def bank_keys(causal, kind):
    keys = []
    for step, n in schedule(causal, kind):
        if step in ("xT", "qk", "ro", "v", "on", "oT", "y", "rT", "lg", "ps", "mx", "mr"):
            keys.append((step, n))
    return keys


class Banks:

    def __init__(self, causal, ready, free, memory):
        self.ready, self.free, self.memory = ready, free, memory
        self.n = len(memory)
        self.place, self.uses = {}, {}
        for kind in KINDS:
            keys = bank_keys(causal, kind)
            self.place[kind] = {key: (i % self.n, i // self.n) for i, key in enumerate(keys)}
            self.uses[kind] = [sum(i % self.n == b for i in range(len(keys))) for b in range(self.n)]

    def base(self, turn, b):
        u = {kind: self.uses[kind][b] for kind in KINDS}
        if turn.kind == "first":
            return 0
        if turn.kind == "second":
            return u["first"]
        before = u["first"] + u["second"]
        if turn.kind == "body":
            return turn.it * (2 * u["body"]) + (before + (turn.s - 2) * u["body"])
        before += (NB - 2) * u["body"]
        return before if turn.kind == "eighth" else before + u["eighth"]

    def acquire(self, pe, turn, key):
        b, n = self.place[turn.kind][key]
        wait(pe, self.free[b], self.base(turn, b) + n)
        return self.memory[b], self.ready[b]

    def filled(self, eng, turn, key):
        b, n = self.place[turn.kind][key]
        eng.wait_ge(self.ready[b], self.base(turn, b) + (n + 1))
        return self.memory[b], self.free[b]

    def read(self, eng, turn, key):
        b, n = self.place[turn.kind][key]
        eng.wait_ge(self.free[b], self.base(turn, b) + (n + 1))

    def total(self, b):
        u = {kind: self.uses[kind][b] for kind in KINDS}
        return sum(u.values()) + (NB - 3) * u["body"]

    def all_before_read(self, eng, turn):
        for b in range(self.n):
            wait(eng, self.free[b], self.base(turn, b))


class Chain:

    def __init__(self, eng, sem, base):
        self.eng, self.sem, self.base, self.n = eng, sem, base, 0

    def unwaited(self, instruction):
        self.n += 1
        instruction.then_inc(self.sem, 1)

    def join(self):
        wait(self.eng, self.sem, self.base + self.n)

    def pause(self):
        yield
        self.join()

    def __call__(self, instruction):
        self.unwaited(instruction)
        yield from self.pause()

    def step(self, instruction):
        self.unwaited(instruction)
        self.join()


def all_of(chained):
    for _ in chained:
        pass


def together(a, b, ratio):
    for _ in a:
        for _ in range(ratio):
            next(b, None)
    all_of(b)


class InPieces:

    def __init__(self, count):
        self.count, self.running = count, {}

    def piece(self, step, i, start):
        if i == 0:
            self.running[step] = start()
        if i == self.count[step] - 1:
            all_of(self.running[step])
        else:
            next(self.running[step], None)


RSQRT_STEPS = 13


def rsqrt(dve, chain, out, x, tmp):
    yield from chain(dve.tensor_scalar(out.bitcast(I32), x.bitcast(I32), -0.5, RSQRT_MAGIC, ALU.mult, ALU.add))
    for _ in range(3):
        yield from chain(dve.tensor_tensor(tmp, out, out, ALU.mult))
        yield from chain(dve.tensor_tensor(tmp, tmp, x, ALU.mult))
        yield from chain(dve.tensor_scalar(tmp, tmp, -0.5, 1.5, ALU.mult, ALU.add))
        yield from chain(dve.tensor_tensor(out, out, tmp, ALU.mult))


def spread(ap, n):
    return ap.unsqueeze(2).broadcast_to([ap.shape[0], ap.shape[1], n])


def build(nc, a, out):
    with ExitStack() as ctx:
        def sb(name, shape, dt=F32):
            return ctx.enter_context(nc.sbuf_tensor(name, shape, dt))

        def psum(name, shape, dt=F32):
            return ctx.enter_context(nc.psum_tensor(name, shape, dt))

        def sem(name):
            return ctx.enter_context(nc.semaphore(name))

        def dram(name, shape, dt=F32):
            return nc.dram_tensor(name, shape, dt, kind="Internal").ap()

        parts = dram("qk_parts", [2, 2, 3, D, S], BF16)
        x1_dram = dram("x1_rows", [NTOK, D])
        x3_dram = dram("x3_rows", [NTOK, D])
        slot_x0 = dram("slot_x0", [E0 * CAP, D])
        slot_y0 = dram("slot_y0", [E0 * CAP, D])
        slot_x1 = dram("slot_x1", [ZROW + P, D])
        slot_y1 = dram("slot_y1", [NBLK * P, D])

        ident = sb("ident", [P, P])
        ident_b = sb("ident_b", [P, P], BF16)
        before = sb("before", [P, P], BF16)
        ones_b = sb("ones_b", [P, P], BF16)
        mask = sb("mask", [P, S])
        rot = sb("rot", [P, P])
        cos_t = sb("cos_t", [P, S])
        sin_t = sb("sin_t", [P, S])
        lane = sb("lane", [P, 304])
        zero = sb("zero", [P, D])

        arena = sb("arena", [P, 21504])
        stack_words = NH * S // 2
        Q = [arena[:, i * stack_words:(i + 1) * stack_words].bitcast(BF16).rearrange("p (h n) -> p h n", h=NH)
             for i in (0, 1)]
        K = [arena[:, i * stack_words:(i + 1) * stack_words].bitcast(BF16).rearrange("p (h n) -> p h n", h=NH)
             for i in (2, 3)]
        pt_at = 4 * stack_words
        PT = [arena[:, pt_at + i * 1024:pt_at + (i + 1) * 1024].rearrange("p (h n) -> p h n", h=GH)
              for i in range(RING)]

        w_qkv = sb("w_qkv", [P, CD, 3 * D])
        w_o = sb("w_o", [P, CD, D])
        w_r = sb("w_r", [P, CD, NE1])
        b_qk = sb("b_qk", [P, 4])
        b_v = sb("b_v", [P, D])
        b_o = sb("b_o", [P, D])
        rn_scale = sb("rn_scale", [P, 2, CD])
        x_in = [sb(f"x_in{i}", [P, TB, D]) for i in range(2)]
        xT = sb("xT", [P, CD, S])
        qk_src = [sb(f"qk_src{j}", [P, 3, S], BF16) for j in range(4)]
        qk_rest = [sb(f"qk_rest{i}", [P, S]) for i in range(2)]
        v_aug = [sb(f"v_aug{i}", [P, TB, NH, 32]) for i in range(2)]
        oT_raw = [sb(f"oT_raw{i}", [P, S]) for i in range(2)]
        o_nat = sb("o_nat", [P, TB, D])
        oT = sb("oT", [P, CD, S])
        x_res = sb("x_res", [P, TB, D])
        y_b = sb("y_b", [P, TB, D])
        x_out = [sb(f"x_out{i}", [P, TB, D]) for i in range(2)]
        rT = oT
        scratch = sb("scratch", [P, S])
        junk = [scratch[:, i * (S // 2):(i + 1) * (S // 2)].bitcast(BF16) for i in range(2)]
        mx = sb("mx", [P, NH * TB])
        mx_rest = sb("mx_rest", [P, NH * TB])
        mx_parts = sb("mx_parts", [P, 3, NH * TB], BF16)
        mx_rows = [sb(f"mx_rows{i}", [NH * TB // 2, 3, P], BF16) for i in range(2)]
        o_sum = sb("o_sum", [P, TB * GH])
        stats = sb("stats", [P, TB, 6])
        mv = sb("mv", [P, TB, 2])
        small = sb("small", [P, 16, TB])
        norm_to = stats, mv, [small[:, i, :] for i in (2, 1, 0)]
        NEM = NE1
        r_lg = sb("r_lg", [P, TB, NEM])
        r_w = sb("r_w", [P, TB, NEM])
        r_c = sb("r_c", [P, TB, NEM])
        r_oh = sb("r_oh", [P, 2, TB, NEM])
        r_pos = sb("r_pos", [P, TB, NEM])
        r_s = sb("r_s", [P, 24, TB])
        r_mask = sb("r_mask", [P, TB, NEM], BF16)
        r_before = sb("r_before", [P, TB + 1, NEM], BF16)
        row_to = [sb(f"row_to{i}", [P, TB, 2], I32) for i in range(2)]
        row_from0 = sb("row_from0", [P, NB + 1, TB * 2], I32)
        gate0 = sb("gate0", [P, NB + 1, TB * 3])
        row_now = [sb(f"row_now{i}", [P, TB * 2], I32) for i in range(2)]

        ST = [psum(f"ST{i}", [P, 1024]) for i in range(2)]
        OT = psum("OT", [P, 512])
        shared = [psum(f"shared{i}", [P, 512]) for i in range(3)]

        s_const = sem("s_const")
        s_fill = sem("s_fill")
        s_fill2 = sem("s_fill2")
        s_zero = sem("s_zero")
        s_tick = sem("s_tick")

        def settle(eng):
            eng.sem_inc(s_tick, 1)

        def layer_sems(t):
            names = dict(
                weights="weights", xp="residual_ready", q1="first_part", q2="second_part", q3="third_part",
                rest="rest_ready", parts_saved="parts_saved",
                st="scores_ready", exp="weights_ready", sel="masked", av="unit_used", oe="out_saved",
                osum="out_sum_ready", ttr="max_taken", mchain="max_split", mtaken="max_rows_taken",
                lnc="norm_chain", x_out="x_out_ready", rc="route_chain", ex="route_exp", ga_idx="rows_known",
                comb="combine_chain", xn="xn_ready", rot="rotated", rope="rope_chain", qf="qk_biased",
                wprep="weights_scaled")
            d = {k: sem(f"{t}_{v}") for k, v in names.items()}
            for k in ("x_load", "scattered", "x_saved", "gathered", "max_rows_saved"):
                d[k] = [sem(f"{t}_{k}{i}") for i in range(2)]
            d["stacked"] = [[sem(f"{t}_stacked{i}{j}") for j in range(2)] for i in range(2)]
            d["ready"] = [sem(f"{t}_bank_ready{i}") for i in range(3)]
            d["free"] = [sem(f"{t}_bank_free{i}") for i in range(3)]
            return d

        LA = layer_sems("a")
        banks_a = Banks(True, LA["ready"], LA["free"], shared)
        U0 = NG * len(UNITS_CAUSAL)

        ROUTE0 = 46
        LN_CHAIN = TB + TB + 1 + RSQRT_STEPS

        block = ctx.enter_context(nc.Block())

        def a_sp(sp):
            L = LA

            def emit(turn):
                for step, n in schedule(True, turn.kind):
                    if step == "xl":
                        k, par, half = turn.batch(0)
                        wait(sp, L["xp"], k - 1)
                        settle(sp)
                        sp.dma_start(x_in[par][:, :, :],
                                     a["x"][bass.ds(k * S, S), :].rearrange("(t p) d -> p t d", p=P)
                                     ).then_inc(L["x_load"][par], 16)
                    elif step == "qk":
                        k, par, half = turn.batch(0)
                        order = CHUNKS.index(n)
                        wait(sp, L["stacked"][par][n % 2], half * STACK_DMAS)
                        settle(sp)
                        sp.wait_ge(L["q3"], k * 4 + (order + 1))
                        settle(sp)
                        sp.dma_start(parts[par, n // 2, :, (n % 2) * P:(n % 2 + 1) * P, :].rearrange("j p n -> p j n"),
                                     qk_src[n][:, :, :]).then_inc(L["parts_saved"], 16)
                    elif step == "st_q":
                        k, par, half = turn.batch(0)
                        sp.wait_ge(L["parts_saved"], k * 64 + (32 * n + 32))
                        settle(sp)
                        wait(sp, L["exp"], (k - 1) * U0)
                        settle(sp)
                        heads = slice(n * NH // 2, (n + 1) * NH // 2)
                        for t, (i, j) in enumerate(PRODUCTS):
                            for side, part, stack in ((0, i, Q), (1, j, K)):
                                sp.dma_start(stack[par][t * HD:(t + 1) * HD, heads, :],
                                             parts[par, side, part, n * P:(n + 1) * P, :].rearrange(
                                                 "(h d) n -> d h n", d=HD)).then_inc(L["stacked"][par][n], 16)
                    elif step == "ms":
                        k, par, half = turn.batch(n)
                        sp.wait_ge(L["mtaken"], k * 2 + (n + 1))
                        settle(sp)
                        for j in range(3):
                            sp.dma_start(Q[par][SK + j:SK + j + 1, n * NH // 2:(n + 1) * NH // 2, :].rearrange(
                                "p h (b n) -> p (h b) n", b=TB), mx_rows[n][:, j, :]
                                         ).then_inc(L["max_rows_saved"][n], 16)
                    elif step == "sv":
                        k, par, half = turn.batch(2)
                        sp.wait_ge(L["x_out"], k * TB + TB)
                        settle(sp)
                        sp.dma_start(x1_dram[bass.ds(k * S, S), :].rearrange("(t p) d -> p t d", p=P),
                                     x_out[par][:, :, :]).then_inc(L["x_saved"][par], 16)
            slots(sp, emit)

        def attention_pe(pe, L, banks, causal, turn, step, n, U):
            k, par, half = turn.batch(1)
            units = UNITS_CAUSAL if causal else UNITS_FULL
            per = len(units)
            rows = SK + 3 if causal else SK
            if step == "st":
                if n == 0:
                    banks.all_before_read(pe, turn)
                if n % (U // 2) == 0:
                    if causal:
                        pe.wait_ge(L["max_rows_saved"][n // (U // 2)], k * 48 + 48)
                    else:
                        pe.wait_ge(L["stacked"][par][n // (U // 2)], half * STACK_DMAS + STACK_DMAS)
                wait(pe, L["exp"], k * U + (n - 1))
                g, u = n // per, n % per
                for i in range(GH):
                    h = g * GH + i
                    for kb, q0, nq, at in units[u]:
                        mm = pe.matmul(ST[n % 2][:, i * 256 + at:i * 256 + at + nq],
                                       K[par][0:rows, h, kb * P:(kb + 1) * P],
                                       Q[par][0:rows, h, q0:q0 + nq], start=True, stop=True)
                mm.then_inc(L["st"], 1)
            elif step == "av":
                g, u = n // per, n % per
                if u == 0:
                    wait(pe, L["oe"], k * NG + g)
                if causal and u in DIAGONAL:
                    pe.wait_ge(L["sel"], k * (3 * NG) + (g * 3 + sorted(DIAGONAL).index(u) + 1))
                else:
                    pe.wait_ge(L["exp"], k * U + (n + 1))
                for piece, (kb, q0, nq, at) in enumerate(units[u]):
                    for i in range(GH):
                        mm = pe.matmul(OT[32 * i:32 * i + 32, q0:q0 + nq],
                                       v_aug[par][:, kb, g * GH + i, :],
                                       PT[n % RING][:, i, at:at + nq],
                                       start=(u == 0), stop=(u == per - 1),
                                       skip_group_check=True, tile_position=(0, 32 * i))
                mm.then_inc(L["av"], 1)
            elif step == "on":
                bank, ready = banks.acquire(pe, turn, ("on", n))
                pe.wait_ge(L["oe"], k * NG + (n + 1))
                for t in range(TB):
                    mm = pe.transpose(bank[:, t * P:(t + 1) * P], oT_raw[n % 2][:, t * P:(t + 1) * P], ident[:, :])
                mm.then_inc(ready, 1)
            elif step == "oT":
                bank, ready = banks.acquire(pe, turn, ("oT", n))
                if n == 0:
                    banks.all_before_read(pe, turn)
                for t in range(TB):
                    mm = pe.transpose(bank[:, t * P:(t + 1) * P], o_nat[:, t, n * P:(n + 1) * P], ident[:, :])
                mm.then_inc(ready, 1)
            elif step == "y":
                bank, ready = banks.acquire(pe, turn, ("y", n))
                if n == 0:
                    banks.read(pe, turn, ("oT", 0))
                    banks.read(pe, turn, ("oT", 1))
                for t in (2 * n, 2 * n + 1):
                    for c in range(CD):
                        mm = pe.matmul(bank[:, (t % 2) * D:(t % 2 + 1) * D], oT[:, c, t * P:(t + 1) * P],
                                       w_o[:, c, :], start=(c == 0), stop=(c == CD - 1))
                mm.then_inc(ready, 1)

        def route_pe(pe, L, banks, turn, step, n, ne, chain_len, mask_at):
            k, par, half = turn.batch(2)
            if step == "rT":
                bank, ready = banks.acquire(pe, turn, ("rT", n))
                pe.wait_ge(L["x_out"], k * TB + TB)
                for t in range(TB):
                    mm = pe.transpose(bank[:, t * P:(t + 1) * P], x_out[par][:, t, n * P:(n + 1) * P], ident[:, :])
                mm.then_inc(ready, 1)
            elif step == "lg":
                bank, ready = banks.acquire(pe, turn, ("lg", 0))
                banks.read(pe, turn, ("rT", 0))
                banks.read(pe, turn, ("rT", 1))
                for t in range(TB):
                    for c in range(CD):
                        mm = pe.matmul(bank[:, t * ne:(t + 1) * ne], rT[:, c, t * P:(t + 1) * P],
                                       w_r[:, c, 0:ne], start=(c == 0), stop=(c == CD - 1))
                mm.then_inc(ready, 1)
            elif step == "ps":
                bank, ready = banks.acquire(pe, turn, ("ps", 0))
                pe.wait_ge(L["rc"], k * chain_len + mask_at)
                for t in range(TB):
                    pe.matmul(bank[:, t * ne:(t + 1) * ne], before[:, :], r_mask[:, t, 0:ne],
                              start=True, stop=False)
                    mm = pe.matmul(bank[:, t * ne:(t + 1) * ne], ones_b[:, :], r_before[:, t, 0:ne],
                                   start=False, stop=True)
                mm.then_inc(ready, 1)

        def a_pe(pe):
            L, banks = LA, banks_a
            pe.wait_ge(s_const, CONST_DMAS * 16)
            pe.wait_ge(s_fill2, 1)

            def emit(turn):
                for step, n in schedule(True, turn.kind):
                    k, par, half = turn.batch(0)
                    if step == "xT":
                        bank, ready = banks.acquire(pe, turn, ("xT", n))
                        if n == 0:
                            pe.wait_ge(L["x_load"][par], half * 16 + 16)
                        for t in range(TB):
                            mm = pe.transpose(bank[:, t * P:(t + 1) * P], x_in[par][:, t, n * P:(n + 1) * P],
                                              ident[:, :])
                        mm.then_inc(ready, 1)
                    elif step == "qk":
                        bank, ready = banks.acquire(pe, turn, ("qk", n))
                        if n == 0:
                            banks.read(pe, turn, ("xT", 0))
                            banks.read(pe, turn, ("xT", 1))
                        for c in range(CD):
                            mm = pe.matmul(bank[:, :], w_qkv[:, c, n * P:(n + 1) * P], xT[:, c, :],
                                           start=(c == 0), stop=(c == CD - 1))
                        mm.then_inc(ready, 1)
                    elif step == "v":
                        bank, ready = banks.acquire(pe, turn, ("v", n))
                        for t in (2 * n, 2 * n + 1):
                            for c in range(CD):
                                mm = pe.matmul(bank[:, (t % 2) * D:(t % 2 + 1) * D], xT[:, c, t * P:(t + 1) * P],
                                               w_qkv[:, c, 2 * D:3 * D], start=(c == 0), stop=(c == CD - 1))
                        mm.then_inc(ready, 1)
                    elif step == "mx":
                        if n % 32 == 0:
                            pe.wait_ge(L["stacked"][par][n // 32], half * STACK_DMAS + STACK_DMAS)
                        head, qb = n // TB, n % TB
                        bank, ready = banks.acquire(pe, turn, ("mx", n))
                        pe.matmul(bank[:, 0:S - qb * P], Q[par][0:SK, head, qb * P:(qb + 1) * P],
                                  K[par][0:SK, head, qb * P:S], start=True, stop=True).then_inc(ready, 1)
                    elif step == "mr":
                        bank, ready = banks.acquire(pe, turn, ("mr", n))
                        pe.wait_ge(L["mchain"], k * 8 + (4 * n + 4))
                        settle(pe)
                        for j in range(3):
                            mm = pe.transpose(bank[0:32, j * 64:(j + 1) * 64].bitcast(BF16),
                                              mx_parts[:, j, n * 32:(n + 1) * 32], ident_b[:, :])
                        mm.then_inc(ready, 1)
                    elif step in ("st", "av", "on", "oT", "y"):
                        attention_pe(pe, L, banks, True, turn, step, n, U0)
                    elif step in ("rT", "lg", "ps"):
                        route_pe(pe, L, banks, turn, step, n, NE0, ROUTE0, MASK0)
            slots(pe, emit)

        def attention_act(act, L, causal, turn, step, n, U, func):
            k, par, half = turn.batch(1)
            if step == "st":
                act.wait_ge(L["st"], k * U + (n + 1))
                wait(act, L["av"], k * U + (n + 1 - RING))
                act.activation(PT[n % RING][:, :, :], ST[n % 2][:, :].rearrange("p (h n) -> p h n", h=GH),
                               func, scale=ATT_SCALE).then_inc(L["exp"], 1)
            elif step == "oe":
                per = U // NG
                act.wait_ge(L["av"], k * U + (n + 1) * per)
                act.activation(oT_raw[n % 2][:, :], OT[:, :], ACT.Identity).then_inc(L["oe"], 1)

        def copy_bank(act, banks, turn, key, to):
            bank, free = banks.filled(act, turn, key)
            act.activation(to, bank[:, :], ACT.Identity).then_inc(free, 1)

        def a_act(act):
            L, banks = LA, banks_a
            act.wait_ge(s_const, CONST_DMAS * 16)

            def emit(turn):
                for step, n in schedule(True, turn.kind):
                    k, par, half = turn.batch(0)
                    if step == "xT":
                        copy_bank(act, banks, turn, ("xT", n), xT[:, n, :])
                    elif step == "qk":
                        bank, free = banks.filled(act, turn, ("qk", n))
                        wait(act, L["parts_saved"], k * 64)
                        act.activation(qk_src[n][:, 0, :], bank[:, :], ACT.Identity,
                                       bias=b_qk[:, n:n + 1]).then_inc(L["q1"], 1)
                    elif step in ("st", "oe"):
                        attention_act(act, L, True, turn, step, n, U0, ACT.Exp)
                    elif step == "oT":
                        copy_bank(act, banks, turn, ("oT", n), oT[:, n, :])
                    elif step == "rT":
                        copy_bank(act, banks, turn, ("rT", n), rT[:, n, :])
                    elif step == "ex":
                        k, par, half = turn.batch(2)
                        act.wait_ge(L["rc"], k * ROUTE0 + 3)
                        act.activation(r_w[:, :, 0:NE0], r_w[:, :, 0:NE0], ACT.Exp).then_inc(L["ex"], 1)
            slots(act, emit)

        def norm_stats_dve(dve, chain, src, to):
            stats, mv, _ = to
            for t in range(TB):
                chain.unwaited(dve.bn_stats(stats[:, t, :], src[:, t, :]))
                yield
            yield from chain.pause()
            settle(dve)
            for t in range(TB):
                chain.unwaited(dve.bn_aggr(mv[:, t, :], stats[:, t, :]))
            yield from chain.pause()

        def norm_root_dve(dve, chain, to):
            _, mv, (tmp, root, shifted) = to
            yield from chain(dve.tensor_scalar(shifted, mv[:, :, 1], LN_EPS, None, ALU.add))
            yield from rsqrt(dve, chain, root, shifted, tmp)

        def attention_dve(dve, L, banks, turn, step, n, eps):
            k, par, half = turn.batch(1 if step == "on" else 2)
            if step == "on":
                bank, free = banks.filled(dve, turn, ("on", n))
                view = bank[:, :].rearrange("p (th c) -> p th c", c=32)
                if n:
                    banks.read(dve, turn, ("on", n - 1))
                if eps:
                    dve.tensor_scalar(o_sum[:, :], view[:, :, HD], eps, None, ALU.add).then_inc(L["osum"], 1)
                    dve.wait_ge(L["osum"], k * (2 * NG) + (2 * n + 1))
                    dve.reciprocal(o_sum[:, :], o_sum[:, :]).then_inc(L["osum"], 1)
                    dve.wait_ge(L["osum"], k * (2 * NG) + (2 * n + 2))
                else:
                    dve.reciprocal(o_sum[:, :], view[:, :, HD]).then_inc(L["osum"], 1)
                    dve.wait_ge(L["osum"], k * NG + (n + 1))
                dve.tensor_tensor(
                    o_nat[:, :, n * GH * HD:(n + 1) * GH * HD].rearrange("p t (h d) -> p t h d", h=GH),
                    view[:, :, 0:HD].rearrange("p (t h) d -> p t h d", t=TB),
                    spread(o_sum[:, :], HD).rearrange("p (t h) d -> p t h d", t=TB),
                    ALU.mult).then_inc(free, 1)
            elif step == "y":
                bank, free = banks.filled(dve, turn, ("y", n))
                wait(dve, L["x_out"], k * TB)
                dve.wait_ge(L["xp"], k + 1)
                dve.tensor_tensor(y_b[:, 2 * n:2 * n + 2, :], bank[:, :].rearrange("p (t d) -> p t d", t=2),
                                  x_res[:, 2 * n:2 * n + 2, :], ALU.add).then_inc(free, 1)

        def finish_dve(dve, L, banks, turn):
            k, par, half = turn.batch(2)
            for i in range(2):
                banks.read(dve, turn, ("y", i))
            chain = Chain(dve, L["lnc"], k * LN_CHAIN)
            yield from norm_stats_dve(dve, chain, y_b, norm_to)
            yield from norm_root_dve(dve, chain, norm_to)
            assert chain.n == LN_CHAIN
            wait(dve, L["x_saved"][par], half * 16)
            wait(dve, L["scattered"][par], half * (16 * 2 * TB))
            for t in range(TB):
                dve.tensor_scalar(x_out[par][:, t, :], y_b[:, t, :], mv[:, t, 0:1], small[:, 1, t:t + 1],
                                  ALU.subtract, ALU.mult).then_inc(L["x_out"], 1)
                yield

        def first_choice(dve, chain, w, ne, best, rank, oh):
            yield from chain(dve.tensor_reduce(best, w, AX_X, ALU.max))
            yield from chain(dve.tensor_tensor(r_c[:, :, 0:ne], w, spread(best, ne), ALU.is_ge))
            yield from chain(dve.tensor_tensor(r_c[:, :, 0:ne], r_c[:, :, 0:ne],
                                    rank.unsqueeze(1).broadcast_to([P, TB, ne]), ALU.mult))
            yield from chain(dve.tensor_reduce(r_s[:, 0, :], r_c[:, :, 0:ne], AX_X, ALU.max))
            yield from chain(dve.tensor_tensor(oh, r_c[:, :, 0:ne], spread(r_s[:, 0, :], ne), ALU.is_equal))

        def count_before(dve, chain, ne):
            yield from chain(dve.tensor_copy(r_before[:, 0, 0:ne], r_before[:, TB, 0:ne]))
            for t in range(TB):
                yield from chain(dve.tensor_tensor(r_before[:, t + 1, 0:ne], r_before[:, t, 0:ne], r_mask[:, t, 0:ne],
                                        ALU.add))

        def lanes(at, n):
            return lane[:, at:at + n].unsqueeze(1).broadcast_to([P, TB, n])

        def a_route_dve(dve, banks, turn, step):
            L, ne = LA, NE0
            k, par, half = turn.batch(2)
            w = r_w[:, :, 0:ne]
            oh = [r_oh[:, i, :, 0:ne] for i in range(2)]
            if step == "l1":
                chain = Chain(dve, L["rc"], k * ROUTE0)
                bank, free = banks.filled(dve, turn, ("lg", 0))
                dve.tensor_tensor(r_lg[:, :, 0:ne], bank[:, 0:TB * ne].rearrange("p (t e) -> p t e", t=TB),
                                  lanes(LANE_RB0, ne), ALU.add).then_inc(free, 1)
                yield
                banks.read(dve, turn, ("lg", 0))
                yield from chain(dve.tensor_reduce(r_s[:, 1, :], r_lg[:, :, 0:ne], AX_X, ALU.max))
                yield from chain(dve.tensor_tensor(w, r_lg[:, :, 0:ne], spread(r_s[:, 1, :], ne), ALU.subtract))
                chain.unwaited(dve.memset(r_s[:, 2, :], 0.0))
                assert chain.n == 3
            elif step == "l2":
                chain = Chain(dve, L["rc"], k * ROUTE0)
                chain.n = 3
                dve.wait_ge(L["ex"], k + 1)
                yield from chain(dve.tensor_reduce(r_s[:, 2, :], w, AX_X, ALU.add))
                yield from chain(dve.reciprocal(r_s[:, 3, :], r_s[:, 2, :]))
                yield from chain(dve.tensor_tensor(w, w, spread(r_s[:, 3, :], ne), ALU.mult))
                yield from first_choice(dve, chain, w, ne, r_s[:, 4, :], lane[:, LANE_RANK0:LANE_RANK0 + ne], oh[0])
                yield from chain(dve.scalar_tensor_tensor(out=r_lg[:, :, 0:ne].rearrange("p t e -> p t e"), in0=oh[0],
                                               scalar=-2.0, in1=w, op0=ALU.mult, op1=ALU.add))
                yield from first_choice(dve, chain, r_lg[:, :, 0:ne], ne, r_s[:, 5, :],
                             lane[:, LANE_RANK0:LANE_RANK0 + ne], oh[1])
                yield from chain(dve.tensor_scalar(r_s[:, 6, :], r_s[:, 5, :], 0.0, None, ALU.is_gt))
                yield from chain(dve.tensor_tensor(oh[1], oh[1], spread(r_s[:, 6, :], ne), ALU.mult))
                yield from chain(dve.tensor_tensor(r_mask[:, :, 0:ne], oh[0], oh[1], ALU.add))
                yield from count_before(dve, chain, ne)
                assert chain.n == MASK0, chain.n
            elif step == "l3":
                chain = Chain(dve, L["rc"], k * ROUTE0)
                chain.n = MASK0
                bank, free = banks.filled(dve, turn, ("ps", 0))
                pos = bank[:, 0:TB * ne].rearrange("p (t e) -> p t e", t=TB)
                chain.unwaited(dve.tensor_tensor(r_c[:, :, 0:ne], pos, lanes(LANE_CAP, ne), ALU.is_lt))
                dve.tensor_tensor(r_pos[:, :, 0:ne], pos, lanes(LANE_SEG0, ne), ALU.add).then_inc(free, 1)
                yield from chain.pause()
                banks.read(dve, turn, ("ps", 0))
                yield from chain(dve.tensor_tensor(r_s[:, 7, :], oh[0][:, :, E0], r_s[:, 4, :], ALU.mult))
                yield from chain(dve.tensor_tensor(r_s[:, 8, :], oh[1][:, :, E0], r_s[:, 5, :], ALU.mult))
                yield from chain(dve.tensor_tensor(r_s[:, 7, :], r_s[:, 7, :], r_s[:, 8, :], ALU.add))
                g = gate0[:, bass.ds(k, 1), :].rearrange("p b (t c) -> p (b t) c", c=3)
                rows = row_from0[:, bass.ds(k, 1), :].rearrange("p b (t c) -> p (b t) c", c=2)
                yield from chain(dve.tensor_scalar(g[:, :, 2], r_s[:, 7, :], 1.0, None, ALU.add))
                wait(dve, L["scattered"][par], half * (16 * 2 * TB))
                for i in range(2):
                    yield from chain(dve.tensor_tensor(oh[i], oh[i], r_c[:, :, 0:ne], ALU.mult))
                    yield from chain(dve.tensor_reduce(r_s[:, 9, :], oh[i], AX_X, ALU.add))
                    yield from chain(dve.tensor_tensor(oh[i], oh[i], r_pos[:, :, 0:ne], ALU.mult))
                    yield from chain(dve.tensor_reduce(r_s[:, 10, :], oh[i], AX_X, ALU.add))
                    yield from chain(dve.tensor_tensor(g[:, :, i], r_s[:, 4 + i, :], r_s[:, 9, :], ALU.mult))
                    yield from chain(dve.tensor_copy(rows[:, :, i], r_s[:, 10, :]))
                    yield from chain(dve.tensor_scalar(r_s[:, 11, :], r_s[:, 9, :], -FAR, FAR, ALU.mult, ALU.add))
                    yield from chain(dve.tensor_tensor(row_to[par][:, :, i], r_s[:, 10, :], r_s[:, 11, :], ALU.add))
                assert chain.n == ROUTE0, chain.n

        def a_dve(dve):
            L, banks = LA, banks_a
            chains = InPieces(dict(zip(("ln", "l1", "l2", "l3"), (N_LN,) + N_ROUTE[True])))
            dve.wait_ge(s_const, CONST_DMAS * 16)
            dve.memset(zero[:, :], 0.0).then_inc(s_zero, 1)
            dve.tensor_copy(ident_b[:, :], ident[:, :]).then_inc(s_fill, 1)
            dve.tensor_copy(before[:, :], scratch[:, 0:P]).then_inc(s_fill, 1)
            dve.memset(ones_b[:, :], 1.0).then_inc(s_fill, 1)
            dve.memset(row_from0[:, NB, :], 0).then_inc(s_fill, 1)
            dve.memset(gate0[:, NB, :], 0.0).then_inc(s_fill, 1)
            for i in range(2):
                dve.memset(v_aug[i][:, :, :, :], 0.0).then_inc(s_fill, 1)
            dve.memset(r_before[:, :, :], 0.0).then_inc(s_fill, 1)
            dve.wait_ge(s_fill, 8)
            for i in range(2):
                dve.memset(v_aug[i][:, :, :, HD], 1.0).then_inc(s_fill, 1)
                dve.memset(K[i][SK:SK + 3, :, :], 1.0).then_inc(s_fill, 1)
            dve.wait_ge(s_fill, 12)
            dve.memset(junk[0][:, 0:2], 0.0).then_inc(s_fill2, 1)
            dve.wait_ge(s_fill2, 1)

            def emit(turn):
                for step, n in schedule(True, turn.kind):
                    k, par, half = turn.batch(0)
                    if step == "qk":
                        order = CHUNKS.index(n)
                        bank, free = banks.filled(dve, turn, ("qk", n))
                        dve.wait_ge(L["q1"], k * 4 + (order + 1))
                        wait(dve, L["q3"], k * 4 + (order - 1))
                        dve.scalar_tensor_tensor(out=qk_rest[order % 2][:, :], in0=bank[:, :],
                                                 scalar=b_qk[:, n:n + 1], in1=qk_src[n][:, 0, :],
                                                 op0=ALU.add, op1=ALU.subtract).then_inc(free, 1)
                        banks.read(dve, turn, ("qk", n))
                        dve.tensor_copy(qk_src[n][:, 1, :], qk_rest[order % 2][:, :]).then_inc(L["q2"], 1)
                    elif step == "v":
                        bank, free = banks.filled(dve, turn, ("v", n))
                        wait(dve, L["av"], (k - 1) * U0)
                        dve.tensor_tensor(
                            v_aug[par][:, 2 * n:2 * n + 2, :, 0:HD],
                            bank[:, :].rearrange("p (t h d) -> p t h d", t=2, h=NH),
                            b_v[:, :].rearrange("p (h d) -> p h d", h=NH).unsqueeze(1).broadcast_to([P, 2, NH, HD]),
                            ALU.add).then_inc(free, 1)
                    elif step == "mx":
                        bank, free = banks.filled(dve, turn, ("mx", n))
                        if n >= 2:
                            banks.read(dve, turn, ("mx", n - 2))
                        elif turn.kind != "first":
                            banks.all_before_read(dve, turn)
                        m = S - n % TB * P
                        settle(dve)
                        dve.tensor_tensor_reduce(out=junk[n % 2][:, 0:m], in0=bank[:, 0:m], in1=mask[:, 0:m],
                                                 scale=1.0, scalar=LOW, op0=ALU.add, op1=ALU.max,
                                                 accum_out=mx[:, n:n + 1]).then_inc(free, 1)
                    elif step == "mr":
                        for i in (30, 31):
                            banks.read(dve, turn, ("mx", 32 * n + i))
                        chain = Chain(dve, L["mchain"], k * 8 + 4 * n)
                        top, rest = mx[:, n * 32:(n + 1) * 32], mx_rest[:, n * 32:(n + 1) * 32]
                        part = [mx_parts[:, j, n * 32:(n + 1) * 32] for j in range(3)]
                        chain.step(dve.tensor_scalar(part[0], top, -1.0, None, ALU.mult))
                        chain.step(dve.scalar_tensor_tensor(out=rest, in0=top, scalar=-1.0, in1=part[0],
                                                            op0=ALU.mult, op1=ALU.subtract))
                        chain.step(dve.tensor_copy(part[1], rest))
                        chain.step(dve.tensor_tensor(part[2], rest, part[1], ALU.subtract))
                        bank, free = banks.filled(dve, turn, ("mr", n))
                        wait(dve, L["max_rows_saved"][n], k * 48)
                        dve.tensor_copy(mx_rows[n][:, :, :],
                                        bank[0:32, 0:192].bitcast(BF16).rearrange("p (j n) -> p j n", j=3)
                                        ).then_inc(free, 1)
                        banks.read(dve, turn, ("mr", n))
                        dve.sem_inc(L["mtaken"], 1)
                    elif step in ("on", "y"):
                        attention_dve(dve, L, banks, turn, step, n, 0)
                    elif step == "ln":
                        chains.piece(step, n, lambda: finish_dve(dve, L, banks, turn))
                    elif step in ("l1", "l2", "l3"):
                        chains.piece(step, n, lambda: a_route_dve(dve, banks, turn, step))
            slots(dve, emit)

        def a_pool(pool):
            L = LA
            pool.wait_ge(s_const, CONST_DMAS * 16)

            def emit(turn):
                for step, n in schedule(True, turn.kind):
                    k, par, half = turn.batch(0)
                    if step == "xp":
                        k, par, half = turn.batch(1)
                        pool.wait_ge(L["x_load"][par], half * 16 + 16)
                        wait(pool, L["x_out"], k * TB)
                        pool.tensor_tensor(out=x_res[:, :, :], in0=x_in[par][:, :, :],
                                           in1=b_o[:, :].unsqueeze(1).broadcast_to([P, TB, D]),
                                           op=ALU.add).then_inc(L["xp"], 1)
                    elif step == "qk":
                        order = CHUNKS.index(n)
                        pool.wait_ge(L["q2"], k * 4 + (order + 1))
                        pool.tensor_tensor(out=qk_src[n][:, 2, :], in0=qk_rest[order % 2][:, :],
                                           in1=qk_src[n][:, 1, :], op=ALU.subtract).then_inc(L["q3"], 1)
                    elif step == "st":
                        k, par, half = turn.batch(1)
                        u = n % len(UNITS_CAUSAL)
                        if u not in DIAGONAL:
                            continue
                        at, blocks = DIAGONAL[u]
                        pool.wait_ge(L["exp"], k * U0 + (n + 1))
                        settle(pool)
                        v = PT[n % RING][:, :, at:at + blocks * P].rearrange("p h (b q) -> p h b q", q=P)
                        pool.affine_select(out=v, in_=v, compare_op=ALU.is_ge, fill=0.0, base=0,
                                           pattern=[[0, GH], [0, blocks], [-1, P]],
                                           channel_multiplier=1).then_inc(L["sel"], 1)
                    elif step == "sc":
                        k, par, half = turn.batch(2)
                        if n == 0:
                            pool.wait_ge(L["rc"], k * ROUTE0 + ROUTE0)
                            pool.wait_ge(s_filled_rows, 16)
                            settle(pool)
                        t, i = n // 2, n % 2
                        pool.indirect_dma_start(
                            out=slot_x0, out_offset=bass.IndirectOffsetOnAxis(ap=row_to[par][:, t, i:i + 1], axis=0),
                            in_=x_out[par][:, t, :], in_offset=None, bounds_check=E0 * CAP - 1,
                            oob_is_err=False).then_inc(L["scattered"][par], 16)
            slots(pool, emit)

        MASK0 = 3 + 3 + 5 + 1 + 5 + 3 + 5
        LANE_RANK0, LANE_CAP, LANE_SEG0, LANE_RB0 = 0, 16, 32, 48
        LANE_RANK1, LANE_FFN, LANE_SEG1, LANE_RB1 = 64, 80, 96, 112
        LANE_STEP, LANE_TRI, LANE_BLK, LANE_IOTA = 128, 160, 224, 296
        CONST_DMAS = 16
        s_filled_rows = sem("s_filled_rows")

        wi = [arena[:, i * 2048:(i + 1) * 2048].rearrange("p (c n) -> p c n", c=CD) for i in (0, 1)]
        wo = [arena[:, 4096 + i * 2048:4096 + (i + 1) * 2048].rearrange("p (c n) -> p c n", c=I0 // P)
              for i in (0, 1)]
        xg = [arena[:, 8192 + i * 1024:8192 + (i + 1) * 1024].rearrange("p (t d) -> p t d", t=TB) for i in (0, 1)]
        xgT = arena[:, 10240:11264].rearrange("p (c n) -> p c n", c=CD)
        hT = arena[:, 11264:15360].rearrange("p (c n) -> p c n", c=I0 // P)
        yo = [arena[:, 15360 + i * 1024:15360 + (i + 1) * 1024].rearrange("p (t d) -> p t d", t=TB) for i in (0, 1)]
        b_load = [sem(f"b_load{i}") for i in range(2)]
        b_turned, b_turned_out = sem("b_turned"), sem("b_turned_out")
        b_up = sem("b_up")
        b_relu = [sem("b_relu_act"), sem("b_relu_dve")]
        b_down, b_down_out = sem("b_down"), sem("b_down_out")
        b_saved = [sem(f"b_saved{i}") for i in range(2)]
        MI = I0 // P
        up_banks = [ST[m // 2][:, (m % 2) * 512:(m % 2 + 1) * 512] for m in range(4)]
        down_banks = [shared[2], OT]

        def experts(eng, emit, pairs):
            def two(it):
                emit(it * 2, 0, it)
                emit(it * 2 + 1, 1, it)
            passes(eng, pairs, two)
            for e in range(2 * pairs, E0):
                emit(e, e % 2, e // 2)

        def b_sp(sp):
            def load(e, par):
                settle(sp)
                sp.dma_start(wi[par], a["experts_inter"][bass.ds(e * D, D), :].rearrange("(c p) n -> p c n", p=P)
                             ).then_inc(b_load[par], 16)
                sp.dma_start(wo[par], a["experts_out"][bass.ds(e * I0, I0), :].rearrange("(c p) n -> p c n", p=P)
                             ).then_inc(b_load[par], 16)
                sp.dma_start(xg[par], slot_x0[bass.ds(e * CAP, CAP), :].rearrange("(t p) d -> p t d", p=P)
                             ).then_inc(b_load[par], 16)

            sp.wait_ge(LA["oe"], NB * NG)
            for i in range(2):
                sp.wait_ge(LA["scattered"][i], NB // 2 * 16 * 2 * TB)
            load(0, 0)
            load(1, 1)

            def emit(e, par, half):
                sp.wait_ge(b_down_out, e * 2 + 2)
                settle(sp)
                sp.dma_start(slot_y0[bass.ds(e * CAP, CAP), :].rearrange("(t p) d -> p t d", p=P), yo[par]
                             ).then_inc(b_saved[par], 16)
                if not isinstance(e, int) or e + 2 < E0:
                    load(e + 2, par)
            experts(sp, emit, 2)
            sp.wait_ge(b_saved[0], 4 * 16)
            sp.wait_ge(b_saved[1], 3 * 16)

        def b_pe(pe):
            for b in range(3):
                pe.wait_ge(banks_a.free[b], banks_a.total(b))
            pe.wait_ge(LA["exp"], NB * U0)
            pe.wait_ge(LA["oe"], NB * NG)

            def emit(e, par, half):
                pe.wait_ge(b_load[par], half * 48 + 48)
                wait(pe, b_turned_out, e * CD)
                for c in range(CD):
                    for t in range(TB):
                        mm = pe.transpose(shared[c][:, t * P:(t + 1) * P], xg[par][:, t, c * P:(c + 1) * P],
                                          ident[:, :])
                    mm.then_inc(b_turned, 1)
                pe.wait_ge(b_turned_out, e * CD + CD)
                for m in range(MI):
                    wait(pe, b_relu[m % 2], e * (MI // 2) + (m // 2 - 1) if m >= 4 else e * (MI // 2))
                    for c in range(CD):
                        mm = pe.matmul(up_banks[m % 4], wi[par][:, c, m * P:(m + 1) * P], xgT[:, c, :],
                                       start=(c == 0), stop=(c == CD - 1))
                    mm.then_inc(b_up, 1)
                wait(pe, b_down_out, e * 2)
                for t in range(TB):
                    for m in range(MI):
                        if t == 0:
                            pe.wait_ge(b_relu[m % 2], e * (MI // 2) + (m // 2 + 1))
                        mm = pe.matmul(down_banks[t // 2][:, (t % 2) * D:(t % 2 + 1) * D],
                                       hT[:, m, t * P:(t + 1) * P], wo[par][:, m, :],
                                       start=(m == 0), stop=(m == MI - 1))
                    if t % 2:
                        mm.then_inc(b_down, 1)
            experts(pe, emit, 3)

        def b_act(act):
            def emit(e, par, half):
                for c in range(CD):
                    act.wait_ge(b_turned, e * CD + (c + 1))
                    act.activation(xgT[:, c, :], shared[c][:, :], ACT.Identity).then_inc(b_turned_out, 1)
                for m in range(0, MI, 2):
                    act.wait_ge(b_up, e * MI + (m + 1))
                    act.activation(hT[:, m, :], up_banks[m % 4], ACT.Relu).then_inc(b_relu[0], 1)
            experts(act, emit, 3)

        def b_dve(dve):
            def emit(e, par, half):
                for m in range(1, MI, 2):
                    dve.wait_ge(b_up, e * MI + (m + 1))
                    dve.tensor_scalar(hT[:, m, :], up_banks[m % 4], 0.0, None, ALU.max).then_inc(b_relu[1], 1)
                wait(dve, b_saved[par], half * 16)
                for i in range(2):
                    dve.wait_ge(b_down, e * 2 + (i + 1))
                    dve.tensor_copy(yo[par][:, 2 * i:2 * i + 2, :],
                                    down_banks[i][:, :].rearrange("p (t d) -> p t d", t=2)).then_inc(b_down_out, 1)
            experts(dve, emit, 3)

        LC = layer_sems("c")
        banks_c = Banks(False, LC["ready"], LC["free"], shared)
        U1 = NG * len(UNITS_FULL)
        gath = sb("gath", [P, 2 * TB, D])
        xn = sb("xn", [P, TB, D])
        c_stats = sb("c_stats", [P, TB, 6])
        c_mv = sb("c_mv", [P, TB, 2])
        combine_to = c_stats, c_mv, [small[:, i, :] for i in (8, 7, 6)]
        gate_now = [sb(f"gate_now{i}", [P, TB * 3]) for i in range(2)]
        qk_flat = [sb(f"qk_flat{i}", [P, S]) for i in range(2)]
        qk_cos = [sb("qk_cos", [P, S]), scratch]
        qk_sin = mask
        chosen1 = sb("chosen1", [P, NB, 2, TB * E1])
        row1 = sb("row1", [P, NB, 2 * TB])
        gate1 = sb("gate1", [P, NB + 1, TB * 3])
        row_from1 = sb("row_from1", [P, NB + 1, TB * 2], I32)
        s_w1, s_w1s = sem("s_w1"), sem("s_w1s")
        W1_DMAS = 8
        NORM = TB + TB + 1 + RSQRT_STEPS
        COMB_E = 3 * TB + NORM
        COMB = COMB_E + TB + TB + TB + 2 + RSQRT_STEPS + 1 + TB + 1
        MASK1 = 5 + 1 + 5 + 2 + 5
        ROUTE1 = MASK1 + 2 * 9 + 2 + 2
        ROPE = 3

        def gather_index_dve(dve, L, k, par, half, row_from, gate):
            wait(dve, L["gathered"][par], half * (16 * 2 * TB))
            dve.tensor_copy(row_now[par][:, :], row_from[:, bass.ds(k, 1), :].rearrange("p b n -> p (b n)")
                            ).then_inc(L["ga_idx"], 1)
            dve.tensor_copy(gate_now[par][:, :], gate[:, bass.ds(k, 1), :].rearrange("p b n -> p (b n)")
                            ).then_inc(L["ga_idx"], 1)

        def gather_pool(pool, L, k, par, n, table, rows, to):
            settle(pool)
            pool.indirect_dma_start(out=to[:, n, :], out_offset=None, in_=table,
                                    in_offset=bass.IndirectOffsetOnAxis(ap=row_now[par][:, n:n + 1], axis=0),
                                    bounds_check=rows - 1, oob_is_err=False).then_inc(L["gathered"][par], 16)

        def weigh_dve(dve, chain, x, x_from, rows, gates):
            for t in range(TB):
                chain.unwaited(dve.tensor_scalar(x[:, t, :], x_from[:, t, :], gates[:, 3 * t + 2:3 * t + 3], None,
                                                 ALU.mult))
                yield
            yield from chain.pause()
            for i in range(2):
                for t in range(TB):
                    chain.unwaited(dve.scalar_tensor_tensor(
                        out=x[:, t, :], in0=rows[:, 2 * t + i, :], scalar=gates[:, 3 * t + i:3 * t + i + 1],
                        in1=x[:, t, :], op0=ALU.mult, op1=ALU.add))
                    yield
                yield from chain.pause()

        def c_combine_dve(dve, L, turn):
            k, par, half = turn.batch(0)
            dve.wait_ge(L["x_load"][par], half * 16 + 16)
            dve.wait_ge(L["gathered"][par], half * (16 * 2 * TB) + 16 * 2 * TB)
            dve.wait_ge(L["ga_idx"], k * 2 + 2)
            chain = Chain(dve, L["comb"], k * COMB)
            x = x_in[par]
            yield from weigh_dve(dve, chain, x, x, gath, gate_now[par])
            yield from norm_stats_dve(dve, chain, x, combine_to)
            yield from norm_root_dve(dve, chain, combine_to)
            for t in range(TB):
                chain.unwaited(dve.tensor_scalar(x[:, t, :], x[:, t, :], c_mv[:, t, 0:1], small[:, 7, t:t + 1],
                                                 ALU.subtract, ALU.mult))
            yield from chain.pause()
            for t in range(TB):
                chain.unwaited(dve.bn_stats(c_stats[:, t, :], x[:, t, :]))
            yield from chain.pause()
            settle(dve)
            for t in range(TB):
                chain.unwaited(dve.bn_aggr(c_mv[:, t, :], c_stats[:, t, :]))
            yield from chain.pause()
            yield from chain(dve.tensor_tensor(small[:, 3, :], c_mv[:, :, 0], c_mv[:, :, 0], ALU.mult))
            yield from chain(dve.scalar_tensor_tensor(out=small[:, 3, :], in0=c_mv[:, :, 1], scalar=RMS_EPS, in1=small[:, 3, :],
                                           op0=ALU.add, op1=ALU.add))
            yield from rsqrt(dve, chain, small[:, 4, :], small[:, 3, :], small[:, 8, :])
            yield from chain(dve.tensor_tensor(small[:, 5, :], small[:, 3, :], small[:, 4, :], ALU.mult))
            for t in range(TB):
                chain.unwaited(dve.tensor_scalar(xn[:, t, :], x[:, t, :], small[:, 4, t:t + 1], None, ALU.mult))
            chain.unwaited(dve.memset(small[:, 15, :], 0.0))
            yield from chain.pause()
            assert chain.n == COMB, chain.n

        def c_sp(sp):
            L = LC

            def emit(turn):
                for step, n in schedule(False, turn.kind):
                    k, par, half = turn.batch(0)
                    if step == "xl":
                        wait(sp, L["xp"], k - 1)
                        settle(sp)
                        sp.dma_start(x_in[par][:, :, :],
                                     x1_dram[bass.ds(k * S, S), :].rearrange("(t p) d -> p t d", p=P)
                                     ).then_inc(L["x_load"][par], 16)
                    elif step == "ro":
                        order = CHUNKS.index(n)
                        wait(sp, L["stacked"][par][n % 2], half * STACK_DMAS)
                        settle(sp)
                        sp.wait_ge(L["q3"], k * 4 + (order + 1))
                        settle(sp)
                        sp.dma_start(parts[par, n // 2, :, (n % 2) * P:(n % 2 + 1) * P, :].rearrange("j p n -> p j n"),
                                     qk_src[n][:, :, :]).then_inc(L["parts_saved"], 16)
                    elif step == "st_q":
                        sp.wait_ge(L["parts_saved"], k * 64 + (32 * n + 32))
                        settle(sp)
                        wait(sp, L["exp"], (k - 1) * U1)
                        settle(sp)
                        heads = slice(n * NH // 2, (n + 1) * NH // 2)
                        for t, (i, j) in enumerate(PRODUCTS):
                            for side, part, stack in ((0, i, Q), (1, j, K)):
                                sp.dma_start(stack[par][t * HD:(t + 1) * HD, heads, :],
                                             parts[par, side, part, n * P:(n + 1) * P, :].rearrange(
                                                 "(h d) n -> d h n", d=HD)).then_inc(L["stacked"][par][n], 16)
                    elif step == "sv":
                        k, par, half = turn.batch(2)
                        sp.wait_ge(L["x_out"], k * TB + TB)
                        settle(sp)
                        sp.dma_start(x3_dram[bass.ds(k * S, S), :].rearrange("(t p) d -> p t d", p=P),
                                     x_out[par][:, :, :]).then_inc(L["x_saved"][par], 16)
            slots(sp, emit)
            for i in range(2):
                sp.wait_ge(L["x_saved"][i], NB // 2 * 16)

        def c_pe(pe):
            L, banks = LC, banks_c
            pe.wait_ge(s_w1, W1_DMAS * 16)
            pe.wait_ge(s_w1s, 2 * CD)
            pe.wait_ge(b_down_out, E0 * 2)
            pe.wait_ge(b_turned_out, E0 * CD)
            for i in range(2):
                pe.wait_ge(b_relu[i], E0 * MI // 2)

            def emit(turn):
                for step, n in schedule(False, turn.kind):
                    k, par, half = turn.batch(0)
                    if step == "xT":
                        bank, ready = banks.acquire(pe, turn, ("xT", n))
                        if n == 0:
                            pe.wait_ge(L["comb"], k * COMB + COMB)
                        for t in range(TB):
                            mm = pe.transpose(bank[:, t * P:(t + 1) * P], xn[:, t, n * P:(n + 1) * P], ident[:, :])
                        mm.then_inc(ready, 1)
                    elif step == "qk":
                        bank, ready = banks.acquire(pe, turn, ("qk", n))
                        if n == 0:
                            banks.read(pe, turn, ("xT", 0))
                            banks.read(pe, turn, ("xT", 1))
                        for c in range(CD):
                            mm = pe.matmul(bank[:, :], w_qkv[:, c, n * P:(n + 1) * P], xT[:, c, :],
                                           start=(c == 0), stop=(c == CD - 1))
                        mm.then_inc(ready, 1)
                    elif step == "ro":
                        bank, ready = banks.acquire(pe, turn, ("ro", n))
                        banks.read(pe, turn, ("qk", n))
                        pe.matmul(bank[:, :], rot[:, :], qk_flat[CHUNKS.index(n) % 2][:, :],
                                  start=True, stop=True).then_inc(ready, 1)
                    elif step == "v":
                        bank, ready = banks.acquire(pe, turn, ("v", n))
                        for t in (2 * n, 2 * n + 1):
                            for c in range(CD):
                                mm = pe.matmul(bank[:, (t % 2) * D:(t % 2 + 1) * D], xT[:, c, t * P:(t + 1) * P],
                                               w_qkv[:, c, 2 * D:3 * D], start=(c == 0), stop=(c == CD - 1))
                        mm.then_inc(ready, 1)
                    elif step in ("st", "av", "on", "oT", "y"):
                        attention_pe(pe, L, banks, False, turn, step, n, U1)
                    elif step in ("rT", "lg", "ps"):
                        route_pe(pe, L, banks, turn, step, n, NE1, ROUTE1, MASK1)
            slots(pe, emit)

        def c_act(act):
            L, banks = LC, banks_c
            act.wait_ge(s_w1, W1_DMAS * 16)

            def emit(turn):
                for step, n in schedule(False, turn.kind):
                    k, par, half = turn.batch(0)
                    if step == "xT":
                        copy_bank(act, banks, turn, ("xT", n), xT[:, n, :])
                    elif step == "qk":
                        order = CHUNKS.index(n)
                        bank, free = banks.filled(act, turn, ("qk", n))
                        wait(act, L["rope"], k * (4 * ROPE) + (ROPE * (order - 1) - 2))
                        act.activation(qk_flat[order % 2][:, :], bank[:, :], ACT.Identity,
                                       bias=b_qk[:, n:n + 1]).then_inc(free, 1)
                    elif step in ("st", "oe"):
                        attention_act(act, L, False, turn, step, n, U1, ACT.Sigmoid)
                    elif step == "oT":
                        copy_bank(act, banks, turn, ("oT", n), oT[:, n, :])
                    elif step == "rT":
                        copy_bank(act, banks, turn, ("rT", n), rT[:, n, :])
                    elif step == "ex":
                        k, par, half = turn.batch(2)
                        act.wait_ge(L["rc"], k * ROUTE1 + MASK1 - 5)
                        act.activation(r_s[:, 12, :], r_s[:, 2, :], ACT.Sigmoid, scale=-1.0).then_inc(L["ex"], 1)
                        act.activation(r_s[:, 13, :], r_s[:, 2, :], ACT.Sigmoid).then_inc(L["ex"], 1)
            slots(act, emit)

        def c_route_dve(dve, banks, turn, step):
            L, ne = LC, NE1
            k, par, half = turn.batch(2)
            oh = [r_oh[:, i, :, 0:ne] for i in range(2)]
            lg = r_lg[:, :, 0:ne]
            rank = lane[:, LANE_RANK1:LANE_RANK1 + ne]
            if step == "l1":
                chain = Chain(dve, L["rc"], k * ROUTE1)
                bank, free = banks.filled(dve, turn, ("lg", 0))
                dve.tensor_tensor(lg, bank[:, 0:TB * ne].rearrange("p (t e) -> p t e", t=TB),
                                  lanes(LANE_RB1, ne), ALU.add).then_inc(free, 1)
                yield
                banks.read(dve, turn, ("lg", 0))
                yield from first_choice(dve, chain, lg, ne, r_s[:, 4, :], rank, oh[0])
                yield from chain(dve.scalar_tensor_tensor(out=r_w[:, :, 0:ne], in0=oh[0], scalar=LOW, in1=lg,
                                               op0=ALU.mult, op1=ALU.add))
                yield from first_choice(dve, chain, r_w[:, :, 0:ne], ne, r_s[:, 5, :], rank, oh[1])
                yield from chain(dve.tensor_tensor(r_s[:, 2, :], r_s[:, 5, :], r_s[:, 4, :], ALU.subtract))
                yield from chain(dve.tensor_tensor(r_mask[:, :, 0:ne], oh[0], oh[1], ALU.add))
            elif step == "l2":
                chain = Chain(dve, L["rc"], k * ROUTE1)
                chain.n = MASK1 - 5
                yield from count_before(dve, chain, ne)
                assert chain.n == MASK1, chain.n
            elif step == "l3":
                chain = Chain(dve, L["rc"], k * ROUTE1)
                chain.n = MASK1
                bank, free = banks.filled(dve, turn, ("ps", 0))
                dve.tensor_tensor(r_pos[:, :, 0:ne], bank[:, 0:TB * ne].rearrange("p (t e) -> p t e", t=TB),
                                  lanes(LANE_SEG1, ne), ALU.add).then_inc(free, 1)
                yield
                banks.read(dve, turn, ("ps", 0))
                dve.wait_ge(L["ex"], k * 2 + 2)
                g = gate1[:, bass.ds(k, 1), :].rearrange("p b (t c) -> p (b t) c", c=3)
                rows = row1[:, bass.ds(k, 1), :].rearrange("p b (t c) -> p (b t) c", c=2)
                wait(dve, L["scattered"][par], half * (16 * 2 * TB))
                for i in range(2):
                    yield from chain(dve.tensor_tensor(oh[i], oh[i], lanes(LANE_FFN, ne), ALU.mult))
                    yield from chain(dve.tensor_reduce(r_s[:, 9, :], oh[i], AX_X, ALU.add))
                    yield from chain(dve.tensor_tensor(r_c[:, :, 0:ne], oh[i], r_pos[:, :, 0:ne], ALU.mult))
                    yield from chain(dve.tensor_reduce(r_s[:, 10, :], r_c[:, :, 0:ne], AX_X, ALU.add))
                    yield from chain(dve.tensor_tensor(g[:, :, i], r_s[:, 12 + i, :], r_s[:, 9, :], ALU.mult))
                    yield from chain(dve.tensor_copy(rows[:, :, i], r_s[:, 10, :]))
                    yield from chain(dve.tensor_scalar(r_s[:, 11, :], r_s[:, 9, :], -FAR, FAR, ALU.mult, ALU.add))
                    yield from chain(dve.tensor_tensor(row_to[par][:, :, i], r_s[:, 10, :], r_s[:, 11, :], ALU.add))
                    yield from chain(dve.tensor_copy(
                        chosen1[:, bass.ds(k, 1), i, :].rearrange("p b (t e) -> p (b t) e", e=E1),
                        oh[i][:, :, 0:E1]))
                yield from chain(dve.tensor_tensor(r_s[:, 14, :], g[:, :, 0], g[:, :, 1], ALU.add))
                yield from chain(dve.tensor_tensor(r_s[:, 15, :], r_s[:, 12, :], r_s[:, 13, :], ALU.add))
                yield from chain(dve.tensor_tensor(r_s[:, 14, :], r_s[:, 15, :], r_s[:, 14, :], ALU.subtract))
                yield from chain(dve.tensor_scalar(g[:, :, 2], r_s[:, 14, :], 1.0, None, ALU.add))
                assert chain.n == ROUTE1, chain.n

        def c_dve(dve):
            L, banks = LC, banks_c
            chains = InPieces(dict(zip(("cb", "ln", "l1", "l2", "l3"), (N_COMBINE, N_LN) + N_ROUTE[False])))
            dve.wait_ge(s_w1, W1_DMAS * 16)
            for c in range(CD):
                for side in range(2):
                    dve.tensor_scalar(w_qkv[:, c, side * D:(side + 1) * D], w_qkv[:, c, side * D:(side + 1) * D],
                                      rn_scale[:, side, c:c + 1], None, ALU.mult).then_inc(s_w1s, 1)
            dve.memset(r_before[:, TB, :], 0.0).then_inc(s_fill2, 1)
            dve.memset(row_from1[:, NB, :], 0).then_inc(s_fill2, 1)
            dve.memset(gate1[:, NB, :], 0.0).then_inc(s_fill2, 1)
            dve.wait_ge(s_fill2, 4)
            gather_index_dve(dve, L, 0, 0, 0, row_from0, gate0)

            def emit(turn):
                for step, n in schedule(False, turn.kind):
                    k, par, half = turn.batch(0)
                    if step == "gi":
                        k, par, half = turn.batch(-1)
                        gather_index_dve(dve, L, k, par, half, row_from0, gate0)
                    elif step == "cb":
                        chains.piece(step, n, lambda: c_combine_dve(dve, L, turn))
                    elif step == "ro":
                        order = CHUNKS.index(n)
                        bank, free = banks.filled(dve, turn, ("ro", n))
                        rest = qk_rest[order % 2]
                        chain = Chain(dve, L["rope"], k * (4 * ROPE))
                        chain.n = order * ROPE
                        dve.tensor_tensor(qk_sin[:, :], bank[:, :], sin_t[:, :], ALU.mult).then_inc(free, 1)
                        banks.read(dve, turn, ("ro", n))
                        dve.wait_ge(L["qf"], k * 4 + (order + 1))
                        wait(dve, L["q3"], k * 4 + (order - 1))
                        chain.step(dve.tensor_tensor(rest[:, :], qk_cos[order % 2][:, :], qk_sin[:, :], ALU.add))
                        wait(dve, L["parts_saved"], k * 64)
                        chain.step(dve.tensor_copy(qk_src[n][:, 0, :], rest[:, :]))
                        chain.step(dve.tensor_tensor(rest[:, :], rest[:, :], qk_src[n][:, 0, :], ALU.subtract))
                        dve.tensor_copy(qk_src[n][:, 1, :], rest[:, :]).then_inc(L["q2"], 1)
                    elif step == "v":
                        bank, free = banks.filled(dve, turn, ("v", n))
                        wait(dve, L["av"], (k - 1) * U1)
                        dve.wait_ge(L["comb"], k * COMB + COMB)
                        for t in (2 * n, 2 * n + 1):
                            v = dve.scalar_tensor_tensor(
                                out=v_aug[par][:, t, :, 0:HD],
                                in0=bank[:, (t % 2) * D:(t % 2 + 1) * D].rearrange("p (h d) -> p h d", h=NH),
                                scalar=small[:, 5, t:t + 1], in1=b_v[:, :].rearrange("p (h d) -> p h d", h=NH),
                                op0=ALU.mult, op1=ALU.add)
                        v.then_inc(free, 1)
                    elif step in ("on", "y"):
                        attention_dve(dve, L, banks, turn, step, n, SUM_EPS)
                    elif step == "ln":
                        chains.piece(step, n, lambda: finish_dve(dve, L, banks, turn))
                    elif step in ("l1", "l2", "l3"):
                        chains.piece(step, n, lambda: c_route_dve(dve, banks, turn, step))
            slots(dve, emit)

        def c_pool(pool):
            L = LC
            pool.wait_ge(s_w1, W1_DMAS * 16)
            pool.wait_ge(L["ga_idx"], 2)
            pool.wait_ge(b_saved[0], 4 * 16)
            pool.wait_ge(b_saved[1], 3 * 16)
            for n in range(2 * TB):
                gather_pool(pool, L, 0, 0, n, slot_y0, E0 * CAP, gath)

            def emit(turn):
                for step, n in schedule(False, turn.kind):
                    k, par, half = turn.batch(0)
                    if step == "ga":
                        k, par, half = turn.batch(-1)
                        if n == 0:
                            pool.wait_ge(L["ga_idx"], k * 2 + 2)
                            pool.wait_ge(L["comb"], (k - 1) * COMB + 3 * TB)
                        gather_pool(pool, L, k, par, n, slot_y0, E0 * CAP, gath)
                    elif step == "ro":
                        order = CHUNKS.index(n)
                        banks_c.read(pool, turn, ("qk", n))
                        wait(pool, L["rope"], k * (4 * ROPE) + (ROPE * (order - 1) - 2))
                        pool.tensor_tensor(out=qk_cos[order % 2][:, :], in0=qk_flat[order % 2][:, :],
                                           in1=cos_t[:, :], op=ALU.mult).then_inc(L["qf"], 1)
                        pool.wait_ge(L["q2"], k * 4 + (order + 1))
                        pool.tensor_tensor(out=qk_src[n][:, 2, :], in0=qk_rest[order % 2][:, :],
                                           in1=qk_src[n][:, 1, :], op=ALU.subtract).then_inc(L["q3"], 1)
                    elif step == "xp":
                        k, par, half = turn.batch(1)
                        pool.wait_ge(L["comb"], k * COMB + COMB)
                        wait(pool, L["x_out"], k * TB)
                        pool.tensor_tensor(out=x_res[:, :, :], in0=x_in[par][:, :, :],
                                           in1=b_o[:, :].unsqueeze(1).broadcast_to([P, TB, D]),
                                           op=ALU.add).then_inc(L["xp"], 1)
                    elif step == "sc":
                        k, par, half = turn.batch(2)
                        if n == 0:
                            pool.wait_ge(L["rc"], k * ROUTE1 + ROUTE1)
                            settle(pool)
                        t, i = n // 2, n % 2
                        pool.indirect_dma_start(
                            out=slot_x1, out_offset=bass.IndirectOffsetOnAxis(ap=row_to[par][:, t, i:i + 1], axis=0),
                            in_=x_out[par][:, t, :], in_offset=None, bounds_check=ZROW - 1,
                            oob_is_err=False).then_inc(L["scattered"][par], 16)
            slots(pool, emit)

        w1t = arena[:, 0:8192]
        w2t = arena[:, 8192:16384]
        free_at = [16384]

        def carve(n):
            free_at[0] += n
            return arena[:, free_at[0] - n:free_at[0]]

        RX = 4
        bx = [gath[:, i, :] for i in range(RX)]
        bxT = [carve(D) for _ in range(2)]
        bh = [carve(F1) for _ in range(2)]
        bhT = [carve(F1) for _ in range(2)]
        by = [carve(D) for _ in range(2)]
        KF = F1 // P
        t_tab = sb("t_tab", [1, 2, NBLK], I32)
        t_cnt = sb("t_cnt", [P, E1])
        t_a = carve(E1 * 32).rearrange("p (e n) -> p e n", e=E1)
        t_nb = sb("t_nb", [P, E1])
        t_tri = carve(E1 * E1).rearrange("p (a b) -> p a b", a=E1)
        t_start = sb("t_start", [P, E1])
        t_end = sb("t_end", [P, E1])
        t_delta = sb("t_delta", [P, E1])
        t_rowf = carve(2 * TB * NB)
        t_pad = sb("t_pad", [P, E1], I32)
        t_b8 = carve(NBLK * E1)[0:1, :].rearrange("p (b e) -> p b e", e=E1)
        t_b8b = carve(NBLK * E1)[0:1, :].rearrange("p (b e) -> p b e", e=E1)
        t_bf = sb("t_bf", [1, 6, NBLK])
        d_cnt, d_chain, d_tab = sem("d_counts"), sem("d_chain"), sem("d_tables")
        d_w = sem("d_weights")
        d_pad = sem("d_padded")
        d_zero = sem("d_zero_rows")
        d_load = [sem(f"d_load{i}") for i in range(RX)]
        d_saved = [sem(f"d_saved{i}") for i in range(2)]
        d_t, d_tout, d_up, d_h, d_ht, d_htout, d_y, d_yout = (
            sem(x) for x in ("d_turned", "d_turned_out", "d_up", "d_hidden", "d_hidden_turned", "d_hidden_out",
                             "d_down", "d_down_out"))
        D_CHAIN = 25

        def tables_dve(dve):
            chain = Chain(dve, d_chain, 0)
            dve.wait_ge(d_cnt, 1)
            yield from chain(dve.tensor_copy(t_cnt[:, :], shared[0][:, 0:E1]))
            yield from chain(dve.tensor_tensor(t_a[:, :, :], spread(t_cnt[:, :], 32),
                                    lane[:, LANE_STEP:LANE_STEP + 32].unsqueeze(1).broadcast_to([P, E1, 32]),
                                    ALU.is_gt))
            yield from chain(dve.tensor_reduce(t_nb[:, :], t_a[:, :, :], AX_X, ALU.add))
            yield from chain(dve.tensor_tensor(t_tri[:, :, :], t_nb[:, :].unsqueeze(1).broadcast_to([P, E1, E1]),
                                    lane[:, LANE_TRI:LANE_TRI + 64].rearrange("p (a b) -> p a b", a=E1), ALU.mult))
            yield from chain(dve.tensor_reduce(t_start[:, :], t_tri[:, :, :], AX_X, ALU.add))
            yield from chain(dve.tensor_tensor(t_end[:, :], t_start[:, :], t_nb[:, :], ALU.add))
            yield from chain(dve.scalar_tensor_tensor(out=t_delta[:, :], in0=t_start[:, :], scalar=float(P),
                                           in1=lane[:, LANE_SEG1:LANE_SEG1 + E1], op0=ALU.mult, op1=ALU.subtract))
            seg = lane[:, LANE_SEG1:LANE_SEG1 + E1]
            yield from chain(dve.tensor_tensor(t_start[:, :], t_cnt[:, :], seg, ALU.add))
            yield from chain(dve.tensor_scalar(t_pad[:, :], t_start[:, :], lane[:, LANE_IOTA:LANE_IOTA + 1], None, ALU.add))
            blk = lane[0:1, LANE_BLK:LANE_BLK + NBLK]
            yield from chain(dve.tensor_tensor(t_b8[:, :, :], spread(blk, E1),
                                    t_end[0:1, :].unsqueeze(1).broadcast_to([1, NBLK, E1]), ALU.is_ge))
            yield from chain(dve.tensor_reduce(t_bf[:, 0, :], t_b8[:, :, :], AX_X, ALU.add))
            yield from chain(dve.tensor_tensor(t_b8[:, :, :], spread(t_bf[:, 0, :], E1),
                                    lane[0:1, LANE_BLK:LANE_BLK + E1].unsqueeze(1).broadcast_to([1, NBLK, E1]),
                                    ALU.is_equal))
            yield from chain(dve.tensor_tensor(t_b8b[:, :, :], t_b8[:, :, :],
                                    t_delta[0:1, :].unsqueeze(1).broadcast_to([1, NBLK, E1]), ALU.mult))
            yield from chain(dve.tensor_reduce(t_bf[:, 1, :], t_b8b[:, :, :], AX_X, ALU.add))
            yield from chain(dve.tensor_reduce(t_bf[:, 2, :], t_b8[:, :, :], AX_X, ALU.add))
            yield from chain(dve.scalar_tensor_tensor(out=t_bf[:, 3, :], in0=blk, scalar=float(P), in1=t_bf[:, 1, :],
                                           op0=ALU.mult, op1=ALU.subtract))
            yield from chain(dve.tensor_tensor(t_bf[:, 3, :], t_bf[:, 3, :], t_bf[:, 2, :], ALU.mult))
            yield from chain(dve.tensor_scalar(t_bf[:, 4, :], t_bf[:, 2, :], -float(ZROW), float(ZROW), ALU.mult, ALU.add))
            yield from chain(dve.tensor_tensor(t_tab[:, 0, :], t_bf[:, 3, :], t_bf[:, 4, :], ALU.add))
            yield from chain(dve.tensor_scalar(t_bf[:, 5, :], t_bf[:, 0, :], float(E1 - 1), None, ALU.min))
            yield from chain(dve.tensor_copy(t_tab[:, 1, :], t_bf[:, 5, :]))
            c2 = chosen1[:, :, :, :].rearrange("p b i (t e) -> p (b i t) e", e=E1)
            yield from chain(dve.tensor_tensor(c2, c2, t_delta[:, :].unsqueeze(1).broadcast_to([P, 2 * TB * NB, E1]), ALU.mult))
            yield from chain(dve.tensor_reduce(t_rowf[:, :], c2, AX_X, ALU.add))
            for i in range(2):
                yield from chain(dve.tensor_tensor(
                    row_from1[:, 0:NB, :].rearrange("p b (t c) -> p b t c", c=2)[:, :, :, i],
                    row1[:, :, :].rearrange("p b (t c) -> p b t c", c=2)[:, :, :, i],
                    t_rowf[:, :].rearrange("p (b i t) -> p b i t", i=2, t=TB)[:, :, i, :], ALU.add))
            assert chain.n == D_CHAIN, chain.n

        def d_sp(sp):
            sp.wait_ge(LC["oe"], NB * NG)
            for e in range(E1):
                sp.dma_start(w1t[:, e * 1024:(e + 1) * 1024].rearrange("p (c n) -> p c n", c=CD),
                             a["w1T"][e * D:(e + 1) * D, :].rearrange("(c p) n -> p c n", p=P)).then_inc(d_w, 16)
                sp.dma_start(w2t[:, e * 1024:(e + 1) * 1024].rearrange("p (c n) -> p c n", c=KF),
                             a["w2T"][e * F1:(e + 1) * F1, :].rearrange("(c p) n -> p c n", p=P)).then_inc(d_w, 16)
            sp.wait_ge(d_chain, 21)
            for i in range(2):
                sp.wait_ge(LC["scattered"][i], NB // 2 * 16 * 2 * TB)
                sp.wait_ge(LC["gathered"][i], (NB // 2 + 1 - i) * 16 * 2 * TB)
            sp.wait_ge(d_pad, 16 * E1)
            sp.wait_ge(d_zero, 16)

            def load(j, buffer):
                row = sp.value_load(t_tab[0:1, 0, bass.ds(j, 1)], min_val=0, max_val=ZROW)
                sp.dma_start(bx[buffer], slot_x1[bass.ds(row, P), :]).then_inc(d_load[buffer], 16)

            for j in range(RX):
                load(j, j)

            def step(j, buffer, more):
                if more:
                    sp.wait_ge(d_t, j + 1)
                    settle(sp)
                    load(j + RX, buffer)
                sp.wait_ge(d_yout, j + 1)
                settle(sp)
                sp.dma_start(slot_y1[bass.ds(j * P, P), :], by[buffer % 2]).then_inc(d_saved[buffer % 2], 16)

            with sp.Fori(0, NBLK // RX - 1) as it:
                for i in range(RX):
                    step(it * RX + i, i, True)
            for i in range(RX):
                step(NBLK - RX + i, i, False)
            for i in range(2):
                sp.wait_ge(d_saved[i], NBLK // 2 * 16)

        T_BANK = shared[0]
        UP = [ST[0][:, 0:512], ST[0][:, 512:1024]]
        HT_BANK = [ST[1][:, 0:512], ST[1][:, 512:1024]]
        Y_BANK = [shared[1], shared[2]]

        def d_pe(pe):
            for b in range(3):
                pe.wait_ge(banks_c.free[b], banks_c.total(b))
            pe.wait_ge(LC["rc"], NB * ROUTE1)
            pe.wait_ge(LC["exp"], NB * U1)
            pe.wait_ge(LC["oe"], NB * NG)
            pe.matmul(shared[0][:, 0:E1], ones_b[:, :], r_before[:, TB, 0:E1], start=True, stop=True
                      ).then_inc(d_cnt, 1)
            pe.wait_ge(d_chain, 21)
            pe.wait_ge(d_w, 2 * E1 * 16)

            def turn_rows(j, buffer, turns):
                wait(pe, d_tout, j)
                pe.wait_ge(d_load[buffer], turns * 16 + 16)
                for c in range(CD):
                    mm = pe.transpose(T_BANK[:, c * P:(c + 1) * P], bx[buffer][:, c * P:(c + 1) * P], ident[:, :])
                mm.then_inc(d_t, 1)

            def up(j, par):
                e = pe.value_load(t_tab[0:1, 1, bass.ds(j, 1)], min_val=0, max_val=E1 - 1)
                pe.wait_ge(d_tout, j + 1)
                for c in range(CD):
                    mm = pe.matmul(UP[par], bxT[par][:, c * P:(c + 1) * P],
                                   w1t[:, bass.ds(e * 1024 + c * F1, F1)], start=(c == 0), stop=(c == CD - 1))
                mm.then_inc(d_up, 1)

            def turn_hidden(j, par):
                pe.wait_ge(d_h, j + 1)
                for c in range(KF):
                    mm = pe.transpose(HT_BANK[par][:, c * P:(c + 1) * P], bh[par][:, c * P:(c + 1) * P],
                                      ident[:, :])
                mm.then_inc(d_ht, 1)

            def down(j, par, clear):
                e = pe.value_load(t_tab[0:1, 1, bass.ds(j, 1)], min_val=0, max_val=E1 - 1)
                pe.wait_ge(d_htout, j + 1)
                if clear is not None:
                    pe.wait_ge(d_yout, clear)
                for c in range(KF):
                    mm = pe.matmul(Y_BANK[par][:, 0:D], bhT[par][:, c * P:(c + 1) * P],
                                   w2t[:, bass.ds(e * 1024 + c * D, D)], start=(c == 0), stop=(c == KF - 1))
                mm.then_inc(d_y, 1)

            turn_rows(0, 0, 0)
            up(0, 0)
            turn_rows(1, 1, 0)
            turn_hidden(0, 0)
            up(1, 1)
            turn_rows(2, 2, 0)
            down(0, 0, None)
            with pe.Fori(0, NBLK // RX - 1) as it:
                for j0 in range(1, RX + 1):
                    par = j0 % 2
                    j = it * RX + j0
                    turn_hidden(j, par)
                    up(j + 1, 1 - par)
                    turn_rows(j + 2, (j0 + 2) % RX, it + (j0 + 2) // RX)
                    down(j, par, j - 1)
            for j in range(NBLK - 3, NBLK):
                turn_hidden(j, j % 2)
                if j + 1 < NBLK:
                    up(j + 1, (j + 1) % 2)
                if j + 2 < NBLK:
                    turn_rows(j + 2, (j + 2) % RX, (j + 2) // RX)
                down(j, j % 2, j - 1)

        def d_act(act):
            act.wait_ge(d_up, 1)
            act.activation(bh[0], UP[0], ACT.Silu).then_inc(d_h, 1)

            def emit_lag(j, par, half, last=False):
                if not last:
                    act.wait_ge(d_up, j + 2)
                    act.activation(bh[1 - par], UP[1 - par], ACT.Silu).then_inc(d_h, 1)
                act.wait_ge(d_y, j + 1)
                wait(act, d_saved[par], half * 16)
                act.activation(by[par], Y_BANK[par][:, 0:D], ACT.Identity).then_inc(d_yout, 1)
            def two(it):
                emit_lag(it * 2, 0, it)
                emit_lag(it * 2 + 1, 1, it)
            passes(act, NBLK // 2 - 1, two)
            emit_lag(NBLK - 2, 0, NBLK // 2 - 1)
            emit_lag(NBLK - 1, 1, NBLK // 2 - 1, True)

        def d_dve(dve):
            all_of(tables_dve(dve))

            def rows_out(j, par):
                dve.wait_ge(d_t, j + 1)
                dve.tensor_copy(bxT[par], T_BANK[:, 0:D]).then_inc(d_tout, 1)

            def hidden_out(j, par):
                dve.wait_ge(d_ht, j + 1)
                dve.tensor_copy(bhT[par], HT_BANK[par]).then_inc(d_htout, 1)

            rows_out(0, 0)
            rows_out(1, 1)
            with dve.Fori(0, NBLK // 2 - 1) as it:
                for par in range(2):
                    hidden_out(it * 2 + par, par)
                    rows_out(it * 2 + par + 2, par)
            hidden_out(NBLK - 2, 0)
            hidden_out(NBLK - 1, 1)

        def d_pool(pool):
            pool.wait_ge(d_chain, 9)
            pool.wait_ge(s_zero, 1)
            for e in range(E1):
                pool.indirect_dma_start(out=slot_x1,
                                        out_offset=bass.IndirectOffsetOnAxis(ap=t_pad[:, e:e + 1], axis=0),
                                        in_=zero[:, :], in_offset=None, bounds_check=ZROW + P - 1,
                                        oob_is_err=False).then_inc(d_pad, 16)

        LE = dict(gathered=[sem(f"e_gathered{i}") for i in range(2)], ga_idx=sem("e_rows_known"),
                  comb=[sem(f"e_combine_chain{i}") for i in range(2)], x_load=[sem(f"e_load{i}") for i in range(2)],
                  out=[sem(f"e_out{i}") for i in range(2)], done=sem("e_rows_done"))
        weighed = [y_b, x_res]
        egath = [arena[:, i * 2048:(i + 1) * 2048].rearrange("p (n d) -> p n d", n=2 * TB) for i in (0, 1)]

        def pairs(eng, emit):
            def two(it):
                emit(it * 2, 0, it)
                emit(it * 2 + 1, 1, it)
            passes(eng, NB // 2, two)

        def e_sp(sp):
            def load(k, par):
                settle(sp)
                sp.dma_start(x_in[par][:, :, :], x3_dram[bass.ds(k * S, S), :].rearrange("(t p) d -> p t d", p=P)
                             ).then_inc(LE["x_load"][par], 16)
            sp.wait_ge(LC["xp"], NB)
            load(0, 0)
            load(1, 1)

            def save(k, par):
                sp.wait_ge(LE["done"], k * TB + TB)
                settle(sp)
                sp.dma_start(out[bass.ds(k * S, S), :].rearrange("(t p) d -> p t d", p=P), x_out[par][:, :, :]
                             ).then_inc(LE["out"][par], 16)

            def two(it):
                for par in range(2):
                    sp.wait_ge(LE["comb"][par], it * COMB_E + TB)
                    load(it * 2 + par + 2, par)
                    if not isinstance(it, int) or par:
                        save(it * 2 + par - 1, 1 - par)
            passes(sp, NB // 2 - 1, two)
            for k in range(NB - 3, NB):
                save(k, k % 2)
            for i in range(2):
                sp.wait_ge(LE["out"][i], NB // 2 * 16)

        def e_dve(dve):
            for i in range(2):
                dve.wait_ge(LC["x_saved"][i], NB // 2 * 16)
                dve.wait_ge(LC["scattered"][i], NB // 2 * 16 * 2 * TB)

            to = norm_to, combine_to

            def total(k, par, half):
                dve.wait_ge(LE["x_load"][par], half * 16 + 16)
                dve.wait_ge(LE["gathered"][par], half * (16 * 2 * TB) + 16 * 2 * TB)
                dve.wait_ge(LE["ga_idx"], k * 2 + 2)
                chain = Chain(dve, LE["comb"][par], half * COMB_E)
                yield from weigh_dve(dve, chain, weighed[par], x_in[par], egath[par], gate_now[par])
                if not isinstance(k, int) or k + 2 <= NB:
                    gather_index_dve(dve, LE, k + 2, par, half + 1, row_from1, gate1)
                yield from norm_stats_dve(dve, chain, weighed[par], to[par])
                assert chain.n == COMB_E - 1 - RSQRT_STEPS

            def rows(k, par, half):
                chain = Chain(dve, LE["comb"][par], half * COMB_E)
                chain.n = COMB_E - 1 - RSQRT_STEPS
                yield from norm_root_dve(dve, chain, to[par])
                assert chain.n == COMB_E
                wait(dve, LE["out"][par], half * 16)
                _, mv, (_, root, _) = to[par]
                for t in range(TB):
                    dve.tensor_scalar(x_out[par][:, t, :], weighed[par][:, t, :], mv[:, t, 0:1], root[:, t:t + 1],
                                      ALU.subtract, ALU.mult).then_inc(LE["done"], 1)
                    yield

            for k in range(2):
                gather_index_dve(dve, LE, k, k, 0, row_from1, gate1)
            all_of(total(0, 0, 0))

            def two(it):
                together(total(it * 2 + 1, 1, it), rows(it * 2, 0, it), 1)
                together(total(it * 2 + 2, 0, it + 1), rows(it * 2 + 1, 1, it), 1)
            passes(dve, NB // 2 - 1, two)
            together(total(NB - 1, 1, NB // 2 - 1), rows(NB - 2, 0, NB // 2 - 1), 1)
            all_of(rows(NB - 1, 1, NB // 2 - 1))

        def e_pool(pool):
            for i in range(2):
                pool.wait_ge(d_saved[i], NBLK // 2 * 16)

            def emit(k, par, half):
                pool.wait_ge(LE["ga_idx"], k * 2 + 2)
                wait(pool, LE["comb"][par], half * COMB_E - (COMB_E - 3 * TB))
                for n in range(2 * TB):
                    gather_pool(pool, LE, k, par, n, slot_y1, NBLK * P, egath[par])
            pairs(pool, emit)

        @block.sync
        def _(sp):
            for dst, src in (
                (ident[:, :], a["c_ident"]), (scratch[:, 0:P], a["c_before"]), (mask[:, :], a["c_mask"]),
                (lane[:, 0:48], a["c_lane"][:, 0:48]), (lane[:, 64:112], a["c_lane"][:, 64:112]),
                (lane[:, 128:304], a["c_lane"][:, 128:304]), (rot[:, :], a["c_rot"]),
                (cos_t[:, :], a["c_cos"]), (sin_t[:, :], a["c_sin"]),
                (lane[:, LANE_RB0:LANE_RB0 + NE0], a["router_b"].partition_broadcast(P)),
                (w_qkv[:, :, :], a["w_qkv"].rearrange("(c p) n -> p c n", p=P)),
                (w_o[:, :, :], a["w_out"].rearrange("(c p) n -> p c n", p=P)),
                (w_r[:, :, 0:NE0], a["router_wT"].rearrange("(c p) n -> p c n", p=P)),
                (b_qk[:, :], a["b_qk_cols"]),
                (b_v[:, :], a["b_qkv"][2 * D:3 * D].partition_broadcast(P)),
                (b_o[:, :], a["b_out"].partition_broadcast(P)),
            ):
                sp.dma_start(dst, src).then_inc(s_const, 16)
            sp.wait_ge(s_zero, 1)
            sp.dma_start(slot_x0.rearrange("(a p) d -> p a d", p=P),
                         zero[:, :].unsqueeze(1).broadcast_to([P, E0 * CAP // P, D])).then_inc(s_filled_rows, 16)
            sp.dma_start(slot_x1[ZROW:ZROW + P, :], zero[:, :]).then_inc(d_zero, 16)
            a_sp(sp)
            for i in range(2):
                sp.wait_ge(LA["x_saved"][i], NB // 2 * 16)
            sp.wait_ge(LA["rc"], NB * ROUTE0)
            for dst, src in (
                (w_qkv[:, :, :], a["w_qkv1T"].rearrange("(c p) n -> p c n", p=P)),
                (w_o[:, :, :], a["w_o1T"].rearrange("(c p) n -> p c n", p=P)),
                (w_r[:, :, :], a["gate_wT"].rearrange("(c p) n -> p c n", p=P)),
                (b_qk[:, :], a["b_qk_cols1"]), (rn_scale[:, :, :], a["rn_cols"]),
                (b_v[:, :], a["b_v1"].partition_broadcast(P)),
                (b_o[:, :], a["b_o1"].partition_broadcast(P)),
                (lane[:, LANE_RB1:LANE_RB1 + NE1], a["expert_bias"].partition_broadcast(P)),
            ):
                sp.dma_start(dst, src).then_inc(s_w1, 16)
            b_sp(sp)
            c_sp(sp)
            d_sp(sp)
            e_sp(sp)

        @block.tensor
        def _(pe):
            a_pe(pe)
            b_pe(pe)
            c_pe(pe)
            d_pe(pe)

        @block.scalar
        def _(act):
            a_act(act)
            b_act(act)
            c_act(act)
            d_act(act)

        @block.vector
        def _(dve):
            a_dve(dve)
            b_dve(dve)
            c_dve(dve)
            d_dve(dve)
            e_dve(dve)

        @block.gpsimd
        def _(pool):
            a_pool(pool)
            c_pool(pool)
            d_pool(pool)
            e_pool(pool)


def shape_constants():
    lane = np.zeros((P, 304), np.float32)
    lane[:, 0:NE0] = NE0 - np.arange(NE0)
    lane[:, 16:16 + E0] = CAP
    lane[:, 32:32 + NE0] = CAP * np.arange(NE0)
    lane[:, 64:64 + NE1] = NE1 - np.arange(NE1)
    lane[:, 80:80 + E1] = 1.0
    lane[:, 96:96 + E1] = SEG * np.arange(E1)
    lane[:, 128:160] = P * np.arange(32)
    lane[:, 160:224] = np.tril(np.ones((E1, E1), np.float32), -1).ravel()
    lane[:, 224:224 + NBLK] = np.arange(NBLK)
    lane[:, 296] = np.arange(P)
    mask = np.zeros((P, S), np.float32)
    mask[:, 0:P] = np.where(np.arange(P)[None, :] >= np.arange(P)[:, None], 0.0, LOW)
    inv = (np.float32(1.0) / np.float32(10000.0) ** (np.arange(0, HD, 2, dtype=np.float32) / np.float32(HD)))
    freqs = np.arange(S, dtype=np.float32)[:, None] * inv.astype(np.float32)[None, :]
    emb = np.concatenate([freqs, freqs], axis=-1)
    cos = np.tile(np.cos(emb).astype(np.float32).T, (P // HD, 1))
    sin = np.tile(np.sin(emb).astype(np.float32).T, (P // HD, 1))
    rot = np.zeros((P, P), np.float32)
    for i in range(0, P, 2):
        rot[i + 1, i] = -1.0
        rot[i, i + 1] = 1.0
    return {
        "c_ident": np.eye(P, dtype=np.float32), "c_before": np.triu(np.ones((P, P), np.float32), 1),
        "c_mask": mask, "c_lane": lane, "c_rot": rot, "c_cos": cos, "c_sin": sin,
    }


def laid_out(i):
    c = np.ascontiguousarray
    i = {k: np.asarray(v) for k, v in i.items()}
    cols = lambda v, n: c(v.reshape(n, P).T)
    return {
        "x": c(i["L0_attn_x"].reshape(NTOK, D)),
        "w_qkv": c(i["L0_attn_w_qkv"]), "b_qkv": c(i["L0_attn_b_qkv"]),
        "b_qk_cols": cols(i["L0_attn_b_qkv"][0:2 * D], 4),
        "w_out": c(i["L0_attn_w_out"]), "b_out": c(i["L0_attn_b_out"]),
        "router_wT": c(i["L0_ffn_router_w"].T), "router_b": c(i["L0_ffn_router_b"]),
        "experts_inter": c(i["L0_ffn_experts_inter"].reshape(E0 * D, I0)),
        "experts_out": c(i["L0_ffn_experts_out"].reshape(E0 * I0, D)),
        "w_qkv1T": c(np.concatenate([i["L1_attn_q_w"].T, i["L1_attn_k_w"].T, i["L1_attn_v_w"].T], axis=1)),
        "w_o1T": c(i["L1_attn_o_w"].T),
        "b_qk_cols1": c(np.concatenate([cols(i["L1_attn_q_b"], 2), cols(i["L1_attn_k_b"], 2)], axis=1)),
        "b_v1": c(i["L1_attn_v_b"]), "b_o1": c(i["L1_attn_o_b"]),
        "rn_cols": c(np.stack([cols(i["L1_attn_qn_scale"], 2), cols(i["L1_attn_kn_scale"], 2)], axis=1)),
        "gate_wT": c(i["L1_ffn_gate_w"].T), "expert_bias": c(i["L1_ffn_expert_bias"]),
        "w1T": c(i["L1_ffn_w1"].transpose(0, 2, 1).reshape(E1 * D, F1)),
        "w2T": c(i["L1_ffn_w2"].transpose(0, 2, 1).reshape(E1 * F1, D)),
    }


def kernel(**inputs):
    import concourse.bacc as bacc
    from concourse.bass_utils import run_bass_kernel_spmd

    nc = bacc.Bacc("TRN2", target_bir_lowering=False, num_devices=1)
    arrays = {f"in_{k}": v for k, v in {**laid_out(inputs), **shape_constants()}.items()}
    a = {k[3:]: nc.dram_tensor(k, v.shape, mybir.dt.from_np(v.dtype), kind="ExternalInput").ap()
         for k, v in arrays.items()}
    out = nc.dram_tensor("out_rows", (NTOK, D), F32, kind="ExternalOutput").ap()
    build(nc, a, out)
    r = run_bass_kernel_spmd(nc, [arrays], core_ids=[0])
    return r.results[0]["out_rows"].reshape(NB, S, D)
```

```python
from contextlib import ExitStack

import numpy as np

import concourse.bass as bass
from concourse import mybir

F32 = mybir.dt.float32
BF16 = mybir.dt.bfloat16
I32 = mybir.dt.int32
ALU = mybir.AluOpType
ACT = mybir.ActivationFunctionType
AX_X = mybir.AxisListType.X

P = 128
NB, S, D = 8, 512, 256
NH, HD = 16, 16
TB = S // P
CD = D // P
GH = 4
NG = NH // GH
E0, I0, CAP = 7, 1024, 512
NE0 = E0 + 1
E1, F1, NE1 = 8, 512, 12
NTOK = NB * S
SEG = NTOK + P
ZROW = E1 * SEG
NBLK = 2 * NTOK // P + E1
LN_EPS, RMS_EPS, SUM_EPS = 1e-5, 1e-8, 1e-8
ATT_SCALE = 0.25
FAR = float(1 << 20)
LOW = -3.0e38
NPROD = 6
SK = NPROD * HD
STACK_DMAS = 2 * NPROD * 16
RING = 4
RSQRT_MAGIC = 1597463007.0

PRODUCTS = [(0, 0), (0, 1), (1, 0), (1, 1), (0, 2), (2, 0)]

FILLS = [
    [(0, 0, 0)],
    [(0, 1, 0), (0, 3, 384)],
    [(0, 2, 0), (1, 2, 256)],
    [(1, 0, 0)],
    [(1, 1, 0), (1, 3, 384)],
]
N_MX = NH // 2 * len(FILLS)
HALF_MX = N_MX // 2

UNITS_CAUSAL = [
    [(3, 0, 256, 0)],
    [(2, 0, 256, 0)],
    [(1, 0, 256, 0)],
    [(3, 256, 256, 0)],
    [(0, 0, 128, 0), (2, 256, 128, 128)],
]
UNITS_FULL = [[(kb, qh * 256, 256, 0)] for qh in range(2) for kb in range(TB)]
DIAGONAL = {2: (128, 1), 3: (128, 1), 4: (0, 2)}


def wait(eng, sem, value):
    if isinstance(value, int) and value <= 0:
        return
    eng.wait_ge(sem, value)


class Turn:

    def __init__(self, kind, s, it=None):
        self.kind, self.s, self.it = kind, s, it

    def batch(self, d):
        if self.it is None:
            k = self.s - d
            return k, k % 2, k // 2
        k = self.s - d
        return self.it * 2 + k, k % 2, (self.it + (k // 2) if k // 2 else self.it)


def passes(eng, n, one):
    one(0)
    with eng.Fori(1, n) as it:
        one(it)


CHUNKS = (0, 2, 1, 3)

AHEAD = {True: ("xl", "xT", "qk", "qs", "st_q"), False: ("xl", "gi", "ga", "cb")}

KINDS = ("zeroth", "first", "second", "body", "eighth", "ninth")


def slots(eng, emit):
    emit(Turn("zeroth", -1))
    emit(Turn("first", 0))
    emit(Turn("second", 1))

    def two(it):
        emit(Turn("body", 2, it))
        emit(Turn("body", 3, it))
    passes(eng, (NB - 2) // 2, two)
    emit(Turn("eighth", NB))
    emit(Turn("ninth", NB + 1))


COST = {
    True: dict(xT=0.5, qk=0.2, y=0.1, v=0.8, oT=0.5, ln=0.05,
               l1=0.05, l2=0.05, l3=0.05, mx=1.2, mr=0.0),
    False: dict(xT=0.5, late=1, qk=0.8, ro=1.5, v=1.7, y=0.9, ln=0.25,
                cb=0.5, l1=0.1, l2=0.1, l3=0.1),
}
N_LN = 23
N_COMBINE = 64
N_ROUTE = {True: (3, 22, 20), False: (13, 5, 22)}


SPACE = ("space", 0)
SPACES = {True: (4, 2, 2, 0, 4), False: (4, 2, 4, 2, 4)}
NORM_FIRST, MAXIMA_LAST, PROJECT_BETWEEN = 12, 4, 10
LATE = ("late", 0)
N_LATE = dict(first=0, second=22)
PROJECT_FIRST = dict(first=12, second=3)


def pieces(step, n):
    return [(step, i) for i in range(n)]


def mixed(a, b):
    if not a:
        return list(b)
    out, at = [], 0
    for i, step in enumerate(a):
        out.append(step)
        if step[0] in ("lg", "ps") and i + 1 < len(a):
            continue
        upto = (i + 1) * len(b) // len(a)
        if upto > at and b[upto - 1][0] in ("lg", "ps"):
            upto += 1
        out += b[at:upto]
        at = max(at, upto)
    return out


def schedule(causal, kind):
    return [step for step in spread_out(causal, kind) if step[0] not in ("space", "late")]


def spread_out(causal, kind):
    prep = kind in ("first", "second", "body")
    attn = kind in ("second", "body", "eighth")
    route = kind in ("body", "eighth", "ninth")
    n1, n2, n3 = N_ROUTE[causal]
    start = [("oT", 0), ("oT", 1)] if route else []
    y = [("y", 0), ("y", 1)] if route else []
    norm = pieces("ln", N_LN) if route else []
    save = ([("sv", 0)] if route else []) + ([("xp", 0)] if attn else [])
    before_rows, behind_rows, before_exp, behind_exp, before_sums = [[SPACE] * n for n in SPACES[causal]]
    rows = before_rows + [("rT", 0), SPACE, ("rT", 1)] + behind_rows if route else []
    route_1 = ([("lg", 0)] + pieces("l1", n1) + before_exp + [("ex", 0)] + behind_exp) if route else []
    route_2 = pieces("l2", n2) if route else []
    route_3 = (before_sums + [("ps", 0)] + pieces("l3", n3)) if route else []
    scatter = [("sc", i) for i in range(2 * TB)] if route else []
    gathers = [("gi", 0)] + [("ga", i) for i in range(2 * TB)]
    combine = pieces("cb", N_COMBINE)
    c = CHUNKS
    project = [("xT", 0), ("xT", 1), ("qk", c[0]), ("qk", c[1]), ("qs", c[0]), ("qk", c[2]), ("qs", c[1]),
               ("st_q", 0), ("qk", c[3]), ("qs", c[2]), ("qs", c[3])]
    if kind == "zeroth":
        return [("xl", 0)] + (project + [("st_q", 1)] if causal else gathers + combine)
    if kind == "eighth":
        start = [("wl", 0)] + start
    if kind == "ninth" and not causal:
        start = [("wl", 1)] + start
    if causal:
        start = ([("mr", 1), ("ms", 1)] if attn else []) + start
    if not prep:
        others = y + norm + save + rows + route_1 + route_2 + route_3 + scatter
    elif causal:
        maxima = [("mx", i) for i in range(N_MX)]
        maxima = (maxima[0:HALF_MX] + [("mc", 0)] + maxima[HALF_MX:HALF_MX + 3] + [("mr", 0), ("ms", 0)]
                  + maxima[HALF_MX + 3:] + [("mc", 1)])
        finish = norm[NORM_FIRST:] + save + [("xl", 0)] + rows + route_1 + route_2 + route_3 + scatter
        others = ([("v", 0), ("v", 1)] + start + y + norm[0:NORM_FIRST]
                  + mixed(maxima[:-MAXIMA_LAST], finish)
                  + mixed(maxima[-MAXIMA_LAST:], project[:PROJECT_BETWEEN]) + project[PROJECT_BETWEEN:])
        start = []
    else:
        turn_x = [("xT", 0), ("xT", 1)]
        project = [("qk", 0), ("qk", 2), ("ro", 0), ("qk", 1), ("ro", 2), ("st_q", 0), ("qk", 3), ("ro", 1),
                   ("v", 0), ("ro", 3), ("v", 1), ("st_q", 1)]
        if not route:
            start = save
            n = PROJECT_FIRST[kind]
            others = ([LATE] * N_LATE[kind] + turn_x + [("xl", 0)] + gathers + project[:n]
                      + mixed(combine, project[n:]))
        else:
            start += turn_x
            others = (y + gathers[0:7] + project[0:1] + norm[0:6] + project[1:3] + norm[6:12]
                      + gathers[7:] + project[3:4] + norm[12:18] + project[4:6] + norm[18:] + save + [("xl", 0)]
                      + project[6:] + mixed(combine, rows + route_1 + route_2 + route_3) + scatter)
    out = []
    out += start
    if not attn:
        return out + others + ([("st_q", 1)] if causal and prep else [])
    per_group = len(UNITS_CAUSAL if causal else UNITS_FULL)
    n_units = NG * per_group
    cost = COST[causal]
    total, at = sum(cost.get(step, 0) for step, _ in others), 0
    others = list(others)
    for half in range(2 * (n_units + 2)):
        n = half // 2
        if half % 2 == 0:
            if n < n_units:
                out.append(("st", n))
            if n >= 4 and (n - 4) % per_group == per_group - 1:
                out.append(("on", (n - 4) // per_group))
        elif n >= 2:
            out.append(("av", n - 2))
            if (n - 2) % per_group == per_group - 1:
                out.append(("oe", (n - 2) // per_group))
        while others and (at + cost.get(others[0][0], 0) / 2) * 2 * (n_units + 2) <= total * (half + 1):
            at += cost.get(others[0][0], 0)
            out.append(others.pop(0))
    out += others + [("on", NG - 1)]
    if causal and prep:
        out.append(("st_q", 1))
    return out


def bank_keys(causal, kind):
    keys = []
    for step, n in schedule(causal, kind):
        if step in ("xT", "qk", "ro", "v", "on", "oT", "y", "rT", "lg", "ps", "mx", "mr"):
            keys.append((step, n))
    return keys


class Banks:

    def __init__(self, causal, ready, free, memory):
        self.ready, self.free, self.memory = ready, free, memory
        self.n = len(memory)
        self.place, self.uses = {}, {}
        for kind in KINDS:
            keys = bank_keys(causal, kind)
            self.place[kind] = {key: (i % self.n, i // self.n) for i, key in enumerate(keys)}
            self.uses[kind] = [sum(i % self.n == b for i in range(len(keys))) for b in range(self.n)]

    def base(self, turn, b):
        u = {kind: self.uses[kind][b] for kind in KINDS}
        if turn.kind == "zeroth":
            return 0
        if turn.kind == "first":
            return u["zeroth"]
        if turn.kind == "second":
            return u["zeroth"] + u["first"]
        before = u["zeroth"] + u["first"] + u["second"]
        if turn.kind == "body":
            return turn.it * (2 * u["body"]) + (before + (turn.s - 2) * u["body"])
        before += (NB - 2) * u["body"]
        return before if turn.kind == "eighth" else before + u["eighth"]

    def acquire(self, pe, turn, key):
        b, n = self.place[turn.kind][key]
        wait(pe, self.free[b], self.base(turn, b) + n)
        return self.memory[b], self.ready[b]

    def filled(self, eng, turn, key):
        b, n = self.place[turn.kind][key]
        eng.wait_ge(self.ready[b], self.base(turn, b) + (n + 1))
        return self.memory[b], self.free[b]

    def read(self, eng, turn, key):
        b, n = self.place[turn.kind][key]
        eng.wait_ge(self.free[b], self.base(turn, b) + (n + 1))

    def both_read(self, pe, turn, step):
        if self.place[turn.kind][(step, 0)][0] != self.place[turn.kind][(step, 1)][0]:
            self.read(pe, turn, (step, 0))
        self.read(pe, turn, (step, 1))

    def total(self, b):
        u = {kind: self.uses[kind][b] for kind in KINDS}
        return sum(u.values()) + (NB - 3) * u["body"]

    def all_before_read(self, eng, turn):
        for b in range(self.n):
            wait(eng, self.free[b], self.base(turn, b))


class Chain:

    def __init__(self, eng, sem, base):
        self.eng, self.sem, self.base, self.n = eng, sem, base, 0

    def unwaited(self, instruction):
        self.n += 1
        instruction.then_inc(self.sem, 1)

    def join(self):
        wait(self.eng, self.sem, self.base + self.n)

    def pause(self):
        yield
        self.join()

    def __call__(self, instruction):
        self.unwaited(instruction)
        yield from self.pause()

    def step(self, instruction):
        self.unwaited(instruction)
        self.join()


def all_of(chained):
    for _ in chained:
        pass


def together(a, b, ratio):
    for _ in a:
        for _ in range(ratio):
            next(b, None)
    all_of(b)


class InPieces:

    def __init__(self, count):
        self.count, self.running = count, {}

    def piece(self, step, i, start):
        if i == 0:
            self.running[step] = start()
        if i == self.count[step] - 1:
            all_of(self.running[step])
        else:
            next(self.running[step], None)


RSQRT_STEPS = 13


def rsqrt(dve, chain, out, x, tmp):
    yield from chain(dve.tensor_scalar(out.bitcast(I32), x.bitcast(I32), -0.5, RSQRT_MAGIC, ALU.mult, ALU.add))
    for _ in range(3):
        yield from chain(dve.tensor_tensor(tmp, out, out, ALU.mult))
        yield from chain(dve.tensor_tensor(tmp, tmp, x, ALU.mult))
        yield from chain(dve.tensor_scalar(tmp, tmp, -0.5, 1.5, ALU.mult, ALU.add))
        yield from chain(dve.tensor_tensor(out, out, tmp, ALU.mult))


def spread(ap, n):
    return ap.unsqueeze(2).broadcast_to([ap.shape[0], ap.shape[1], n])


def build(nc, a, out):
    with ExitStack() as ctx:
        def sb(name, shape, dt=F32):
            return ctx.enter_context(nc.sbuf_tensor(name, shape, dt))

        def psum(name, shape, dt=F32):
            return ctx.enter_context(nc.psum_tensor(name, shape, dt))

        def sem(name):
            return ctx.enter_context(nc.semaphore(name))

        def dram(name, shape, dt=F32):
            return nc.dram_tensor(name, shape, dt, kind="Internal").ap()

        parts = dram("qk_parts", [2, 2, 3, D, S], BF16)
        x1_dram = dram("x1_rows", [NTOK + S, D])
        x3_dram = dram("x3_rows", [NTOK, D])
        slot_x0 = dram("slot_x0", [E0 * CAP, D])
        slot_y0 = dram("slot_y0", [E0 * CAP, D])
        slot_x1 = dram("slot_x1", [ZROW + P, D])
        slot_y1 = dram("slot_y1", [NBLK * P, D])

        ident = sb("ident", [P, P])
        ident_b = sb("ident_b", [P, P], BF16)
        before = sb("before", [P, P], BF16)
        ones_b = sb("ones_b", [P, P], BF16)
        mask = sb("mask", [P, S])
        rot = sb("rot", [P, P])
        cos_t = sb("cos_t", [P, S])
        sin_t = sb("sin_t", [P, S])
        lane = sb("lane", [P, 304])
        zero = sb("zero", [P, D])

        arena = sb("arena", [P, 21504])
        stack_words = NH * S // 2
        Q = [arena[:, i * stack_words:(i + 1) * stack_words].bitcast(BF16).rearrange("p (h n) -> p h n", h=NH)
             for i in (0, 1)]
        K = [arena[:, i * stack_words:(i + 1) * stack_words].bitcast(BF16).rearrange("p (h n) -> p h n", h=NH)
             for i in (2, 3)]
        pt_at = 4 * stack_words
        PT = [arena[:, pt_at + i * 1024:pt_at + (i + 1) * 1024].rearrange("p (h n) -> p h n", h=GH)
              for i in range(RING)]

        w_qkv = sb("w_qkv", [P, CD, 3 * D])
        w_o = sb("w_o", [P, CD, D])
        w_r = sb("w_r", [P, CD, NE1])
        b_qk = sb("b_qk", [P, 4])
        b_v = sb("b_v", [P, D])
        b_o = sb("b_o", [P, D])
        rn_scale = sb("rn_scale", [P, 2, CD])
        x_in = [sb(f"x_in{i}", [P, TB, D]) for i in range(2)]
        xT = sb("xT", [P, CD, S])
        qk_src = [sb(f"qk_src{j}", [P, 3, S], BF16) for j in range(4)]
        qk_rest = [sb(f"qk_rest{i}", [P, S]) for i in range(2)]
        qk_flat = [sb(f"qk_flat{i}", [P, S]) for i in range(2)]
        v_aug = [sb(f"v_aug{i}", [P, TB, NH, 32]) for i in range(2)]
        oT_raw = [sb(f"oT_raw{i}", [P, S]) for i in range(2)]
        o_nat = sb("o_nat", [P, TB, D])
        oT = sb("oT", [P, CD, S])
        x_res = sb("x_res", [P, TB, D])
        y_b = sb("y_b", [P, TB, D])
        x_out = [sb(f"x_out{i}", [P, TB, D]) for i in range(2)]
        rT = oT
        scratch = sb("scratch", [P, S])
        junk = [scratch[:, i * (S // 2):(i + 1) * (S // 2)].bitcast(BF16) for i in range(2)]
        mx = sb("mx", [P, NH * TB])
        mx_rest = sb("mx_rest", [P, NH * TB])
        mx_parts = sb("mx_parts", [P, 3, NH * TB], BF16)
        mx_rows = [sb(f"mx_rows{i}", [NH * TB // 2, 3, P], BF16) for i in range(2)]
        o_sum = sb("o_sum", [P, TB * GH])
        stats = sb("stats", [P, TB, 6])
        mv = sb("mv", [P, TB, 2])
        small = sb("small", [P, 16, TB])
        norm_to = stats, mv, [small[:, i, :] for i in (2, 1, 0)]
        NEM = NE1
        r_lg = sb("r_lg", [P, TB, NEM])
        r_w = sb("r_w", [P, TB, NEM])
        r_c = sb("r_c", [P, TB, NEM])
        r_oh = sb("r_oh", [P, 2, TB, NEM])
        r_pos = sb("r_pos", [P, TB, NEM])
        r_s = sb("r_s", [P, 24, TB])
        r_mask = sb("r_mask", [P, TB, NEM], BF16)
        r_before = sb("r_before", [P, TB + 1, NEM], BF16)
        row_to = [sb(f"row_to{i}", [P, TB, 2], I32) for i in range(2)]
        row_from0 = sb("row_from0", [P, NB + 1, TB * 2], I32)
        gate0 = sb("gate0", [P, NB + 1, TB * 3])
        row_now = [sb(f"row_now{i}", [P, TB * 2], I32) for i in range(2)]

        ST = [psum(f"ST{i}", [P, 1024]) for i in range(2)]
        OT = psum("OT", [P, 512])
        shared = [psum(f"shared{i}", [P, 512]) for i in range(3)]

        s_const = sem("s_const")
        s_fill = sem("s_fill")
        s_fill2 = sem("s_fill2")
        s_zero = sem("s_zero")
        s_ones = sem("s_ones")
        s_tick = sem("s_tick")

        def settle(eng):
            eng.sem_inc(s_tick, 1)

        def layer_sems(t):
            names = dict(
                xp="residual_ready", q1="first_part", q2="second_part", q3="third_part",
                rest="rest_ready", parts_saved="parts_saved",
                st="scores_ready", exp="weights_ready", sel="masked", av="unit_used", oe="out_saved",
                osum="out_sum_ready", mchain="max_split", mtaken="max_rows_taken",
                lnc="norm_chain", x_out="x_out_ready", rc="route_chain", ex="route_exp", ga_idx="rows_known",
                comb="combine_chain", rope="rope_chain")
            d = {k: sem(f"{t}_{v}") for k, v in names.items()}
            for k in ("x_load", "scattered", "x_saved", "gathered", "max_rows_saved"):
                d[k] = [sem(f"{t}_{k}{i}") for i in range(2)]
            d["stacked"] = [[sem(f"{t}_stacked{i}{j}") for j in range(2)] for i in range(2)]
            d["ready"] = [sem(f"{t}_bank_ready{i}") for i in range(3)]
            d["free"] = [sem(f"{t}_bank_free{i}") for i in range(3)]
            return d

        LA = layer_sems("a")
        banks_a = Banks(True, LA["ready"], LA["free"], shared)
        U0 = NG * len(UNITS_CAUSAL)

        ROUTE0 = 46
        LN_CHAIN = TB + TB + 1 + RSQRT_STEPS

        wi = [arena[:, i * 8192:i * 8192 + 2048].rearrange("p (c n) -> p c n", c=CD) for i in (0, 1)]
        wo = [arena[:, i * 8192 + 2048:i * 8192 + 4096].rearrange("p (c n) -> p c n", c=I0 // P) for i in (0, 1)]
        xg = [arena[:, 4096 + i * 1024:5120 + i * 1024].rearrange("p (t d) -> p t d", t=TB) for i in (0, 1)]
        xgT = arena[:, 6144:7168].rearrange("p (c n) -> p c n", c=CD)
        hT = arena[:, 12288:16384].rearrange("p (c n) -> p c n", c=I0 // P)
        yo = [arena[:, 16384 + i * 1024:17408 + i * 1024].rearrange("p (t d) -> p t d", t=TB) for i in (0, 1)]
        b_load = [sem(f"b_load{i}") for i in range(2)]

        block = ctx.enter_context(nc.Block())

        def zero_rows(sp):
            sp.wait_ge(s_zero, 1)
            sp.dma_start(slot_x0.rearrange("(a p) d -> p a d", p=P),
                         zero[:, :].unsqueeze(1).broadcast_to([P, E0 * CAP // P, D])).then_inc(s_filled_rows, 16)
            sp.dma_start(slot_x1[ZROW:ZROW + P, :], zero[:, :]).then_inc(d_zero, 16)
            sp.dma_start(x1_dram[NTOK:NTOK + S, :].rearrange("(t p) d -> p t d", p=P),
                         zero[:, :].unsqueeze(1).broadcast_to([P, TB, D])).then_inc(d_zero, 16)

        def expert_weights(sp, e, par):
            settle(sp)
            sp.dma_start(wi[par], a["experts_inter"][bass.ds(e * D, D), :].rearrange("(c p) n -> p c n", p=P)
                         ).then_inc(b_load[par], 16)
            sp.dma_start(wo[par], a["experts_out"][bass.ds(e * I0, I0), :].rearrange("(c p) n -> p c n", p=P)
                         ).then_inc(b_load[par], 16)

        def a_sp(sp):
            L = LA

            def emit(turn):
                for step, n in schedule(True, turn.kind):
                    if step == "xl":
                        k, par, half = turn.batch(-1 if step in AHEAD[True] else 0)
                        wait(sp, L["xp"], k - 1)
                        settle(sp)
                        sp.dma_start(x_in[par][:, :, :],
                                     a["x"][bass.ds(k * S, S), :].rearrange("(t p) d -> p t d", p=P)
                                     ).then_inc(L["x_load"][par], 16)
                        if turn.kind == "zeroth":
                            zero_rows(sp)
                    elif step == "qs":
                        k, par, half = turn.batch(-1)
                        order = CHUNKS.index(n)
                        wait(sp, L["stacked"][par][n % 2], half * STACK_DMAS)
                        settle(sp)
                        sp.wait_ge(L["q3"], k * 4 + (order + 1))
                        settle(sp)
                        rows = slice((n % 2) * P, (n % 2 + 1) * P)
                        sp.dma_start(parts[par, n // 2, :, rows, :].rearrange("j p n -> p j n"),
                                     qk_src[n][:, :, :]).then_inc(L["parts_saved"], 16)
                    elif step == "st_q":
                        k, par, half = turn.batch(-1 if step in AHEAD[True] else 0)
                        sp.wait_ge(L["parts_saved"], k * 64 + (32 * n + 32))
                        settle(sp)
                        wait(sp, L["exp"], (k - 2) * U0 + (n + 1) * U0 // 2)
                        settle(sp)
                        heads = slice(n * NH // 2, (n + 1) * NH // 2)
                        for t, (i, j) in enumerate(PRODUCTS):
                            for side, part, stack in ((0, i, Q), (1, j, K)):
                                sp.dma_start(stack[par][t * HD:(t + 1) * HD, heads, :],
                                             parts[par, side, part, n * P:(n + 1) * P, :].rearrange(
                                                 "(h d) n -> d h n", d=HD)).then_inc(L["stacked"][par][n], 16)
                    elif step == "ms":
                        k, par, half = turn.batch(n)
                        sp.wait_ge(L["mtaken"], k * 2 + (n + 1))
                        settle(sp)
                        for j in range(3):
                            sp.dma_start(Q[par][SK + j:SK + j + 1, n * NH // 2:(n + 1) * NH // 2, :].rearrange(
                                "p h (b n) -> p (h b) n", b=TB), mx_rows[n][:, j, :]
                                         ).then_inc(L["max_rows_saved"][n], 16)
                    elif step == "wl":
                        sp.wait_ge(L["exp"], (NB - 1) * U0)
                        settle(sp)
                        for i in range(2):
                            sp.wait_ge(L["stacked"][0][i], (NB // 2 + 1) * STACK_DMAS)
                            settle(sp)
                        for e in range(2):
                            expert_weights(sp, e, e)
                    elif step == "sv":
                        k, par, half = turn.batch(2)
                        sp.wait_ge(L["x_out"], k * TB + TB)
                        settle(sp)
                        sp.dma_start(x1_dram[bass.ds(k * S, S), :].rearrange("(t p) d -> p t d", p=P),
                                     x_out[par][:, :, :]).then_inc(L["x_saved"][par], 16)
            slots(sp, emit)

        def attention_pe(pe, L, banks, causal, turn, step, n, U):
            k, par, half = turn.batch(1)
            units = UNITS_CAUSAL if causal else UNITS_FULL
            per = len(units)
            rows = SK + 3 if causal else SK
            if step == "st":
                if n % (U // 2) == 0:
                    if causal:
                        pe.wait_ge(L["max_rows_saved"][n // (U // 2)], k * 48 + 48)
                    else:
                        pe.wait_ge(L["stacked"][par][n // (U // 2)], half * STACK_DMAS + STACK_DMAS)
                wait(pe, L["exp"], k * U + (n - 1))
                g, u = n // per, n % per
                for i in range(GH):
                    h = g * GH + i
                    for kb, q0, nq, at in units[u]:
                        mm = pe.matmul(ST[n % 2][:, i * 256 + at:i * 256 + at + nq],
                                       K[par][0:rows, h, kb * P:(kb + 1) * P],
                                       Q[par][0:rows, h, q0:q0 + nq], start=True, stop=True)
                mm.then_inc(L["st"], 1)
            elif step == "av":
                g, u = n // per, n % per
                if n == 0:
                    banks.all_before_read(pe, turn)
                if u == 0:
                    wait(pe, L["oe"], k * NG + g)
                if causal and u in DIAGONAL:
                    pe.wait_ge(L["sel"], k * (3 * NG) + (g * 3 + sorted(DIAGONAL).index(u) + 1))
                else:
                    pe.wait_ge(L["exp"], k * U + (n + 1))
                for piece, (kb, q0, nq, at) in enumerate(units[u]):
                    for i in range(GH):
                        mm = pe.matmul(OT[32 * i:32 * i + 32, q0:q0 + nq],
                                       v_aug[par][:, kb, g * GH + i, :],
                                       PT[n % RING][:, i, at:at + nq],
                                       start=(u == 0), stop=(u == per - 1),
                                       skip_group_check=True, tile_position=(0, 32 * i))
                mm.then_inc(L["av"], 1)
            elif step == "on":
                bank, ready = banks.acquire(pe, turn, ("on", n))
                pe.wait_ge(L["oe"], k * NG + (n + 1))
                for t in range(TB):
                    mm = pe.transpose(bank[:, t * P:(t + 1) * P], oT_raw[n % 2][:, t * P:(t + 1) * P], ident[:, :])
                mm.then_inc(ready, 1)
            elif step == "oT":
                bank, ready = banks.acquire(pe, turn, ("oT", n))
                if n == 0:
                    banks.all_before_read(pe, turn)
                for t in range(TB):
                    mm = pe.transpose(bank[:, t * P:(t + 1) * P], o_nat[:, t, n * P:(n + 1) * P], ident[:, :])
                mm.then_inc(ready, 1)
            elif step == "y":
                bank, ready = banks.acquire(pe, turn, ("y", n))
                if n == 0:
                    banks.both_read(pe, turn, "oT")
                for t in (2 * n, 2 * n + 1):
                    for c in range(CD):
                        mm = pe.matmul(bank[:, (t % 2) * D:(t % 2 + 1) * D], oT[:, c, t * P:(t + 1) * P],
                                       w_o[:, c, :], start=(c == 0), stop=(c == CD - 1))
                mm.then_inc(ready, 1)

        def route_pe(pe, L, banks, turn, step, n, ne, chain_len, mask_at):
            k, par, half = turn.batch(2)
            if step == "rT":
                bank, ready = banks.acquire(pe, turn, ("rT", n))
                pe.wait_ge(L["x_out"], k * TB + TB)
                for t in range(TB):
                    mm = pe.transpose(bank[:, t * P:(t + 1) * P], x_out[par][:, t, n * P:(n + 1) * P], ident[:, :])
                mm.then_inc(ready, 1)
            elif step == "lg":
                bank, ready = banks.acquire(pe, turn, ("lg", 0))
                banks.both_read(pe, turn, "rT")
                for t in range(TB):
                    for c in range(CD):
                        mm = pe.matmul(bank[:, t * ne:(t + 1) * ne], rT[:, c, t * P:(t + 1) * P],
                                       w_r[:, c, 0:ne], start=(c == 0), stop=(c == CD - 1))
                mm.then_inc(ready, 1)
            elif step == "ps":
                bank, ready = banks.acquire(pe, turn, ("ps", 0))
                pe.wait_ge(L["rc"], k * chain_len + mask_at)
                for t in range(TB):
                    pe.matmul(bank[:, t * ne:(t + 1) * ne], before[:, :], r_mask[:, t, 0:ne],
                              start=True, stop=False)
                    mm = pe.matmul(bank[:, t * ne:(t + 1) * ne], ones_b[:, :], r_before[:, t, 0:ne],
                                   start=False, stop=True)
                mm.then_inc(ready, 1)

        def a_pe(pe):
            L, banks = LA, banks_a
            pe.wait_ge(s_const, CONST_DMAS * 16)

            def emit(turn):
                if turn.kind == "first":
                    pe.wait_ge(s_fill2, 2)
                for step, n in schedule(True, turn.kind):
                    k, par, half = turn.batch(-1 if step in AHEAD[True] else 0)
                    if step == "xT":
                        bank, ready = banks.acquire(pe, turn, ("xT", n))
                        if n == 0:
                            pe.wait_ge(L["x_load"][par], half * 16 + 16)
                        for t in range(TB):
                            mm = pe.transpose(bank[:, t * P:(t + 1) * P], x_in[par][:, t, n * P:(n + 1) * P],
                                              ident[:, :])
                        mm.then_inc(ready, 1)
                    elif step == "qk":
                        bank, ready = banks.acquire(pe, turn, ("qk", n))
                        if n == 0:
                            banks.both_read(pe, turn, "xT")
                        for c in range(CD):
                            mm = pe.matmul(bank[:, :], w_qkv[:, c, n * P:(n + 1) * P], xT[:, c, :],
                                           start=(c == 0), stop=(c == CD - 1))
                        mm.then_inc(ready, 1)
                    elif step == "v":
                        bank, ready = banks.acquire(pe, turn, ("v", n))
                        for t in (2 * n, 2 * n + 1):
                            for c in range(CD):
                                mm = pe.matmul(bank[:, (t % 2) * D:(t % 2 + 1) * D], xT[:, c, t * P:(t + 1) * P],
                                               w_qkv[:, c, 2 * D:3 * D], start=(c == 0), stop=(c == CD - 1))
                        mm.then_inc(ready, 1)
                    elif step == "mx":
                        if n % HALF_MX == 0:
                            pe.wait_ge(L["stacked"][par][n // HALF_MX], half * STACK_DMAS + STACK_DMAS)
                        bank, ready = banks.acquire(pe, turn, ("mx", n))
                        for of_pair, qb, at in FILLS[n % len(FILLS)]:
                            head = n // len(FILLS) * 2 + of_pair
                            mm = pe.matmul(bank[:, at:at + S - qb * P], Q[par][0:SK, head, qb * P:(qb + 1) * P],
                                           K[par][0:SK, head, qb * P:S], start=True, stop=True)
                        mm.then_inc(ready, 1)
                    elif step == "mr":
                        k, par, half = turn.batch(n)
                        bank, ready = banks.acquire(pe, turn, ("mr", n))
                        pe.wait_ge(L["mchain"], k * 8 + (4 * n + 4))
                        settle(pe)
                        for j in range(3):
                            mm = pe.transpose(bank[0:32, j * 64:(j + 1) * 64].bitcast(BF16),
                                              mx_parts[:, j, n * 32:(n + 1) * 32], ident_b[:, :])
                        mm.then_inc(ready, 1)
                    elif step in ("st", "av", "on", "oT", "y"):
                        attention_pe(pe, L, banks, True, turn, step, n, U0)
                    elif step in ("rT", "lg", "ps"):
                        route_pe(pe, L, banks, turn, step, n, NE0, ROUTE0, MASK0)
            slots(pe, emit)

        def attention_act(act, L, causal, turn, step, n, U, func):
            k, par, half = turn.batch(1)
            if step == "st":
                act.wait_ge(L["st"], k * U + (n + 1))
                wait(act, L["av"], k * U + (n + 1 - RING))
                act.activation(PT[n % RING][:, :, :], ST[n % 2][:, :].rearrange("p (h n) -> p h n", h=GH),
                               func, scale=ATT_SCALE).then_inc(L["exp"], 1)
            elif step == "oe":
                per = U // NG
                act.wait_ge(L["av"], k * U + (n + 1) * per)
                act.activation(oT_raw[n % 2][:, :], OT[:, :], ACT.Identity).then_inc(L["oe"], 1)

        def copy_bank(act, banks, turn, key, to):
            bank, free = banks.filled(act, turn, key)
            act.activation(to, bank[:, :], ACT.Identity).then_inc(free, 1)

        def a_act(act):
            L, banks = LA, banks_a
            act.wait_ge(s_const, CONST_DMAS * 16)

            def emit(turn):
                for step, n in schedule(True, turn.kind):
                    k, par, half = turn.batch(-1 if step in AHEAD[True] else 0)
                    if step == "xT":
                        copy_bank(act, banks, turn, ("xT", n), xT[:, n, :])
                    elif step == "qk":
                        bank, free = banks.filled(act, turn, ("qk", n))
                        wait(act, L["parts_saved"], k * 64)
                        act.activation(qk_src[n][:, 0, :], bank[:, :], ACT.Identity,
                                       bias=b_qk[:, n:n + 1]).then_inc(L["q1"], 1)
                        order = CHUNKS.index(n)
                        wait(act, L["q2"], k * 4 + (order - 1))
                        act.activation(qk_flat[order % 2][:, :], bank[:, :], ACT.Identity,
                                       bias=b_qk[:, n:n + 1]).then_inc(free, 1)
                    elif step in ("st", "oe"):
                        attention_act(act, L, True, turn, step, n, U0, ACT.Exp)
                    elif step == "oT":
                        copy_bank(act, banks, turn, ("oT", n), oT[:, n, :])
                    elif step == "rT":
                        copy_bank(act, banks, turn, ("rT", n), rT[:, n, :])
                    elif step == "ex":
                        k, par, half = turn.batch(2)
                        act.wait_ge(L["rc"], k * ROUTE0 + 3)
                        act.activation(r_w[:, :, 0:NE0], r_w[:, :, 0:NE0], ACT.Exp).then_inc(L["ex"], 1)
            slots(act, emit)

        def norm_stats_dve(dve, chain, src, to):
            stats, mv, _ = to
            for t in range(TB):
                chain.unwaited(dve.bn_stats(stats[:, t, :], src[:, t, :]))
                yield
            yield from chain.pause()
            settle(dve)
            for t in range(TB):
                chain.unwaited(dve.bn_aggr(mv[:, t, :], stats[:, t, :]))
            yield from chain.pause()

        def norm_root_dve(dve, chain, to):
            _, mv, (tmp, root, shifted) = to
            yield from chain(dve.tensor_scalar(shifted, mv[:, :, 1], LN_EPS, None, ALU.add))
            yield from rsqrt(dve, chain, root, shifted, tmp)

        def attention_dve(dve, L, banks, turn, step, n, eps):
            k, par, half = turn.batch(1 if step == "on" else 2)
            if step == "on":
                bank, free = banks.filled(dve, turn, ("on", n))
                view = bank[:, :].rearrange("p (th c) -> p th c", c=32)
                if n:
                    banks.read(dve, turn, ("on", n - 1))
                if eps:
                    dve.tensor_scalar(o_sum[:, :], view[:, :, HD], eps, None, ALU.add).then_inc(L["osum"], 1)
                    dve.wait_ge(L["osum"], k * (2 * NG) + (2 * n + 1))
                    dve.reciprocal(o_sum[:, :], o_sum[:, :]).then_inc(L["osum"], 1)
                    dve.wait_ge(L["osum"], k * (2 * NG) + (2 * n + 2))
                else:
                    dve.reciprocal(o_sum[:, :], view[:, :, HD]).then_inc(L["osum"], 1)
                    dve.wait_ge(L["osum"], k * NG + (n + 1))
                dve.tensor_tensor(
                    o_nat[:, :, n * GH * HD:(n + 1) * GH * HD].rearrange("p t (h d) -> p t h d", h=GH),
                    view[:, :, 0:HD].rearrange("p (t h) d -> p t h d", t=TB),
                    spread(o_sum[:, :], HD).rearrange("p (t h) d -> p t h d", t=TB),
                    ALU.mult).then_inc(free, 1)
            elif step == "y":
                bank, free = banks.filled(dve, turn, ("y", n))
                wait(dve, L["x_out"], k * TB)
                dve.wait_ge(L["xp"], k + 1)
                dve.tensor_tensor(y_b[:, 2 * n:2 * n + 2, :], bank[:, :].rearrange("p (t d) -> p t d", t=2),
                                  x_res[:, 2 * n:2 * n + 2, :], ALU.add).then_inc(free, 1)

        def finish_dve(dve, L, banks, turn):
            k, par, half = turn.batch(2)
            for i in range(2):
                banks.read(dve, turn, ("y", i))
                settle(dve)
            chain = Chain(dve, L["lnc"], k * LN_CHAIN)
            yield from norm_stats_dve(dve, chain, y_b, norm_to)
            yield from norm_root_dve(dve, chain, norm_to)
            assert chain.n == LN_CHAIN
            wait(dve, L["x_saved"][par], half * 16)
            wait(dve, L["scattered"][par], half * (16 * 2 * TB))
            for t in range(TB):
                dve.tensor_scalar(x_out[par][:, t, :], y_b[:, t, :], mv[:, t, 0:1], small[:, 1, t:t + 1],
                                  ALU.subtract, ALU.mult).then_inc(L["x_out"], 1)
                yield

        def first_choice(dve, chain, w, ne, best, rank, oh):
            yield from chain(dve.tensor_reduce(best, w, AX_X, ALU.max))
            yield from chain(dve.tensor_tensor(r_c[:, :, 0:ne], w, spread(best, ne), ALU.is_ge))
            yield from chain(dve.tensor_tensor(r_c[:, :, 0:ne], r_c[:, :, 0:ne],
                                    rank.unsqueeze(1).broadcast_to([P, TB, ne]), ALU.mult))
            yield from chain(dve.tensor_reduce(r_s[:, 0, :], r_c[:, :, 0:ne], AX_X, ALU.max))
            yield from chain(dve.tensor_tensor(oh, r_c[:, :, 0:ne], spread(r_s[:, 0, :], ne), ALU.is_equal))

        def count_before(dve, chain, ne):
            yield from chain(dve.tensor_copy(r_before[:, 0, 0:ne], r_before[:, TB, 0:ne]))
            for t in range(TB):
                yield from chain(dve.tensor_tensor(r_before[:, t + 1, 0:ne], r_before[:, t, 0:ne], r_mask[:, t, 0:ne],
                                        ALU.add))

        def lanes(at, n):
            return lane[:, at:at + n].unsqueeze(1).broadcast_to([P, TB, n])

        def a_route_dve(dve, banks, turn, step):
            L, ne = LA, NE0
            k, par, half = turn.batch(2)
            w = r_w[:, :, 0:ne]
            oh = [r_oh[:, i, :, 0:ne] for i in range(2)]
            if step == "l1":
                chain = Chain(dve, L["rc"], k * ROUTE0)
                bank, free = banks.filled(dve, turn, ("lg", 0))
                dve.tensor_tensor(r_lg[:, :, 0:ne], bank[:, 0:TB * ne].rearrange("p (t e) -> p t e", t=TB),
                                  lanes(LANE_RB0, ne), ALU.add).then_inc(free, 1)
                yield
                banks.read(dve, turn, ("lg", 0))
                yield from chain(dve.tensor_reduce(r_s[:, 1, :], r_lg[:, :, 0:ne], AX_X, ALU.max))
                yield from chain(dve.tensor_tensor(w, r_lg[:, :, 0:ne], spread(r_s[:, 1, :], ne), ALU.subtract))
                chain.unwaited(dve.memset(r_s[:, 2, :], 0.0))
                assert chain.n == 3
            elif step == "l2":
                chain = Chain(dve, L["rc"], k * ROUTE0)
                chain.n = 3
                dve.wait_ge(L["ex"], k + 1)
                yield from chain(dve.tensor_reduce(r_s[:, 2, :], w, AX_X, ALU.add))
                yield from chain(dve.reciprocal(r_s[:, 3, :], r_s[:, 2, :]))
                yield from chain(dve.tensor_tensor(w, w, spread(r_s[:, 3, :], ne), ALU.mult))
                yield from first_choice(dve, chain, w, ne, r_s[:, 4, :], lane[:, LANE_RANK0:LANE_RANK0 + ne], oh[0])
                yield from chain(dve.scalar_tensor_tensor(out=r_lg[:, :, 0:ne].rearrange("p t e -> p t e"), in0=oh[0],
                                               scalar=-2.0, in1=w, op0=ALU.mult, op1=ALU.add))
                yield from first_choice(dve, chain, r_lg[:, :, 0:ne], ne, r_s[:, 5, :],
                             lane[:, LANE_RANK0:LANE_RANK0 + ne], oh[1])
                yield from chain(dve.tensor_scalar(r_s[:, 6, :], r_s[:, 5, :], 0.0, None, ALU.is_gt))
                yield from chain(dve.tensor_tensor(oh[1], oh[1], spread(r_s[:, 6, :], ne), ALU.mult))
                yield from chain(dve.tensor_tensor(r_mask[:, :, 0:ne], oh[0], oh[1], ALU.add))
                yield from count_before(dve, chain, ne)
                assert chain.n == MASK0, chain.n
            elif step == "l3":
                chain = Chain(dve, L["rc"], k * ROUTE0)
                chain.n = MASK0
                bank, free = banks.filled(dve, turn, ("ps", 0))
                pos = bank[:, 0:TB * ne].rearrange("p (t e) -> p t e", t=TB)
                chain.unwaited(dve.tensor_tensor(r_c[:, :, 0:ne], pos, lanes(LANE_CAP, ne), ALU.is_lt))
                dve.tensor_tensor(r_pos[:, :, 0:ne], pos, lanes(LANE_SEG0, ne), ALU.add).then_inc(free, 1)
                yield from chain.pause()
                banks.read(dve, turn, ("ps", 0))
                yield from chain(dve.tensor_tensor(r_s[:, 7, :], oh[0][:, :, E0], r_s[:, 4, :], ALU.mult))
                yield from chain(dve.tensor_tensor(r_s[:, 8, :], oh[1][:, :, E0], r_s[:, 5, :], ALU.mult))
                yield from chain(dve.tensor_tensor(r_s[:, 7, :], r_s[:, 7, :], r_s[:, 8, :], ALU.add))
                g = gate0[:, bass.ds(k, 1), :].rearrange("p b (t c) -> p (b t) c", c=3)
                rows = row_from0[:, bass.ds(k, 1), :].rearrange("p b (t c) -> p (b t) c", c=2)
                yield from chain(dve.tensor_scalar(g[:, :, 2], r_s[:, 7, :], 1.0, None, ALU.add))
                wait(dve, L["scattered"][par], half * (16 * 2 * TB))
                for i in range(2):
                    yield from chain(dve.tensor_tensor(oh[i], oh[i], r_c[:, :, 0:ne], ALU.mult))
                    yield from chain(dve.tensor_reduce(r_s[:, 9, :], oh[i], AX_X, ALU.add))
                    yield from chain(dve.tensor_tensor(oh[i], oh[i], r_pos[:, :, 0:ne], ALU.mult))
                    yield from chain(dve.tensor_reduce(r_s[:, 10, :], oh[i], AX_X, ALU.add))
                    yield from chain(dve.tensor_tensor(g[:, :, i], r_s[:, 4 + i, :], r_s[:, 9, :], ALU.mult))
                    yield from chain(dve.tensor_copy(rows[:, :, i], r_s[:, 10, :]))
                    yield from chain(dve.tensor_scalar(r_s[:, 11, :], r_s[:, 9, :], -FAR, FAR, ALU.mult, ALU.add))
                    yield from chain(dve.tensor_tensor(row_to[par][:, :, i], r_s[:, 10, :], r_s[:, 11, :], ALU.add))
                assert chain.n == ROUTE0, chain.n

        def a_dve(dve):
            L, banks = LA, banks_a
            chains = InPieces(dict(zip(("ln", "l1", "l2", "l3"), (N_LN,) + N_ROUTE[True])))
            dve.wait_ge(s_const, CONST_DMAS * 16)
            dve.memset(zero[:, :], 0.0).then_inc(s_zero, 1)
            dve.tensor_copy(ident_b[:, :], ident[:, :]).then_inc(s_fill, 1)
            dve.tensor_copy(before[:, :], scratch[:, 0:P]).then_inc(s_fill, 1)
            dve.memset(ones_b[:, :], 1.0).then_inc(s_fill, 1)
            dve.memset(row_from0[:, NB, :], 0).then_inc(s_fill, 1)
            dve.memset(gate0[:, NB, :], 0.0).then_inc(s_fill, 1)
            dve.memset(r_before[:, :, :], 0.0).then_inc(s_fill, 1)
            for i in range(2):
                dve.memset(v_aug[i][:, :, :, HD + 1:], 0.0).then_inc(s_fill, 1)
                dve.memset(v_aug[i][:, :, :, HD], 1.0).then_inc(s_fill, 1)
            dve.wait_ge(s_fill, 10)
            dve.sem_inc(s_fill2, 1)

            def emit(turn):
                for step, n in schedule(True, turn.kind):
                    k, par, half = turn.batch(-1 if step in AHEAD[True] else 0)
                    if step == "qs":
                        order = CHUNKS.index(n)
                        rest = qk_rest[order % 2]
                        dve.wait_ge(L["q1"], k * 4 + (order + 1))
                        banks.read(dve, turn, ("qk", n))
                        wait(dve, L["q3"], k * 4 + (order - 1))
                        dve.tensor_tensor(rest[:, :], qk_flat[order % 2][:, :], qk_src[n][:, 0, :],
                                          ALU.subtract).then_inc(L["rest"], 1)
                        dve.wait_ge(L["rest"], k * 4 + (order + 1))
                        dve.tensor_copy(qk_src[n][:, 1, :], rest[:, :]).then_inc(L["q2"], 1)
                    elif step == "v":
                        bank, free = banks.filled(dve, turn, ("v", n))
                        wait(dve, L["av"], (k - 1) * U0)
                        dve.tensor_tensor(
                            v_aug[par][:, 2 * n:2 * n + 2, :, 0:HD],
                            bank[:, :].rearrange("p (t h d) -> p t h d", t=2, h=NH),
                            b_v[:, :].rearrange("p (h d) -> p h d", h=NH).unsqueeze(1).broadcast_to([P, 2, NH, HD]),
                            ALU.add).then_inc(free, 1)
                    elif step == "mx":
                        bank, free = banks.filled(dve, turn, ("mx", n))
                        if n >= 2:
                            banks.read(dve, turn, ("mx", n - 2))
                        elif turn.kind != "first":
                            banks.all_before_read(dve, turn)
                        settle(dve)
                        for of_pair, qb, at in FILLS[n % len(FILLS)]:
                            i = (n // len(FILLS) * 2 + of_pair) * TB + qb
                            m = S - qb * P
                            taken = dve.tensor_tensor_reduce(
                                out=junk[n % 2][:, at:at + m], in0=bank[:, at:at + m], in1=mask[:, 0:m],
                                scale=1.0, scalar=LOW, op0=ALU.add, op1=ALU.max, accum_out=mx[:, i:i + 1])
                        taken.then_inc(free, 1)
                    elif step == "mc":
                        for i in (2, 1):
                            banks.read(dve, turn, ("mx", (n + 1) * HALF_MX - i))
                        chain = Chain(dve, L["mchain"], k * 8 + 4 * n)
                        top, rest = mx[:, n * 32:(n + 1) * 32], mx_rest[:, n * 32:(n + 1) * 32]
                        part = [mx_parts[:, j, n * 32:(n + 1) * 32] for j in range(3)]
                        chain.step(dve.tensor_scalar(part[0], top, -1.0, None, ALU.mult))
                        chain.step(dve.scalar_tensor_tensor(out=rest, in0=top, scalar=-1.0, in1=part[0],
                                                            op0=ALU.mult, op1=ALU.subtract))
                        chain.step(dve.tensor_copy(part[1], rest))
                        chain.step(dve.tensor_tensor(part[2], rest, part[1], ALU.subtract))
                    elif step == "mr":
                        k, par, half = turn.batch(n)
                        bank, free = banks.filled(dve, turn, ("mr", n))
                        wait(dve, L["max_rows_saved"][n], k * 48)
                        dve.tensor_copy(mx_rows[n][:, :, :],
                                        bank[0:32, 0:192].bitcast(BF16).rearrange("p (j n) -> p j n", j=3)
                                        ).then_inc(free, 1)
                        banks.read(dve, turn, ("mr", n))
                        dve.sem_inc(L["mtaken"], 1)
                    elif step in ("on", "y"):
                        attention_dve(dve, L, banks, turn, step, n, 0)
                    elif step == "ln":
                        chains.piece(step, n, lambda: finish_dve(dve, L, banks, turn))
                    elif step in ("l1", "l2", "l3"):
                        chains.piece(step, n, lambda: a_route_dve(dve, banks, turn, step))
            slots(dve, emit)

        def a_pool(pool):
            L = LA
            for i in range(2):
                pool.memset(K[i][SK:SK + 3, :, :], 1.0).then_inc(s_ones, 1)
            pool.wait_ge(s_ones, 2)
            pool.sem_inc(s_fill2, 1)
            pool.wait_ge(s_const, CONST_DMAS * 16)

            def emit(turn):
                for step, n in schedule(True, turn.kind):
                    k, par, half = turn.batch(-1 if step in AHEAD[True] else 0)
                    if step == "xp":
                        k, par, half = turn.batch(1)
                        pool.wait_ge(L["x_load"][par], half * 16 + 16)
                        wait(pool, L["x_out"], k * TB)
                        pool.tensor_tensor(out=x_res[:, :, :], in0=x_in[par][:, :, :],
                                           in1=b_o[:, :].unsqueeze(1).broadcast_to([P, TB, D]),
                                           op=ALU.add).then_inc(L["xp"], 1)
                    elif step == "qs":
                        order = CHUNKS.index(n)
                        pool.wait_ge(L["q2"], k * 4 + (order + 1))
                        pool.tensor_tensor(out=qk_src[n][:, 2, :], in0=qk_rest[order % 2][:, :],
                                           in1=qk_src[n][:, 1, :], op=ALU.subtract).then_inc(L["q3"], 1)
                    elif step == "st":
                        k, par, half = turn.batch(1)
                        u = n % len(UNITS_CAUSAL)
                        if u not in DIAGONAL:
                            continue
                        at, blocks = DIAGONAL[u]
                        pool.wait_ge(L["exp"], k * U0 + (n + 1))
                        settle(pool)
                        v = PT[n % RING][:, :, at:at + blocks * P].rearrange("p h (b q) -> p h b q", q=P)
                        pool.affine_select(out=v, in_=v, compare_op=ALU.is_ge, fill=0.0, base=0,
                                           pattern=[[0, GH], [0, blocks], [-1, P]],
                                           channel_multiplier=1).then_inc(L["sel"], 1)
                    elif step == "sc":
                        k, par, half = turn.batch(2)
                        if n == 0:
                            pool.wait_ge(L["rc"], k * ROUTE0 + ROUTE0)
                            pool.wait_ge(s_filled_rows, 16)
                            settle(pool)
                        t, i = n // 2, n % 2
                        pool.indirect_dma_start(
                            out=slot_x0, out_offset=bass.IndirectOffsetOnAxis(ap=row_to[par][:, t, i:i + 1], axis=0),
                            in_=x_out[par][:, t, :], in_offset=None, bounds_check=E0 * CAP - 1,
                            oob_is_err=False).then_inc(L["scattered"][par], 16)
            slots(pool, emit)

        MASK0 = 3 + 3 + 5 + 1 + 5 + 3 + 5
        LANE_RANK0, LANE_CAP, LANE_SEG0, LANE_RB0 = 0, 16, 32, 48
        LANE_RANK1, LANE_FFN, LANE_SEG1, LANE_RB1 = 64, 80, 96, 112
        LANE_STEP, LANE_TRI, LANE_BLK, LANE_IOTA = 128, 160, 224, 296
        CONST_DMAS = 16
        s_filled_rows = sem("s_filled_rows")

        b_turned, b_turned_out = sem("b_turned"), sem("b_turned_out")
        b_up = sem("b_up")
        b_relu = [sem("b_relu_act"), sem("b_relu_dve")]
        b_down, b_down_out = sem("b_down"), sem("b_down_out")
        b_saved = [sem(f"b_saved{i}") for i in range(2)]
        MI = I0 // P
        up_banks = [ST[m // 2][:, (m % 2) * 512:(m % 2 + 1) * 512] for m in range(4)]
        down_banks = [shared[2], OT]

        def experts(eng, emit, pairs):
            def two(it):
                emit(it * 2, 0, it)
                emit(it * 2 + 1, 1, it)
            passes(eng, pairs, two)
            for e in range(2 * pairs, E0):
                emit(e, e % 2, e // 2)

        def b_sp(sp):
            def load_rows(e, par):
                settle(sp)
                sp.dma_start(xg[par], slot_x0[bass.ds(e * CAP, CAP), :].rearrange("(t p) d -> p t d", p=P)
                             ).then_inc(b_load[par], 16)

            sp.wait_ge(LA["oe"], NB * NG)
            for i in range(2):
                sp.wait_ge(LA["scattered"][i], NB // 2 * 16 * 2 * TB)
            load_rows(0, 0)
            load_rows(1, 1)
            for i in range(2):
                sp.wait_ge(LA["x_saved"][i], NB // 2 * 16)
            sp.wait_ge(LA["rc"], NB * ROUTE0)
            for dst, src in (
                (w_qkv[:, :, :], a["w_qkv1T"].rearrange("(c p) n -> p c n", p=P)),
                (w_o[:, :, :], a["w_o1T"].rearrange("(c p) n -> p c n", p=P)),
                (w_r[:, :, :], a["gate_wT"].rearrange("(c p) n -> p c n", p=P)),
                (b_qk[:, :], a["b_qk_cols1"]), (rn_scale[:, :, :], a["rn_cols"]),
                (b_v[:, :], a["b_v1"].partition_broadcast(P)),
                (b_o[:, :], a["b_o1"].partition_broadcast(P)),
                (lane[:, LANE_RB1:LANE_RB1 + NE1], a["expert_bias"].partition_broadcast(P)),
            ):
                sp.dma_start(dst, src).then_inc(s_w1, 16)

            def emit(e, par, half):
                sp.wait_ge(b_down_out, e * 2 + 2)
                settle(sp)
                sp.dma_start(slot_y0[bass.ds(e * CAP, CAP), :].rearrange("(t p) d -> p t d", p=P), yo[par]
                             ).then_inc(b_saved[par], 16)
                if not isinstance(e, int) or e + 2 < E0:
                    load_rows(e + 2, par)
                    expert_weights(sp, e + 2, par)
            experts(sp, emit, 2)
            sp.wait_ge(b_saved[0], 4 * 16)
            sp.wait_ge(b_saved[1], 3 * 16)

        def b_pe(pe):
            for b in range(3):
                pe.wait_ge(banks_a.free[b], banks_a.total(b))
            pe.wait_ge(LA["exp"], NB * U0)
            pe.wait_ge(LA["oe"], NB * NG)

            def emit(e, par, half):
                pe.wait_ge(b_load[par], half * 48 + 48)
                wait(pe, b_turned_out, e * CD)
                for c in range(CD):
                    for t in range(TB):
                        mm = pe.transpose(shared[c][:, t * P:(t + 1) * P], xg[par][:, t, c * P:(c + 1) * P],
                                          ident[:, :])
                    mm.then_inc(b_turned, 1)
                pe.wait_ge(b_turned_out, e * CD + CD)
                for m in range(MI):
                    wait(pe, b_relu[m % 2], e * (MI // 2) + (m // 2 - 1) if m >= 4 else e * (MI // 2))
                    for c in range(CD):
                        mm = pe.matmul(up_banks[m % 4], wi[par][:, c, m * P:(m + 1) * P], xgT[:, c, :],
                                       start=(c == 0), stop=(c == CD - 1))
                    mm.then_inc(b_up, 1)
                wait(pe, b_down_out, e * 2)
                for t in range(TB):
                    for m in range(MI):
                        if t == 0:
                            pe.wait_ge(b_relu[m % 2], e * (MI // 2) + (m // 2 + 1))
                        mm = pe.matmul(down_banks[t // 2][:, (t % 2) * D:(t % 2 + 1) * D],
                                       hT[:, m, t * P:(t + 1) * P], wo[par][:, m, :],
                                       start=(m == 0), stop=(m == MI - 1))
                    if t % 2:
                        mm.then_inc(b_down, 1)
            experts(pe, emit, 3)

        def b_act(act):
            def emit(e, par, half):
                for c in range(CD):
                    act.wait_ge(b_turned, e * CD + (c + 1))
                    act.activation(xgT[:, c, :], shared[c][:, :], ACT.Identity).then_inc(b_turned_out, 1)
                for m in range(0, MI, 2):
                    act.wait_ge(b_up, e * MI + (m + 1))
                    act.activation(hT[:, m, :], up_banks[m % 4], ACT.Relu).then_inc(b_relu[0], 1)
            experts(act, emit, 3)

        def b_dve(dve):
            def emit(e, par, half):
                for m in range(1, MI, 2):
                    dve.wait_ge(b_up, e * MI + (m + 1))
                    dve.tensor_scalar(hT[:, m, :], up_banks[m % 4], 0.0, None, ALU.max).then_inc(b_relu[1], 1)
                wait(dve, b_saved[par], half * 16)
                for i in range(2):
                    dve.wait_ge(b_down, e * 2 + (i + 1))
                    dve.tensor_copy(yo[par][:, 2 * i:2 * i + 2, :],
                                    down_banks[i][:, :].rearrange("p (t d) -> p t d", t=2)).then_inc(b_down_out, 1)
            experts(dve, emit, 3)

        LC = layer_sems("c")
        banks_c = Banks(False, LC["ready"], LC["free"], shared)
        U1 = NG * len(UNITS_FULL)
        gath = sb("gath", [P, 2 * TB, D])
        xn = sb("xn", [P, TB, D])
        c_stats = sb("c_stats", [P, TB, 6])
        c_mv = sb("c_mv", [P, TB, 2])
        combine_to = c_stats, c_mv, [small[:, i, :] for i in (8, 7, 6)]
        rms = [small[:, 9 + i, :] for i in range(2)]
        gate_now = [sb(f"gate_now{i}", [P, TB * 3]) for i in range(2)]
        qk_cos = scratch
        qk_sin = mask
        chosen1 = sb("chosen1", [P, NB, 2, TB * E1])
        row1 = sb("row1", [P, NB, 2 * TB])
        gate1 = sb("gate1", [P, NB + 1, TB * 3])
        row_from1 = sb("row_from1", [P, NB + 1, TB * 2], I32)
        w1t = arena[:, 0:8192]
        w2t = arena[:, 8192:16384]
        KF = F1 // P
        d_w = sem("d_weights")
        s_w1, s_w1s = sem("c_weights"), sem("c_weights_scaled")
        W1_DMAS = 8
        NORM = TB + TB + 1 + RSQRT_STEPS
        COMB_E = 2 * TB + NORM
        COMB = COMB_E + TB + TB + TB + TB + 2 + RSQRT_STEPS + 1 + TB + 1
        MASK1 = 5 + 1 + 5 + 2 + 5
        ROUTE1 = MASK1 + 2 * 9 + 2 + 2
        ROPE = 4

        def gather_index_dve(dve, L, k, par, half, row_from, gate):
            wait(dve, L["gathered"][par], half * (16 * 2 * TB))
            dve.tensor_copy(row_now[par][:, :], row_from[:, bass.ds(k, 1), :].rearrange("p b n -> p (b n)")
                            ).then_inc(L["ga_idx"], 1)
            dve.tensor_copy(gate_now[par][:, :], gate[:, bass.ds(k, 1), :].rearrange("p b n -> p (b n)")
                            ).then_inc(L["ga_idx"], 1)

        def gather_pool(pool, L, k, par, n, table, rows, to):
            settle(pool)
            pool.indirect_dma_start(out=to[:, n, :], out_offset=None, in_=table,
                                    in_offset=bass.IndirectOffsetOnAxis(ap=row_now[par][:, n:n + 1], axis=0),
                                    bounds_check=rows - 1, oob_is_err=False).then_inc(L["gathered"][par], 16)

        def weigh_dve(dve, chain, x, x_from, rows, gates):
            for i in range(2):
                for t in range(TB):
                    chain.unwaited(dve.scalar_tensor_tensor(
                        out=x[:, t, :], in0=rows[:, 2 * t + i, :], scalar=gates[:, 3 * t + i:3 * t + i + 1],
                        in1=(x if i else x_from)[:, t, :], op0=ALU.mult, op1=ALU.add))
                    yield
                yield from chain.pause()

        def c_combine_dve(dve, L, turn):
            k, par, half = turn.batch(-1)
            dve.wait_ge(L["x_load"][par], half * 16 + 16)
            dve.wait_ge(L["gathered"][par], half * (16 * 2 * TB) + 16 * 2 * TB)
            dve.wait_ge(L["ga_idx"], k * 2 + 2)
            chain = Chain(dve, L["comb"], k * COMB)
            x = x_in[par]
            for t in range(TB):
                chain.unwaited(dve.tensor_scalar(x[:, t, :], x[:, t, :], gate_now[par][:, 3 * t + 2:3 * t + 3], None,
                                                 ALU.mult))
                yield
            yield from chain.pause()
            yield from weigh_dve(dve, chain, x, x, gath, gate_now[par])
            yield from norm_stats_dve(dve, chain, x, combine_to)
            yield from norm_root_dve(dve, chain, combine_to)
            for t in range(TB):
                chain.unwaited(dve.tensor_scalar(x[:, t, :], x[:, t, :], c_mv[:, t, 0:1], small[:, 7, t:t + 1],
                                                 ALU.subtract, ALU.mult))
            yield from chain.pause()
            for t in range(TB):
                chain.unwaited(dve.bn_stats(c_stats[:, t, :], x[:, t, :]))
            yield from chain.pause()
            settle(dve)
            for t in range(TB):
                chain.unwaited(dve.bn_aggr(c_mv[:, t, :], c_stats[:, t, :]))
            yield from chain.pause()
            yield from chain(dve.tensor_tensor(small[:, 3, :], c_mv[:, :, 0], c_mv[:, :, 0], ALU.mult))
            yield from chain(dve.scalar_tensor_tensor(out=small[:, 3, :], in0=c_mv[:, :, 1], scalar=RMS_EPS,
                                                      in1=small[:, 3, :], op0=ALU.add, op1=ALU.add))
            yield from rsqrt(dve, chain, small[:, 4, :], small[:, 3, :], small[:, 8, :])
            yield from chain(dve.tensor_tensor(rms[par], small[:, 3, :], small[:, 4, :], ALU.mult))
            for t in range(TB):
                chain.unwaited(dve.tensor_scalar(xn[:, t, :], x[:, t, :], small[:, 4, t:t + 1], None, ALU.mult))
            chain.unwaited(dve.memset(small[:, 15, :], 0.0))
            yield from chain.pause()
            assert chain.n == COMB, chain.n

        def block_weights(sp, experts):
            for e in experts:
                sp.dma_start(w1t[:, e * 1024:(e + 1) * 1024].rearrange("p (c n) -> p c n", c=CD),
                             a["w1T"][e * D:(e + 1) * D, :].rearrange("(c p) n -> p c n", p=P)).then_inc(d_w, 16)
                sp.dma_start(w2t[:, e * 1024:(e + 1) * 1024].rearrange("p (c n) -> p c n", c=KF),
                             a["w2T"][e * F1:(e + 1) * F1, :].rearrange("(c p) n -> p c n", p=P)).then_inc(d_w, 16)

        def c_sp(sp):
            L = LC
            sp.wait_ge(d_zero, 32)

            def emit(turn):
                for step, n in schedule(False, turn.kind):
                    k, par, half = turn.batch(-1 if step in AHEAD[False] else 0)
                    if step == "xl":
                        wait(sp, L["xp"], k - 1)
                        settle(sp)
                        sp.dma_start(x_in[par][:, :, :],
                                     x1_dram[bass.ds(k * S, S), :].rearrange("(t p) d -> p t d", p=P)
                                     ).then_inc(L["x_load"][par], 16)
                    elif step == "ro":
                        order = CHUNKS.index(n)
                        wait(sp, L["stacked"][par][n % 2], half * STACK_DMAS)
                        settle(sp)
                        sp.wait_ge(L["q3"], k * 4 + (order + 1))
                        settle(sp)
                        sp.dma_start(parts[par, n // 2, :, (n % 2) * P:(n % 2 + 1) * P, :].rearrange("j p n -> p j n"),
                                     qk_src[n][:, :, :]).then_inc(L["parts_saved"], 16)
                    elif step == "st_q":
                        sp.wait_ge(L["parts_saved"], k * 64 + (32 * n + 32))
                        settle(sp)
                        wait(sp, L["exp"], (k - 1) * U1)
                        settle(sp)
                        heads = slice(n * NH // 2, (n + 1) * NH // 2)
                        for t, (i, j) in enumerate(PRODUCTS):
                            for side, part, stack in ((0, i, Q), (1, j, K)):
                                sp.dma_start(stack[par][t * HD:(t + 1) * HD, heads, :],
                                             parts[par, side, part, n * P:(n + 1) * P, :].rearrange(
                                                 "(h d) n -> d h n", d=HD)).then_inc(L["stacked"][par][n], 16)
                    elif step == "wl":
                        sp.wait_ge(L["exp"], (NB - 1 + n) * U1)
                        settle(sp)
                        block_weights(sp, range(n * 4, n * 4 + 4))
                    elif step == "sv":
                        k, par, half = turn.batch(2)
                        sp.wait_ge(L["x_out"], k * TB + TB)
                        settle(sp)
                        sp.dma_start(x3_dram[bass.ds(k * S, S), :].rearrange("(t p) d -> p t d", p=P),
                                     x_out[par][:, :, :]).then_inc(L["x_saved"][par], 16)
            slots(sp, emit)
            for i in range(2):
                sp.wait_ge(L["x_saved"][i], NB // 2 * 16)
                sp.wait_ge(L["x_load"][i], (NB // 2 + 1 - i) * 16)

        def c_pe(pe):
            L, banks = LC, banks_c
            pe.wait_ge(s_w1, W1_DMAS * 16)
            pe.wait_ge(s_w1s, 2 * CD)
            pe.wait_ge(b_down_out, E0 * 2)
            pe.wait_ge(b_turned_out, E0 * CD)
            for i in range(2):
                pe.wait_ge(b_relu[i], E0 * MI // 2)

            def emit(turn):
                for step, n in schedule(False, turn.kind):
                    k, par, half = turn.batch(-1 if step in AHEAD[False] else 0)
                    if step == "xT":
                        bank, ready = banks.acquire(pe, turn, ("xT", n))
                        if n == 0:
                            pe.wait_ge(L["comb"], k * COMB + COMB)
                        for t in range(TB):
                            mm = pe.transpose(bank[:, t * P:(t + 1) * P], xn[:, t, n * P:(n + 1) * P], ident[:, :])
                        mm.then_inc(ready, 1)
                    elif step == "qk":
                        bank, ready = banks.acquire(pe, turn, ("qk", n))
                        if n == 0:
                            banks.both_read(pe, turn, "xT")
                        for c in range(CD):
                            mm = pe.matmul(bank[:, :], w_qkv[:, c, n * P:(n + 1) * P], xT[:, c, :],
                                           start=(c == 0), stop=(c == CD - 1))
                        mm.then_inc(ready, 1)
                    elif step == "ro":
                        bank, ready = banks.acquire(pe, turn, ("ro", n))
                        banks.read(pe, turn, ("qk", n))
                        pe.matmul(bank[:, :], rot[:, :], qk_flat[CHUNKS.index(n) % 2][:, :],
                                  start=True, stop=True).then_inc(ready, 1)
                    elif step == "v":
                        bank, ready = banks.acquire(pe, turn, ("v", n))
                        for t in (2 * n, 2 * n + 1):
                            for c in range(CD):
                                mm = pe.matmul(bank[:, (t % 2) * D:(t % 2 + 1) * D], xT[:, c, t * P:(t + 1) * P],
                                               w_qkv[:, c, 2 * D:3 * D], start=(c == 0), stop=(c == CD - 1))
                        mm.then_inc(ready, 1)
                    elif step in ("st", "av", "on", "oT", "y"):
                        attention_pe(pe, L, banks, False, turn, step, n, U1)
                    elif step in ("rT", "lg", "ps"):
                        route_pe(pe, L, banks, turn, step, n, NE1, ROUTE1, MASK1)
            slots(pe, emit)

        def c_act(act):
            L, banks = LC, banks_c
            act.wait_ge(s_w1, W1_DMAS * 16)

            def emit(turn):
                for step, n in schedule(False, turn.kind):
                    k, par, half = turn.batch(-1 if step in AHEAD[False] else 0)
                    if step == "xT":
                        copy_bank(act, banks, turn, ("xT", n), xT[:, n, :])
                    elif step == "qk":
                        order = CHUNKS.index(n)
                        bank, free = banks.filled(act, turn, ("qk", n))
                        wait(act, L["rope"], k * (4 * ROPE) + (ROPE * (order - 1) - 2))
                        act.activation(qk_flat[order % 2][:, :], bank[:, :], ACT.Identity,
                                       bias=b_qk[:, n:n + 1]).then_inc(free, 1)
                    elif step in ("st", "oe"):
                        attention_act(act, L, False, turn, step, n, U1, ACT.Sigmoid)
                    elif step == "oT":
                        copy_bank(act, banks, turn, ("oT", n), oT[:, n, :])
                    elif step == "rT":
                        copy_bank(act, banks, turn, ("rT", n), rT[:, n, :])
                    elif step == "ex":
                        k, par, half = turn.batch(2)
                        act.wait_ge(L["rc"], k * ROUTE1 + MASK1 - 5)
                        act.activation(r_s[:, 12, :], r_s[:, 2, :], ACT.Sigmoid, scale=-1.0).then_inc(L["ex"], 1)
                        act.activation(r_s[:, 13, :], r_s[:, 2, :], ACT.Sigmoid).then_inc(L["ex"], 1)
            slots(act, emit)

        def c_route_dve(dve, banks, turn, step):
            L, ne = LC, NE1
            k, par, half = turn.batch(2)
            oh = [r_oh[:, i, :, 0:ne] for i in range(2)]
            lg = r_lg[:, :, 0:ne]
            rank = lane[:, LANE_RANK1:LANE_RANK1 + ne]
            if step == "l1":
                chain = Chain(dve, L["rc"], k * ROUTE1)
                bank, free = banks.filled(dve, turn, ("lg", 0))
                dve.tensor_tensor(lg, bank[:, 0:TB * ne].rearrange("p (t e) -> p t e", t=TB),
                                  lanes(LANE_RB1, ne), ALU.add).then_inc(free, 1)
                yield
                banks.read(dve, turn, ("lg", 0))
                yield from first_choice(dve, chain, lg, ne, r_s[:, 4, :], rank, oh[0])
                yield from chain(dve.scalar_tensor_tensor(out=r_w[:, :, 0:ne], in0=oh[0], scalar=LOW, in1=lg,
                                               op0=ALU.mult, op1=ALU.add))
                yield from first_choice(dve, chain, r_w[:, :, 0:ne], ne, r_s[:, 5, :], rank, oh[1])
                yield from chain(dve.tensor_tensor(r_s[:, 2, :], r_s[:, 5, :], r_s[:, 4, :], ALU.subtract))
                yield from chain(dve.tensor_tensor(r_mask[:, :, 0:ne], oh[0], oh[1], ALU.add))
            elif step == "l2":
                chain = Chain(dve, L["rc"], k * ROUTE1)
                chain.n = MASK1 - 5
                yield from count_before(dve, chain, ne)
                assert chain.n == MASK1, chain.n
            elif step == "l3":
                chain = Chain(dve, L["rc"], k * ROUTE1)
                chain.n = MASK1
                bank, free = banks.filled(dve, turn, ("ps", 0))
                dve.tensor_tensor(r_pos[:, :, 0:ne], bank[:, 0:TB * ne].rearrange("p (t e) -> p t e", t=TB),
                                  lanes(LANE_SEG1, ne), ALU.add).then_inc(free, 1)
                yield
                banks.read(dve, turn, ("ps", 0))
                dve.wait_ge(L["ex"], k * 2 + 2)
                g = gate1[:, bass.ds(k, 1), :].rearrange("p b (t c) -> p (b t) c", c=3)
                rows = row1[:, bass.ds(k, 1), :].rearrange("p b (t c) -> p (b t) c", c=2)
                wait(dve, L["scattered"][par], half * (16 * 2 * TB))
                for i in range(2):
                    yield from chain(dve.tensor_tensor(oh[i], oh[i], lanes(LANE_FFN, ne), ALU.mult))
                    yield from chain(dve.tensor_reduce(r_s[:, 9, :], oh[i], AX_X, ALU.add))
                    yield from chain(dve.tensor_tensor(r_c[:, :, 0:ne], oh[i], r_pos[:, :, 0:ne], ALU.mult))
                    yield from chain(dve.tensor_reduce(r_s[:, 10, :], r_c[:, :, 0:ne], AX_X, ALU.add))
                    yield from chain(dve.tensor_tensor(g[:, :, i], r_s[:, 12 + i, :], r_s[:, 9, :], ALU.mult))
                    yield from chain(dve.tensor_copy(rows[:, :, i], r_s[:, 10, :]))
                    yield from chain(dve.tensor_scalar(r_s[:, 11, :], r_s[:, 9, :], -FAR, FAR, ALU.mult, ALU.add))
                    yield from chain(dve.tensor_tensor(row_to[par][:, :, i], r_s[:, 10, :], r_s[:, 11, :], ALU.add))
                    yield from chain(dve.tensor_copy(
                        chosen1[:, bass.ds(k, 1), i, :].rearrange("p b (t e) -> p (b t) e", e=E1),
                        oh[i][:, :, 0:E1]))
                yield from chain(dve.tensor_tensor(r_s[:, 14, :], g[:, :, 0], g[:, :, 1], ALU.add))
                yield from chain(dve.tensor_tensor(r_s[:, 15, :], r_s[:, 12, :], r_s[:, 13, :], ALU.add))
                yield from chain(dve.tensor_tensor(r_s[:, 14, :], r_s[:, 15, :], r_s[:, 14, :], ALU.subtract))
                yield from chain(dve.tensor_scalar(g[:, :, 2], r_s[:, 14, :], 1.0, None, ALU.add))
                assert chain.n == ROUTE1, chain.n

        def c_dve(dve):
            L, banks = LC, banks_c
            chains = InPieces(dict(zip(("cb", "ln", "l1", "l2", "l3"), (N_COMBINE, N_LN) + N_ROUTE[False])))
            dve.wait_ge(s_w1, W1_DMAS * 16)
            for c in range(CD):
                for side in range(2):
                    dve.tensor_scalar(w_qkv[:, c, side * D:(side + 1) * D], w_qkv[:, c, side * D:(side + 1) * D],
                                      rn_scale[:, side, c:c + 1], None, ALU.mult).then_inc(s_w1s, 1)
            dve.memset(r_before[:, TB, :], 0.0).then_inc(s_fill2, 1)
            dve.memset(row_from1[:, NB, :], 0).then_inc(s_fill2, 1)
            dve.memset(gate1[:, NB, :], 0.0).then_inc(s_fill2, 1)
            dve.wait_ge(s_fill2, 5)
            dve.wait_ge(LA["parts_saved"], (NB + 1) * 64)

            def emit(turn):
                for step, n in schedule(False, turn.kind):
                    k, par, half = turn.batch(-1 if step in AHEAD[False] else 0)
                    if step == "gi":
                        k, par, half = turn.batch(-1)
                        gather_index_dve(dve, L, k, par, half, row_from0, gate0)
                    elif step == "cb":
                        chains.piece(step, n, lambda: c_combine_dve(dve, L, turn))
                    elif step == "ro":
                        order = CHUNKS.index(n)
                        rest = qk_rest[order % 2]
                        chain = Chain(dve, L["rope"], k * (4 * ROPE))
                        chain.n = order * ROPE
                        banks.read(dve, turn, ("qk", n))
                        chain.unwaited(dve.tensor_tensor(qk_cos[:, :], qk_flat[order % 2][:, :], cos_t[:, :],
                                                         ALU.mult))
                        bank, free = banks.filled(dve, turn, ("ro", n))
                        dve.tensor_tensor(qk_sin[:, :], bank[:, :], sin_t[:, :], ALU.mult).then_inc(free, 1)
                        banks.read(dve, turn, ("ro", n))
                        chain.join()
                        settle(dve)
                        wait(dve, L["q3"], k * 4 + (order - 1))
                        chain.step(dve.tensor_tensor(rest[:, :], qk_cos[:, :], qk_sin[:, :], ALU.add))
                        wait(dve, L["parts_saved"], k * 64)
                        chain.step(dve.tensor_copy(qk_src[n][:, 0, :], rest[:, :]))
                        chain.step(dve.tensor_tensor(rest[:, :], rest[:, :], qk_src[n][:, 0, :], ALU.subtract))
                        dve.tensor_copy(qk_src[n][:, 1, :], rest[:, :]).then_inc(L["q2"], 1)
                    elif step == "v":
                        bank, free = banks.filled(dve, turn, ("v", n))
                        wait(dve, L["av"], (k - 1) * U1)
                        dve.wait_ge(L["comb"], k * COMB + COMB)
                        for t in (2 * n, 2 * n + 1):
                            v = dve.scalar_tensor_tensor(
                                out=v_aug[par][:, t, :, 0:HD],
                                in0=bank[:, (t % 2) * D:(t % 2 + 1) * D].rearrange("p (h d) -> p h d", h=NH),
                                scalar=rms[par][:, t:t + 1], in1=b_v[:, :].rearrange("p (h d) -> p h d", h=NH),
                                op0=ALU.mult, op1=ALU.add)
                        v.then_inc(free, 1)
                    elif step in ("on", "y"):
                        attention_dve(dve, L, banks, turn, step, n, SUM_EPS)
                    elif step == "ln":
                        chains.piece(step, n, lambda: finish_dve(dve, L, banks, turn))
                    elif step in ("l1", "l2", "l3"):
                        chains.piece(step, n, lambda: c_route_dve(dve, banks, turn, step))
            slots(dve, emit)

        def c_pool(pool):
            L = LC
            pool.wait_ge(s_w1, W1_DMAS * 16)
            pool.wait_ge(b_saved[0], 4 * 16)
            pool.wait_ge(b_saved[1], 3 * 16)

            def emit(turn):
                for step, n in schedule(False, turn.kind):
                    k, par, half = turn.batch(-1 if step in AHEAD[False] else 0)
                    if step == "ga":
                        k, par, half = turn.batch(-1)
                        if n == 0:
                            pool.wait_ge(L["ga_idx"], k * 2 + 2)
                            wait(pool, L["comb"], (k - 1) * COMB + 3 * TB)
                        gather_pool(pool, L, k, par, n, slot_y0, E0 * CAP, gath)
                    elif step == "ro":
                        order = CHUNKS.index(n)
                        pool.wait_ge(L["q2"], k * 4 + (order + 1))
                        pool.tensor_tensor(out=qk_src[n][:, 2, :], in0=qk_rest[order % 2][:, :],
                                           in1=qk_src[n][:, 1, :], op=ALU.subtract).then_inc(L["q3"], 1)
                    elif step == "xp":
                        k, par, half = turn.batch(1)
                        pool.wait_ge(L["comb"], k * COMB + COMB)
                        wait(pool, L["x_out"], k * TB)
                        pool.tensor_tensor(out=x_res[:, :, :], in0=x_in[par][:, :, :],
                                           in1=b_o[:, :].unsqueeze(1).broadcast_to([P, TB, D]),
                                           op=ALU.add).then_inc(L["xp"], 1)
                    elif step == "sc":
                        k, par, half = turn.batch(2)
                        if n == 0:
                            pool.wait_ge(L["rc"], k * ROUTE1 + ROUTE1)
                            settle(pool)
                        t, i = n // 2, n % 2
                        pool.indirect_dma_start(
                            out=slot_x1, out_offset=bass.IndirectOffsetOnAxis(ap=row_to[par][:, t, i:i + 1], axis=0),
                            in_=x_out[par][:, t, :], in_offset=None, bounds_check=ZROW - 1,
                            oob_is_err=False).then_inc(L["scattered"][par], 16)
            slots(pool, emit)

        free_at = [16384]

        def carve(n):
            free_at[0] += n
            return arena[:, free_at[0] - n:free_at[0]]

        RX = 4
        bx = [gath[:, i, :] for i in range(RX)]
        bxT = [carve(D) for _ in range(2)]
        w1_now = [carve(CD * F1), xn[:, :, :].rearrange("p t d -> p (t d)")]
        bhT = [carve(F1) for _ in range(2)]
        by = [carve(D) for _ in range(2)]
        t_tab = sb("t_tab", [1, 2, NBLK], I32)
        t_cnt = sb("t_cnt", [P, E1])
        t_a = carve(E1 * 32).rearrange("p (e n) -> p e n", e=E1)
        t_nb = sb("t_nb", [P, E1])
        t_tri = carve(E1 * E1).rearrange("p (a b) -> p a b", a=E1)
        t_start = sb("t_start", [P, E1])
        t_end = sb("t_end", [P, E1])
        t_delta = sb("t_delta", [P, E1])
        t_rowf = carve(2 * TB * NB)
        t_pad = sb("t_pad", [P, E1], I32)
        t_b8 = carve(NBLK * E1)[0:1, :].rearrange("p (b e) -> p b e", e=E1)
        t_b8b = carve(NBLK * E1)[0:1, :].rearrange("p (b e) -> p b e", e=E1)
        t_bf = sb("t_bf", [1, 6, NBLK])
        d_cnt, d_chain = sem("d_counts"), sem("d_chain")
        d_pad = sem("d_padded")
        d_zero = sem("d_zero_rows")
        d_load = [sem(f"d_load{i}") for i in range(RX)]
        d_saved = [sem(f"d_saved{i}") for i in range(2)]
        d_t, d_tout, d_w1, d_up, d_h, d_y, d_yout = (
            sem(x) for x in ("d_turned", "d_turned_out", "d_expert_weights", "d_up", "d_hidden",
                             "d_down", "d_down_out"))
        D_CHAIN = 25
        D_PADS = 9
        D_TABLE = 21

        def tables_dve(dve):
            chain = Chain(dve, d_chain, 0)
            dve.wait_ge(d_cnt, 1)
            yield from chain(dve.tensor_copy(t_cnt[:, :], shared[0][:, 0:E1]))
            yield from chain(dve.tensor_tensor(t_a[:, :, :], spread(t_cnt[:, :], 32),
                                    lane[:, LANE_STEP:LANE_STEP + 32].unsqueeze(1).broadcast_to([P, E1, 32]),
                                    ALU.is_gt))
            yield from chain(dve.tensor_reduce(t_nb[:, :], t_a[:, :, :], AX_X, ALU.add))
            yield from chain(dve.tensor_tensor(t_tri[:, :, :], t_nb[:, :].unsqueeze(1).broadcast_to([P, E1, E1]),
                                    lane[:, LANE_TRI:LANE_TRI + 64].rearrange("p (a b) -> p a b", a=E1), ALU.mult))
            yield from chain(dve.tensor_reduce(t_start[:, :], t_tri[:, :, :], AX_X, ALU.add))
            yield from chain(dve.tensor_tensor(t_end[:, :], t_start[:, :], t_nb[:, :], ALU.add))
            yield from chain(dve.scalar_tensor_tensor(out=t_delta[:, :], in0=t_start[:, :], scalar=float(P),
                                           in1=lane[:, LANE_SEG1:LANE_SEG1 + E1], op0=ALU.mult, op1=ALU.subtract))
            seg = lane[:, LANE_SEG1:LANE_SEG1 + E1]
            yield from chain(dve.tensor_tensor(t_start[:, :], t_cnt[:, :], seg, ALU.add))
            yield from chain(dve.tensor_scalar(t_pad[:, :], t_start[:, :], lane[:, LANE_IOTA:LANE_IOTA + 1], None, ALU.add))
            blk = lane[0:1, LANE_BLK:LANE_BLK + NBLK]
            yield from chain(dve.tensor_tensor(t_b8[:, :, :], spread(blk, E1),
                                    t_end[0:1, :].unsqueeze(1).broadcast_to([1, NBLK, E1]), ALU.is_ge))
            yield from chain(dve.tensor_reduce(t_bf[:, 0, :], t_b8[:, :, :], AX_X, ALU.add))
            yield from chain(dve.tensor_tensor(t_b8[:, :, :], spread(t_bf[:, 0, :], E1),
                                    lane[0:1, LANE_BLK:LANE_BLK + E1].unsqueeze(1).broadcast_to([1, NBLK, E1]),
                                    ALU.is_equal))
            yield from chain(dve.tensor_tensor(t_b8b[:, :, :], t_b8[:, :, :],
                                    t_delta[0:1, :].unsqueeze(1).broadcast_to([1, NBLK, E1]), ALU.mult))
            yield from chain(dve.tensor_reduce(t_bf[:, 1, :], t_b8b[:, :, :], AX_X, ALU.add))
            yield from chain(dve.tensor_reduce(t_bf[:, 2, :], t_b8[:, :, :], AX_X, ALU.add))
            yield from chain(dve.scalar_tensor_tensor(out=t_bf[:, 3, :], in0=blk, scalar=float(P), in1=t_bf[:, 1, :],
                                           op0=ALU.mult, op1=ALU.subtract))
            yield from chain(dve.tensor_tensor(t_bf[:, 3, :], t_bf[:, 3, :], t_bf[:, 2, :], ALU.mult))
            yield from chain(dve.tensor_scalar(t_bf[:, 4, :], t_bf[:, 2, :], -float(ZROW), float(ZROW), ALU.mult, ALU.add))
            yield from chain(dve.tensor_tensor(t_tab[:, 0, :], t_bf[:, 3, :], t_bf[:, 4, :], ALU.add))
            yield from chain(dve.tensor_scalar(t_bf[:, 5, :], t_bf[:, 0, :], float(E1 - 1), None, ALU.min))
            yield from chain(dve.tensor_copy(t_tab[:, 1, :], t_bf[:, 5, :]))
            c2 = chosen1[:, :, :, :].rearrange("p b i (t e) -> p (b i t) e", e=E1)
            yield from chain(dve.tensor_tensor(c2, c2, t_delta[:, :].unsqueeze(1).broadcast_to([P, 2 * TB * NB, E1]), ALU.mult))
            yield from chain(dve.tensor_reduce(t_rowf[:, :], c2, AX_X, ALU.add))
            for i in range(2):
                yield from chain(dve.tensor_tensor(
                    row_from1[:, 0:NB, :].rearrange("p b (t c) -> p b t c", c=2)[:, :, :, i],
                    row1[:, :, :].rearrange("p b (t c) -> p b t c", c=2)[:, :, :, i],
                    t_rowf[:, :].rearrange("p (b i t) -> p b i t", i=2, t=TB)[:, :, i, :], ALU.add))
            assert chain.n == D_CHAIN, chain.n

        def d_sp(sp):
            sp.wait_ge(d_chain, D_TABLE)
            for i in range(2):
                sp.wait_ge(LC["scattered"][i], NB // 2 * 16 * 2 * TB)
                sp.wait_ge(LC["gathered"][i], (NB // 2 + 1 - i) * 16 * 2 * TB)
            sp.wait_ge(d_pad, 16 * E1)
            sp.wait_ge(d_zero, 32)

            def load(j, buffer):
                row = sp.value_load(t_tab[0:1, 0, bass.ds(j, 1)], min_val=0, max_val=ZROW)
                sp.dma_start(bx[buffer], slot_x1[bass.ds(row, P), :]).then_inc(d_load[buffer], 16)

            for j in range(RX):
                load(j, j)

            def step(j, buffer, more):
                if more:
                    sp.wait_ge(d_t, j + 1)
                    settle(sp)
                    load(j + RX, buffer)
                sp.wait_ge(d_yout, j + 1)
                settle(sp)
                sp.dma_start(slot_y1[bass.ds(j * P, P), :], by[buffer % 2]).then_inc(d_saved[buffer % 2], 16)

            with sp.Fori(0, NBLK // RX - 1) as it:
                for i in range(RX):
                    step(it * RX + i, i, True)
            for i in range(RX):
                step(NBLK - RX + i, i, False)
            for i in range(2):
                sp.wait_ge(d_saved[i], NBLK // 2 * 16)

        T_BANK = shared[0]
        UP = [ST[0][:, 0:512], ST[0][:, 512:1024]]
        Y_BANK = [shared[1], shared[2]]

        def d_pe(pe):
            for b in range(3):
                pe.wait_ge(banks_c.free[b], banks_c.total(b))
            pe.wait_ge(LC["rc"], NB * ROUTE1)
            pe.wait_ge(LC["exp"], NB * U1)
            pe.wait_ge(LC["oe"], NB * NG)
            pe.matmul(shared[0][:, 0:E1], ones_b[:, :], r_before[:, TB, 0:E1], start=True, stop=True
                      ).then_inc(d_cnt, 1)
            pe.wait_ge(d_chain, D_TABLE)
            pe.wait_ge(d_w, 2 * E1 * 16)

            def turn_rows(j, buffer, turns):
                wait(pe, d_tout, j)
                pe.wait_ge(d_load[buffer], turns * 16 + 16)
                for c in range(CD):
                    mm = pe.transpose(T_BANK[:, c * P:(c + 1) * P], bx[buffer][:, c * P:(c + 1) * P], ident[:, :])
                mm.then_inc(d_t, 1)

            def up(j, par):
                pe.wait_ge(d_tout, j + 1)
                pe.wait_ge(d_w1, j + 1)
                for f in range(KF):
                    for c in range(CD):
                        mm = pe.matmul(UP[par][:, f * P:(f + 1) * P],
                                       w1_now[par][:, c * F1 + f * P:c * F1 + (f + 1) * P],
                                       bxT[par][:, c * P:(c + 1) * P], start=(c == 0), stop=(c == CD - 1))
                mm.then_inc(d_up, 1)

            def down(j, par, clear):
                e = pe.value_load(t_tab[0:1, 1, bass.ds(j, 1)], min_val=0, max_val=E1 - 1)
                pe.wait_ge(d_h, j + 1)
                wait(pe, d_yout, clear)
                for c in range(KF):
                    mm = pe.matmul(Y_BANK[par][:, 0:D], bhT[par][:, c * P:(c + 1) * P],
                                   w2t[:, bass.ds(e * 1024 + c * D, D)], start=(c == 0), stop=(c == KF - 1))
                mm.then_inc(d_y, 1)

            turn_rows(0, 0, 0)
            up(0, 0)
            turn_rows(1, 1, 0)
            up(1, 1)
            turn_rows(2, 2, 0)
            down(0, 0, 0)

            def four(it):
                for j0 in range(1, RX + 1):
                    par = j0 % 2
                    j = it * RX + j0
                    up(j + 1, 1 - par)
                    turn_rows(j + 2, (j0 + 2) % RX, it + (j0 + 2) // RX)
                    down(j, par, j - 1)
            passes(pe, NBLK // RX - 1, four)
            for j in range(NBLK - 3, NBLK):
                if j + 1 < NBLK:
                    up(j + 1, (j + 1) % 2)
                if j + 2 < NBLK:
                    turn_rows(j + 2, (j + 2) % RX, (j + 2) // RX)
                down(j, j % 2, j - 1)

        def d_act(act):
            act.wait_ge(d_up, 1)
            act.activation(bhT[0], UP[0], ACT.Silu).then_inc(d_h, 1)

            def emit_lag(j, par, half, last=False):
                if not last:
                    act.wait_ge(d_up, j + 2)
                    act.activation(bhT[1 - par], UP[1 - par], ACT.Silu).then_inc(d_h, 1)
                act.wait_ge(d_y, j + 1)
                wait(act, d_saved[par], half * 16)
                act.activation(by[par], Y_BANK[par][:, 0:D], ACT.Identity).then_inc(d_yout, 1)
            def two(it):
                emit_lag(it * 2, 0, it)
                emit_lag(it * 2 + 1, 1, it)
            passes(act, NBLK // 2 - 1, two)
            emit_lag(NBLK - 2, 0, NBLK // 2 - 1)
            emit_lag(NBLK - 1, 1, NBLK // 2 - 1, True)

        def d_dve(dve):
            all_of(tables_dve(dve))

            def rows_out(j, par):
                dve.wait_ge(d_t, j + 1)
                dve.tensor_copy(bxT[par], T_BANK[:, 0:D]).then_inc(d_tout, 1)

            def weights_now(j, par):
                e = dve.value_load(t_tab[0:1, 1, bass.ds(j, 1)], min_val=0, max_val=E1 - 1)
                dve.tensor_copy(w1_now[par], w1t[:, bass.ds(e * 1024, 1024)]).then_inc(d_w1, 1)

            dve.wait_ge(d_w, 2 * E1 * 16)
            dve.wait_ge(d_chain, D_CHAIN)
            weights_now(0, 0)
            rows_out(0, 0)
            weights_now(1, 1)
            rows_out(1, 1)

            def two(it):
                for par in range(2):
                    dve.wait_ge(d_up, it * 2 + par + 1)
                    weights_now(it * 2 + par + 2, par)
                    rows_out(it * 2 + par + 2, par)
            passes(dve, NBLK // 2 - 1, two)

        def d_pool(pool):
            pool.wait_ge(d_chain, D_PADS)
            pool.wait_ge(s_zero, 1)
            for e in range(E1):
                pool.indirect_dma_start(out=slot_x1,
                                        out_offset=bass.IndirectOffsetOnAxis(ap=t_pad[:, e:e + 1], axis=0),
                                        in_=zero[:, :], in_offset=None, bounds_check=ZROW + P - 1,
                                        oob_is_err=False).then_inc(d_pad, 16)

        LE = dict(gathered=[sem(f"e_gathered{i}") for i in range(2)], ga_idx=sem("e_rows_known"),
                  scaled=sem("e_rows_scaled"),
                  comb=[sem(f"e_combine_chain{i}") for i in range(2)], x_load=[sem(f"e_load{i}") for i in range(2)],
                  out=[sem(f"e_out{i}") for i in range(2)], done=sem("e_rows_done"))
        weighed = [y_b, x_res]
        egath = [arena[:, i * 2048:(i + 1) * 2048].rearrange("p (n d) -> p n d", n=2 * TB) for i in (0, 1)]

        def pairs(eng, emit):
            def two(it):
                emit(it * 2, 0, it)
                emit(it * 2 + 1, 1, it)
            passes(eng, NB // 2, two)

        def e_sp(sp):
            def load(k, par):
                settle(sp)
                sp.dma_start(x_in[par][:, :, :], x3_dram[bass.ds(k * S, S), :].rearrange("(t p) d -> p t d", p=P)
                             ).then_inc(LE["x_load"][par], 16)
            sp.wait_ge(LC["xp"], NB)
            load(0, 0)
            load(1, 1)

            def save(k, par):
                sp.wait_ge(LE["done"], k * TB + TB)
                settle(sp)
                sp.dma_start(out[bass.ds(k * S, S), :].rearrange("(t p) d -> p t d", p=P), x_out[par][:, :, :]
                             ).then_inc(LE["out"][par], 16)

            def two(it):
                for par in range(2):
                    sp.wait_ge(LE["comb"][par], it * COMB_E + TB)
                    load(it * 2 + par + 2, par)
                    if not isinstance(it, int) or par:
                        save(it * 2 + par - 1, 1 - par)
            passes(sp, NB // 2 - 1, two)
            for k in range(NB - 3, NB):
                save(k, k % 2)
            for i in range(2):
                sp.wait_ge(LE["out"][i], NB // 2 * 16)

        def e_act(act):
            def emit(k, par, half):
                act.wait_ge(LE["x_load"][par], half * 16 + 16)
                act.wait_ge(LE["ga_idx"], k * 2 + 2)
                for t in range(TB):
                    act.activation(x_in[par][:, t, :], x_in[par][:, t, :], ACT.Identity,
                                   scale=gate_now[par][:, 3 * t + 2:3 * t + 3]).then_inc(LE["scaled"], 1)
            pairs(act, emit)

        def e_dve(dve):
            for i in range(2):
                dve.wait_ge(LC["x_saved"][i], NB // 2 * 16)
                dve.wait_ge(LC["scattered"][i], NB // 2 * 16 * 2 * TB)

            to = norm_to, combine_to

            def total(k, par, half):
                dve.wait_ge(LE["scaled"], k * TB + TB)
                dve.wait_ge(LE["gathered"][par], half * (16 * 2 * TB) + 16 * 2 * TB)
                dve.wait_ge(LE["ga_idx"], k * 2 + 2)
                wait(dve, LE["done"], (k - 1) * TB)
                chain = Chain(dve, LE["comb"][par], half * COMB_E)
                yield from weigh_dve(dve, chain, weighed[par], x_in[par], egath[par], gate_now[par])
                if not isinstance(k, int) or k + 2 <= NB:
                    gather_index_dve(dve, LE, k + 2, par, half + 1, row_from1, gate1)
                yield from norm_stats_dve(dve, chain, weighed[par], to[par])
                assert chain.n == COMB_E - 1 - RSQRT_STEPS

            def rows(k, par, half):
                chain = Chain(dve, LE["comb"][par], half * COMB_E)
                chain.n = COMB_E - 1 - RSQRT_STEPS
                yield from norm_root_dve(dve, chain, to[par])
                assert chain.n == COMB_E
                wait(dve, LE["out"][par], half * 16)
                _, mv, (_, root, _) = to[par]
                for t in range(TB):
                    dve.tensor_scalar(x_out[par][:, t, :], weighed[par][:, t, :], mv[:, t, 0:1], root[:, t:t + 1],
                                      ALU.subtract, ALU.mult).then_inc(LE["done"], 1)
                    yield

            for k in range(2):
                gather_index_dve(dve, LE, k, k, 0, row_from1, gate1)
            all_of(total(0, 0, 0))

            def two(it):
                together(rows(it * 2, 0, it), total(it * 2 + 1, 1, it), 2)
                together(rows(it * 2 + 1, 1, it), total(it * 2 + 2, 0, it + 1), 2)
            passes(dve, NB // 2 - 1, two)
            together(rows(NB - 2, 0, NB // 2 - 1), total(NB - 1, 1, NB // 2 - 1), 2)
            all_of(rows(NB - 1, 1, NB // 2 - 1))

        def e_pool(pool):
            for i in range(2):
                pool.wait_ge(d_saved[i], NBLK // 2 * 16)

            def emit(k, par, half):
                pool.wait_ge(LE["ga_idx"], k * 2 + 2)
                wait(pool, LE["comb"][par], half * COMB_E - (COMB_E - 2 * TB))
                for n in range(2 * TB):
                    gather_pool(pool, LE, k, par, n, slot_y1, NBLK * P, egath[par])
            pairs(pool, emit)

        @block.sync
        def _(sp):
            for dst, src in (
                (ident[:, :], a["c_ident"]), (scratch[:, 0:P], a["c_before"]), (mask[:, :], a["c_mask"]),
                (lane[:, 0:48], a["c_lane"][:, 0:48]), (lane[:, 64:112], a["c_lane"][:, 64:112]),
                (lane[:, 128:304], a["c_lane"][:, 128:304]), (rot[:, :], a["c_rot"]),
                (cos_t[:, :], a["c_cos"]), (sin_t[:, :], a["c_sin"]),
                (lane[:, LANE_RB0:LANE_RB0 + NE0], a["router_b"].partition_broadcast(P)),
                (w_qkv[:, :, :], a["w_qkv"].rearrange("(c p) n -> p c n", p=P)),
                (w_o[:, :, :], a["w_out"].rearrange("(c p) n -> p c n", p=P)),
                (w_r[:, :, 0:NE0], a["router_wT"].rearrange("(c p) n -> p c n", p=P)),
                (b_qk[:, :], a["b_qk_cols"]),
                (b_v[:, :], a["b_qkv"][2 * D:3 * D].partition_broadcast(P)),
                (b_o[:, :], a["b_out"].partition_broadcast(P)),
            ):
                sp.dma_start(dst, src).then_inc(s_const, 16)
            a_sp(sp)
            b_sp(sp)
            c_sp(sp)
            d_sp(sp)
            e_sp(sp)

        @block.tensor
        def _(pe):
            a_pe(pe)
            b_pe(pe)
            c_pe(pe)
            d_pe(pe)

        @block.scalar
        def _(act):
            a_act(act)
            b_act(act)
            c_act(act)
            d_act(act)
            e_act(act)

        @block.vector
        def _(dve):
            a_dve(dve)
            b_dve(dve)
            c_dve(dve)
            d_dve(dve)
            e_dve(dve)

        @block.gpsimd
        def _(pool):
            a_pool(pool)
            c_pool(pool)
            d_pool(pool)
            e_pool(pool)


def shape_constants():
    lane = np.zeros((P, 304), np.float32)
    lane[:, 0:NE0] = NE0 - np.arange(NE0)
    lane[:, 16:16 + E0] = CAP
    lane[:, 32:32 + NE0] = CAP * np.arange(NE0)
    lane[:, 64:64 + NE1] = NE1 - np.arange(NE1)
    lane[:, 80:80 + E1] = 1.0
    lane[:, 96:96 + E1] = SEG * np.arange(E1)
    lane[:, 128:160] = P * np.arange(32)
    lane[:, 160:224] = np.tril(np.ones((E1, E1), np.float32), -1).ravel()
    lane[:, 224:224 + NBLK] = np.arange(NBLK)
    lane[:, 296] = np.arange(P)
    mask = np.zeros((P, S), np.float32)
    mask[:, 0:P] = np.where(np.arange(P)[None, :] >= np.arange(P)[:, None], 0.0, LOW)
    inv = (np.float32(1.0) / np.float32(10000.0) ** (np.arange(0, HD, 2, dtype=np.float32) / np.float32(HD)))
    freqs = np.arange(S, dtype=np.float32)[:, None] * inv.astype(np.float32)[None, :]
    emb = np.concatenate([freqs, freqs], axis=-1)
    cos = np.tile(np.cos(emb).astype(np.float32).T, (P // HD, 1))
    sin = np.tile(np.sin(emb).astype(np.float32).T, (P // HD, 1))
    rot = np.zeros((P, P), np.float32)
    for i in range(0, P, 2):
        rot[i + 1, i] = -1.0
        rot[i, i + 1] = 1.0
    return {
        "c_ident": np.eye(P, dtype=np.float32), "c_before": np.triu(np.ones((P, P), np.float32), 1),
        "c_mask": mask, "c_lane": lane, "c_rot": rot, "c_cos": cos, "c_sin": sin,
    }


def laid_out(i):
    c = np.ascontiguousarray
    i = {k: np.asarray(v) for k, v in i.items()}
    cols = lambda v, n: c(v.reshape(n, P).T)
    return {
        "x": c(np.concatenate([i["L0_attn_x"], i["L0_attn_x"][0:1]]).reshape(NTOK + S, D)),
        "w_qkv": c(i["L0_attn_w_qkv"]), "b_qkv": c(i["L0_attn_b_qkv"]),
        "b_qk_cols": cols(i["L0_attn_b_qkv"][0:2 * D], 4),
        "w_out": c(i["L0_attn_w_out"]), "b_out": c(i["L0_attn_b_out"]),
        "router_wT": c(i["L0_ffn_router_w"].T), "router_b": c(i["L0_ffn_router_b"]),
        "experts_inter": c(i["L0_ffn_experts_inter"].reshape(E0 * D, I0)),
        "experts_out": c(i["L0_ffn_experts_out"].reshape(E0 * I0, D)),
        "w_qkv1T": c(np.concatenate([i["L1_attn_q_w"].T, i["L1_attn_k_w"].T, i["L1_attn_v_w"].T], axis=1)),
        "w_o1T": c(i["L1_attn_o_w"].T),
        "b_qk_cols1": c(np.concatenate([cols(i["L1_attn_q_b"], 2), cols(i["L1_attn_k_b"], 2)], axis=1)),
        "b_v1": c(i["L1_attn_v_b"]), "b_o1": c(i["L1_attn_o_b"]),
        "rn_cols": c(np.stack([cols(i["L1_attn_qn_scale"], 2), cols(i["L1_attn_kn_scale"], 2)], axis=1)),
        "gate_wT": c(i["L1_ffn_gate_w"].T), "expert_bias": c(i["L1_ffn_expert_bias"]),
        "w1T": c(i["L1_ffn_w1"].transpose(0, 2, 1).reshape(E1 * D, F1)),
        "w2T": c(i["L1_ffn_w2"].transpose(0, 2, 1).reshape(E1 * F1, D)),
    }


def kernel(**inputs):
    import concourse.bacc as bacc
    from concourse.bass_utils import run_bass_kernel_spmd

    nc = bacc.Bacc("TRN2", target_bir_lowering=False, num_devices=1)
    arrays = {f"in_{k}": v for k, v in {**laid_out(inputs), **shape_constants()}.items()}
    a = {k[3:]: nc.dram_tensor(k, v.shape, mybir.dt.from_np(v.dtype), kind="ExternalInput").ap()
         for k, v in arrays.items()}
    out = nc.dram_tensor("out_rows", (NTOK, D), F32, kind="ExternalOutput").ap()
    build(nc, a, out)
    r = run_bass_kernel_spmd(nc, [arrays], core_ids=[0])
    return r.results[0]["out_rows"].reshape(NB, S, D)
```
